# Optimizing a Trainium2 kernel written in Bass

```python
import numpy as np
import jax
import jax.numpy as jnp

def _softmax(x, axis=-1):
    return jax.nn.softmax(x, axis=axis)

def _gelu(x):
    return jax.nn.gelu(x, approximate=True)

def _silu(x):
    return jax.nn.silu(x)

def _sigmoid(x):
    return jax.nn.sigmoid(x)

def _layernorm(x, axis=-1, eps=1e-05):
    m = jnp.mean(x, axis=axis, keepdims=True)
    v = jnp.var(x, axis=axis, keepdims=True)
    return (x - m) / jnp.sqrt(v + eps)

def _scatter_add(tgt, idx, src, axis=0):
    return tgt.at[idx].add(src)

def _segment_sum(src, seg, n):
    return jax.ops.segment_sum(src, seg, n)
kernel_name = 'mk_seq_postln_d2_jaxref_r8_f00cc0'

def setup_inputs(seed: int=0):
    np.random.seed(seed)
    _w = jnp.asarray

    def _L0_attn_setup():
        import jax, jax.numpy as jnp
        import numpy as np
        H = 32
        D = 64
        BS = 32
        LAYER_IDX = 0
        NUM_LAYERS = 32
        EPS = 1e-05

        def _decay_buffers():
            base = 1.0 / 2.0 ** (8.0 / H)
            rate = base ** (jnp.arange(H, dtype=jnp.float32) + 1.0)
            factor = 1.0 - LAYER_IDX / (NUM_LAYERS - 1 + 1e-05) + 1e-05
            slope = (rate * factor)[:, None, None]
            r = jnp.arange(BS, dtype=jnp.float32) + 1.0
            query_decay = jnp.exp(-slope * r[:, None])
            key_decay = jnp.exp(-slope * (BS - r[:, None]))
            dd = r[:, None] - r[None, :]
            dd = slope * dd[None, :, :]
            dd = jnp.where(dd >= 0, -dd, -jnp.inf)
            diagonal_decay = jnp.exp(dd)[None]
            block_decay = jnp.exp(-slope * BS)
            return (slope, query_decay, key_decay, diagonal_decay, block_decay)

        def _rmsnorm(x, w):
            v = jnp.mean(x.astype(jnp.float32) ** 2, axis=-1, keepdims=True)
            return (x * jax.lax.rsqrt(v + EPS)).astype(x.dtype) * w
        key = jax.random.key(seed)
        ks = jax.random.split(key, 4)
        b, s, hid = (2, 512, 256)
        return {'hidden_states': jax.random.normal(ks[0], (b, s, hid), jnp.float32), 'qkv_w': jax.random.normal(ks[1], (3 * H * D, hid), jnp.float32) * 0.02, 'out_w': jax.random.normal(ks[2], (hid, H * D), jnp.float32) * 0.02, 'gate_w': jax.random.normal(ks[3], (H * D, hid), jnp.float32) * 0.02, 'norm_w': jnp.ones((H * D,), jnp.float32)}
    _L0_attn_in = _L0_attn_setup()

    def _L0_ffn_setup():
        import jax, jax.numpy as jnp
        import numpy as np
        D_MODEL, D_FF, NS, NR, KR = (256, 176, 2, 16, 4)
        B, S = (4, 256)

        def _moe_forward(u, shared_w1, shared_b1, shared_w2, shared_b2, routed_w1, routed_b1, routed_w2, routed_b2, centroids, bias):
            b, s, d = u.shape
            flat = u.reshape(-1, d)
            T = flat.shape[0]
            h = jax.nn.relu(jnp.einsum('td,ndf->ntf', flat, shared_w1) + shared_b1[:, None, :])
            shared_out = jnp.einsum('ntf,nfd->td', h, shared_w2) + shared_b2.sum(0)
            out = flat + shared_out
            scores = jax.nn.sigmoid(flat @ centroids.T) + bias
            vals, idx = jax.lax.top_k(scores, KR)
            gating = jnp.zeros_like(scores).at[jnp.arange(T)[:, None], idx].set(vals)
            gating = gating / jnp.clip(gating.sum(-1, keepdims=True), 1e-08)

            def step(acc, ew):
                w1, b1, w2, b2, g = ew
                hj = jax.nn.relu(flat @ w1 + b1)
                yj = hj @ w2 + b2
                return (acc + yj * g[:, None], None)
            rout0 = jnp.zeros_like(flat)
            rout, _ = jax.lax.scan(step, rout0, (routed_w1, routed_b1, routed_w2, routed_b2, gating.T))
            return (out + rout).reshape(b, s, d)
        key = jax.random.key(seed)
        ks = jax.random.split(key, 10)
        s1 = 1.0 / np.sqrt(D_MODEL)
        s2 = 1.0 / np.sqrt(D_FF)
        return {'u': jax.random.normal(ks[0], (B, S, D_MODEL), dtype=jnp.float32), 'shared_w1': jax.random.normal(ks[1], (NS, D_MODEL, D_FF), dtype=jnp.float32) * s1, 'shared_b1': jnp.zeros((NS, D_FF), dtype=jnp.float32), 'shared_w2': jax.random.normal(ks[2], (NS, D_FF, D_MODEL), dtype=jnp.float32) * s2, 'shared_b2': jnp.zeros((NS, D_MODEL), dtype=jnp.float32), 'routed_w1': jax.random.normal(ks[3], (NR, D_MODEL, D_FF), dtype=jnp.float32) * s1, 'routed_b1': jnp.zeros((NR, D_FF), dtype=jnp.float32), 'routed_w2': jax.random.normal(ks[4], (NR, D_FF, D_MODEL), dtype=jnp.float32) * s2, 'routed_b2': jnp.zeros((NR, D_MODEL), dtype=jnp.float32), 'centroids': jax.random.normal(ks[5], (NR, D_MODEL), dtype=jnp.float32) * s1, 'bias': jnp.zeros((NR,), dtype=jnp.float32)}
    _L0_ffn_in = _L0_ffn_setup()

    def _L1_attn_setup():
        import jax, jax.numpy as jnp
        import numpy as np
        B_SZ, L, D, DR, N = (2, 256, 256, 128, 16)
        DT_MIN, DT_MAX = (0.001, 0.1)
        key = jax.random.key(seed)
        ks = jax.random.split(key, 6)
        x = jax.random.normal(ks[0], (B_SZ, L, D), dtype=jnp.float32)
        W_xproj = jax.random.normal(ks[1], (DR + 2 * N, D), dtype=jnp.float32) / jnp.sqrt(D)
        b_xproj = jax.random.normal(ks[2], (DR + 2 * N,), dtype=jnp.float32) * 0.01
        W_dt = jax.random.uniform(ks[3], (D, DR), dtype=jnp.float32, minval=-1.0 / jnp.sqrt(DR), maxval=1.0 / jnp.sqrt(DR))
        dt = jnp.exp(jax.random.uniform(ks[4], (D,), dtype=jnp.float32) * (np.log(DT_MAX) - np.log(DT_MIN)) + np.log(DT_MIN))
        dt = jnp.clip(dt, DT_MIN, None)
        b_dt = dt + jnp.log(-jnp.expm1(-dt))
        A_log = jnp.log(jnp.broadcast_to(jnp.arange(1, N + 1, dtype=jnp.float32), (D, N)))
        return {'x': x, 'W_xproj': W_xproj, 'b_xproj': b_xproj, 'W_dt': W_dt, 'b_dt': b_dt, 'A_log': A_log}
    _L1_attn_in = _L1_attn_setup()

    def _L1_ffn_setup():
        import jax, jax.numpy as jnp
        import numpy as np
        from jax import lax
        D_MODEL = 256
        D_CROSS = 1024
        D_RETR = 128
        D_PRIV = 128
        N_EXPERTS = 2048
        N_HEADS = 8
        K_PER_HEAD = 8
        NUM_KEYS = int(np.sqrt(N_EXPERTS))
        BATCH, SEQ = (2, 256)
        key = jax.random.key(seed)
        ks = jax.random.split(key, 10)
        s = 0.02
        return {'hidden_states': jax.random.normal(ks[0], (BATCH, SEQ, D_MODEL), jnp.float32), 'W_up': jax.random.normal(ks[1], (D_CROSS, D_MODEL), jnp.float32) * s, 'b_up': jnp.zeros((D_CROSS,), jnp.float32), 'W_down': jax.random.normal(ks[2], (D_PRIV, D_CROSS), jnp.float32) * s, 'b_down': jnp.zeros((D_PRIV,), jnp.float32), 'W_q': jax.random.normal(ks[3], (D_RETR * N_HEADS, D_PRIV), jnp.float32) * s, 'keys': jax.random.normal(ks[4], (N_HEADS, NUM_KEYS, 2, D_RETR // 2), jnp.float32) * s, 'down_embed': jax.random.normal(ks[5], (N_EXPERTS, D_PRIV), jnp.float32) * s, 'up_embed': jax.random.normal(ks[6], (N_EXPERTS, D_MODEL), jnp.float32) * s}
    _L1_ffn_in = _L1_ffn_setup()
    _d = {'L0_attn_hidden_states': _L0_attn_in['hidden_states'], 'L0_attn_qkv_w': _L0_attn_in['qkv_w'], 'L0_attn_out_w': _L0_attn_in['out_w'], 'L0_attn_gate_w': _L0_attn_in['gate_w'], 'L0_attn_norm_w': _L0_attn_in['norm_w'], 'L0_ffn_shared_w1': _L0_ffn_in['shared_w1'], 'L0_ffn_shared_b1': _L0_ffn_in['shared_b1'], 'L0_ffn_shared_w2': _L0_ffn_in['shared_w2'], 'L0_ffn_shared_b2': _L0_ffn_in['shared_b2'], 'L0_ffn_routed_w1': _L0_ffn_in['routed_w1'], 'L0_ffn_routed_b1': _L0_ffn_in['routed_b1'], 'L0_ffn_routed_w2': _L0_ffn_in['routed_w2'], 'L0_ffn_routed_b2': _L0_ffn_in['routed_b2'], 'L0_ffn_centroids': _L0_ffn_in['centroids'], 'L0_ffn_bias': _L0_ffn_in['bias'], 'L1_attn_W_xproj': _L1_attn_in['W_xproj'], 'L1_attn_b_xproj': _L1_attn_in['b_xproj'], 'L1_attn_W_dt': _L1_attn_in['W_dt'], 'L1_attn_b_dt': _L1_attn_in['b_dt'], 'L1_attn_A_log': _L1_attn_in['A_log'], 'L1_ffn_W_up': _L1_ffn_in['W_up'], 'L1_ffn_b_up': _L1_ffn_in['b_up'], 'L1_ffn_W_down': _L1_ffn_in['W_down'], 'L1_ffn_b_down': _L1_ffn_in['b_down'], 'L1_ffn_W_q': _L1_ffn_in['W_q'], 'L1_ffn_keys': _L1_ffn_in['keys'], 'L1_ffn_down_embed': _L1_ffn_in['down_embed'], 'L1_ffn_up_embed': _L1_ffn_in['up_embed']}
    _x0 = _d['L0_attn_hidden_states']
    _d['L0_attn_hidden_states'] = jax.random.normal(jax.random.fold_in(jax.random.key(seed), 1), (4, 512, 256), dtype=_x0.dtype)
    del _x0
    return _d

def reference(L0_attn_hidden_states, L0_attn_qkv_w, L0_attn_out_w, L0_attn_gate_w, L0_attn_norm_w, L0_ffn_shared_w1, L0_ffn_shared_b1, L0_ffn_shared_w2, L0_ffn_shared_b2, L0_ffn_routed_w1, L0_ffn_routed_b1, L0_ffn_routed_w2, L0_ffn_routed_b2, L0_ffn_centroids, L0_ffn_bias, L1_attn_W_xproj, L1_attn_b_xproj, L1_attn_W_dt, L1_attn_b_dt, L1_attn_A_log, L1_ffn_W_up, L1_ffn_b_up, L1_ffn_W_down, L1_ffn_b_down, L1_ffn_W_q, L1_ffn_keys, L1_ffn_down_embed, L1_ffn_up_embed):

    def _L0_attn_ref(hidden_states, qkv_w, out_w, gate_w, norm_w):
        import jax, jax.numpy as jnp
        import numpy as np
        H = 32
        D = 64
        BS = 32
        LAYER_IDX = 0
        NUM_LAYERS = 32
        EPS = 1e-05

        def _decay_buffers():
            base = 1.0 / 2.0 ** (8.0 / H)
            rate = base ** (jnp.arange(H, dtype=jnp.float32) + 1.0)
            factor = 1.0 - LAYER_IDX / (NUM_LAYERS - 1 + 1e-05) + 1e-05
            slope = (rate * factor)[:, None, None]
            r = jnp.arange(BS, dtype=jnp.float32) + 1.0
            query_decay = jnp.exp(-slope * r[:, None])
            key_decay = jnp.exp(-slope * (BS - r[:, None]))
            dd = r[:, None] - r[None, :]
            dd = slope * dd[None, :, :]
            dd = jnp.where(dd >= 0, -dd, -jnp.inf)
            diagonal_decay = jnp.exp(dd)[None]
            block_decay = jnp.exp(-slope * BS)
            return (slope, query_decay, key_decay, diagonal_decay, block_decay)

        def _rmsnorm(x, w):
            v = jnp.mean(x.astype(jnp.float32) ** 2, axis=-1, keepdims=True)
            return (x * jax.lax.rsqrt(v + EPS)).astype(x.dtype) * w
        b, s, hid = hidden_states.shape
        nb = s // BS
        _, qd, kd, dd, bd = _decay_buffers()
        qkv = jax.nn.silu(hidden_states @ qkv_w.T)
        qkv = qkv.reshape(b, s, H, 3 * D)
        q, k, v = jnp.split(qkv, 3, axis=-1)

        def to_blocks(t):
            return t.transpose(0, 2, 1, 3).reshape(b, H, nb, BS, D).transpose(2, 0, 1, 3, 4)
        qb, kb, vb = (to_blocks(q), to_blocks(k), to_blocks(v))
        qd_ = qd[None]
        kd_ = kd[None]
        bd_ = bd[None]

        def step(state, blk):
            qi, ki, vi = blk
            aw = jnp.einsum('bhid,bhjd->bhij', qi, ki) * dd
            intra = jnp.einsum('bhij,bhjd->bhid', aw, vi)
            inter = jnp.einsum('bhid,bhde->bhie', qi * qd_, state)
            new_state = state * bd_ + jnp.einsum('bhsd,bhse->bhde', ki * kd_, vi)
            return (new_state, intra + inter)
        state0 = jnp.zeros((b, H, D, D), hidden_states.dtype)
        _, ys = jax.lax.scan(step, state0, (qb, kb, vb))
        attn = ys.transpose(1, 2, 0, 3, 4).reshape(b, H, s, D)
        attn = attn.transpose(0, 2, 1, 3).reshape(b, s, H * D)
        attn = _rmsnorm(attn, norm_w)
        gate = jax.nn.sigmoid(hidden_states @ gate_w.T)
        return gate * attn @ out_w.T

    def _L0_ffn_ref(u, shared_w1, shared_b1, shared_w2, shared_b2, routed_w1, routed_b1, routed_w2, routed_b2, centroids, bias):
        import jax, jax.numpy as jnp
        import numpy as np
        D_MODEL, D_FF, NS, NR, KR = (256, 176, 2, 16, 4)
        B, S = (4, 256)

        def _moe_forward(u, shared_w1, shared_b1, shared_w2, shared_b2, routed_w1, routed_b1, routed_w2, routed_b2, centroids, bias):
            b, s, d = u.shape
            flat = u.reshape(-1, d)
            T = flat.shape[0]
            h = jax.nn.relu(jnp.einsum('td,ndf->ntf', flat, shared_w1) + shared_b1[:, None, :])
            shared_out = jnp.einsum('ntf,nfd->td', h, shared_w2) + shared_b2.sum(0)
            out = flat + shared_out
            scores = jax.nn.sigmoid(flat @ centroids.T) + bias
            vals, idx = jax.lax.top_k(scores, KR)
            gating = jnp.zeros_like(scores).at[jnp.arange(T)[:, None], idx].set(vals)
            gating = gating / jnp.clip(gating.sum(-1, keepdims=True), 1e-08)

            def step(acc, ew):
                w1, b1, w2, b2, g = ew
                hj = jax.nn.relu(flat @ w1 + b1)
                yj = hj @ w2 + b2
                return (acc + yj * g[:, None], None)
            rout0 = jnp.zeros_like(flat)
            rout, _ = jax.lax.scan(step, rout0, (routed_w1, routed_b1, routed_w2, routed_b2, gating.T))
            return (out + rout).reshape(b, s, d)
        return _moe_forward(u, shared_w1, shared_b1, shared_w2, shared_b2, routed_w1, routed_b1, routed_w2, routed_b2, centroids, bias)

    def _L1_attn_ref(x, W_xproj, b_xproj, W_dt, b_dt, A_log):
        import jax, jax.numpy as jnp
        import numpy as np
        B_SZ, L, D, DR, N = (2, 256, 256, 128, 16)
        DT_MIN, DT_MAX = (0.001, 0.1)
        dr = W_dt.shape[1]
        n = A_log.shape[1]
        proj = x @ W_xproj.T + b_xproj
        dt_r, Bm, Cm = jnp.split(proj, [dr, dr + n], axis=-1)
        dt = jax.nn.softplus(dt_r @ W_dt.T + b_dt)
        A = -jnp.exp(A_log)
        dA = jnp.exp(jnp.einsum('bld,dn->bldn', dt, A))
        dBX = jnp.einsum('bld,bln,bld->bldn', dt, Bm, x)

        def comb(e1, e2):
            a1, b1 = e1
            a2, b2 = e2
            return (a2 * a1, a2 * b1 + b2)
        _, h = jax.lax.associative_scan(comb, (dA, dBX), axis=1)
        y = jnp.einsum('bldn,bln->bld', h, Cm)
        return y

    def _L1_ffn_ref(hidden_states, W_up, b_up, W_down, b_down, W_q, keys, down_embed, up_embed):
        import jax, jax.numpy as jnp
        import numpy as np
        from jax import lax
        D_MODEL = 256
        D_CROSS = 1024
        D_RETR = 128
        D_PRIV = 128
        N_EXPERTS = 2048
        N_HEADS = 8
        K_PER_HEAD = 8
        NUM_KEYS = int(np.sqrt(N_EXPERTS))
        BATCH, SEQ = (2, 256)
        b, t, _ = hidden_states.shape
        act = jax.nn.silu
        h = act(jnp.einsum('btd,cd->btc', hidden_states, W_up) + b_up)
        h = jnp.einsum('btc,pc->btp', h, W_down) + b_down
        q = jnp.einsum('btp,rp->btr', h, W_q)
        q = q.reshape(b, t, 2, N_HEADS, D_RETR // 2).transpose(2, 0, 1, 3, 4)
        sim = jnp.einsum('pbthn,hkpn->pbthk', q, keys)
        scores, idx = lax.top_k(sim, K_PER_HEAD)
        sx, sy = (scores[0], scores[1])
        ix, iy = (idx[0], idx[1])
        all_scores = (sx[..., :, None] + sy[..., None, :]).reshape(b, t, N_HEADS, K_PER_HEAD * K_PER_HEAD)
        all_indices = (ix[..., :, None] * NUM_KEYS + iy[..., None, :]).reshape(b, t, N_HEADS, K_PER_HEAD * K_PER_HEAD)
        sc, pk = lax.top_k(all_scores, K_PER_HEAD)
        indices = jnp.take_along_axis(all_indices, pk, axis=-1)
        de = down_embed[indices]
        ue = up_embed[indices]
        z = jnp.einsum('btd,bthkd->bthk', h, de)
        z = act(z * jax.nn.softmax(sc, axis=-1))
        out = jnp.einsum('bthk,bthkd->btd', z, ue)
        return out
    x = L0_attn_hidden_states
    x = _layernorm(x + _L0_attn_ref(x, L0_attn_qkv_w, L0_attn_out_w, L0_attn_gate_w, L0_attn_norm_w), axis=-1)
    x = _layernorm(x + _L0_ffn_ref(x, L0_ffn_shared_w1, L0_ffn_shared_b1, L0_ffn_shared_w2, L0_ffn_shared_b2, L0_ffn_routed_w1, L0_ffn_routed_b1, L0_ffn_routed_w2, L0_ffn_routed_b2, L0_ffn_centroids, L0_ffn_bias), axis=-1)
    x = _layernorm(x + _L1_attn_ref(x, L1_attn_W_xproj, L1_attn_b_xproj, L1_attn_W_dt, L1_attn_b_dt, L1_attn_A_log), axis=-1)
    x = _layernorm(x + _L1_ffn_ref(x, L1_ffn_W_up, L1_ffn_b_up, L1_ffn_W_down, L1_ffn_b_down, L1_ffn_W_q, L1_ffn_keys, L1_ffn_down_embed, L1_ffn_up_embed), axis=-1)
    return x

_drawn_inputs = setup_inputs


def setup_inputs(seed=0):
    import zlib

    import numpy as np

    out = dict(_drawn_inputs(seed))
    spreads = {'L0_attn_norm_w': (1.0, 0.2),
     'L0_ffn_shared_b1': (0.0, 0.1),
     'L0_ffn_shared_b2': (0.0, 0.1),
     'L0_ffn_routed_b1': (0.0, 0.499),
     'L0_ffn_routed_b2': (0.0, 0.343),
     'L0_ffn_bias': (0.0, 0.1),
     'L1_ffn_b_up': (0.0, 0.8),
     'L1_ffn_b_down': (0.0, 0.8)}
    factors = {'L1_attn_b_xproj': 8.0,
     'L1_ffn_W_up': 8.0,
     'L1_ffn_W_down': 8.0,
     'L1_ffn_W_q': 8.0,
     'L1_ffn_keys': 8.0,
     'L1_ffn_down_embed': 8.0,
     'L1_ffn_up_embed': 8.0}
    for name, (base, spread) in spreads.items():
        noise = np.random.default_rng([zlib.crc32(name.encode()), seed]).standard_normal(out[name].shape)
        drawn = base * np.exp(spread * noise) if base else spread * noise
        out[name] = jnp.asarray(drawn.astype(out[name].dtype))
    for name, factor in factors.items():
        out[name] = (out[name] * factor).astype(out[name].dtype)
    return out
```

```python
import concourse.bass as bass
from concourse import mybir
from contextlib import ExitStack, contextmanager

FP32 = mybir.dt.float32
FP32R = mybir.dt.float32r
BF16 = mybir.dt.bfloat16
ALU = mybir.AluOpType
ACT = mybir.ActivationFunctionType
AX = mybir.AxisListType
ds = bass.ds

P = 128
BATCH, SEQ, DM = 4, 512, 256
TOKENS = BATCH * SEQ
TILES = TOKENS // P
BLK = 512
NBLK = TOKENS // BLK
KD = DM // P
LN_EPS = 1e-5
ONE_BITS = 0x3F80



def wait_apart(eng, sem, value, passed):
    eng.wait_ge(sem, value)
    eng.sem_inc(passed, 1)


class Scope:

    def __init__(self, nc, prefix, ctx):
        self.nc, self.prefix, self.ctx = nc, prefix, ctx

    def sb(self, name, shape, dt=FP32):
        return self.ctx.enter_context(self.nc.sbuf_tensor(f"{self.prefix}_sb_{name}", shape, dt))

    def ps(self, name, shape=(P, 512), dt=FP32):
        return self.ctx.enter_context(self.nc.psum_tensor(f"{self.prefix}_ps_{name}", list(shape), dt))

    def sem(self, name):
        return self.ctx.enter_context(self.nc.semaphore(f"{self.prefix}_{name}"))


@contextmanager
def scope(nc, prefix):
    with ExitStack() as ctx:
        yield Scope(nc, prefix, ctx)


def load_phase(nc, M, D):
    with scope(nc, "ld") as s:
        loaded = s.sem("loaded")
        zeroed = s.sem("zeroed")
        with nc.Block() as block:
            @block.sync
            def _(sp):
                sp.dma_start(M.xT[:, :, :], D["xT"].rearrange("(k p) t -> p k t", p=P)).then_inc(loaded, 16)
                sp.dma_start(M.x[:, :, :], D["x"].rearrange("(n p) d -> p n d", p=P)).then_inc(loaded, 16)
                sp.wait_ge(loaded, 32)

            @block.gpsimd
            def _(pool):
                nc.gpsimd.memset(M.ident[:, :], 0.0).then_inc(zeroed, 1)
                nc.gpsimd.memset(M.ones[:, :], 1.0)
                nc.gpsimd.memset(M.ident16[:, :], 0.0).then_inc(zeroed, 1)
                pool.wait_ge(zeroed, 2)
                nc.gpsimd.affine_select(out=M.ident16[:, :], in_=M.ident16[:, :], compare_op=ALU.not_equal,
                                        fill=1.0, base=0, pattern=[[-1, P]], channel_multiplier=1)
                nc.gpsimd.affine_select(out=M.ident[:, :], in_=M.ident[:, :], compare_op=ALU.not_equal,
                                        fill=1.0, base=0, pattern=[[-1, P]],
                                        channel_multiplier=1).then_inc(zeroed, 1)


HEADS, HD = 32, 64
FEAT = HEADS * HD
PAIRS = HEADS // 2
CHUNKS = SEQ // P
HALVES = 2
UNITS = HALVES * BATCH
TURNS = PAIRS // HALVES


def gate_phase(nc, M, D, G):
    with scope(nc, "gt") as s:
        w = [s.sb(f"w{j}", [P, KD, P]) for j in range(HALVES)]
        bank = [s.ps(f"bank{n}") for n in range(4)]
        w_loaded = [s.sem(f"w_loaded{j}") for j in range(HALVES)]
        product = s.sem("product")
        gate = s.sem("gate")

        def done(i, k):
            return i * UNITS + (UNITS + k + 1)

        with nc.Block() as block:
            @block.sync
            def _(sp):
                with sp.Fori(0, TURNS) as i:
                    for j in range(HALVES):
                        sp.wait_ge(product, done(i, BATCH * (j + 1) - 1 - UNITS))
                        sp.dma_start(w[j][:, :, :],
                                     D["gate_w"][ds(i * HALVES + j, 1), :, :].rearrange("o p (k f) -> p (o k) f", k=KD)
                                     ).then_inc(w_loaded[j], 16)

            @block.tensor
            def _(pe):
                pe.sem_inc(product, UNITS)
                with pe.Fori(0, TURNS) as i:
                    for j in range(HALVES):
                        pe.wait_ge(w_loaded[j], i * 16 + 16)
                        for b in range(BATCH):
                            k = j * BATCH + b
                            pe.wait_ge(gate, done(i, k - 4))
                            for c in range(KD):
                                last = nc.tensor.matmul(bank[k % 4][:, :], w[j][:, c, :],
                                                        M.xT[:, c, b * BLK:(b + 1) * BLK],
                                                        start=(c == 0), stop=(c == KD - 1))
                            last.then_inc(product, 1)

            @block.scalar
            def _(act):
                act.sem_inc(gate, UNITS)
                with act.Fori(0, TURNS) as i:
                    for j in range(HALVES):
                        for b in range(BATCH):
                            k = j * BATCH + b
                            act.wait_ge(product, done(i, k))
                            nc.scalar.activation(G[:, ds(i * HALVES + j, 1), b * BLK:(b + 1) * BLK],
                                                 bank[k % 4][:, :].unsqueeze(1), ACT.Sigmoid).then_inc(gate, 1)


TBL = 2 * P + P + 2 + 1


def decay_table():
    import numpy as np
    base = 1.0 / 2.0 ** (8.0 / HEADS)
    slope = base ** (np.arange(HEADS) + 1.0) * (1.0 + 1e-5)
    r = np.arange(P, dtype=np.float64)
    t = np.zeros((PAIRS, P, TBL))
    for a in range(PAIRS):
        for h in range(2):
            m = slope[2 * a + h]
            dist = r[None, :] - r[:, None]
            t[a, :, h * P:(h + 1) * P] = np.where(dist >= 0, np.exp(-m * np.maximum(dist, 0)), 0.0)
            t[a, h * HD:(h + 1) * HD, 2 * P:3 * P] = np.exp(-m * (r + 1))[None, :]
            t[a, :, 3 * P + h] = np.exp(-m * (P - 1 - r))
            t[a, h * HD:(h + 1) * HD, 3 * P + 2] = np.exp(-m * P)
    return t.astype(np.float32)


def attention_phase(nc, M, D, G, squares_sum):
    with scope(nc, "at") as s:
        w = [s.sb(f"w{j}", [P, KD, 3 * P]) for j in range(HALVES)]
        tbl = [s.sb(f"tbl{j}", [P, TBL]) for j in range(HALVES)]
        nw = [s.sb(f"nw{j}", [P, 1]) for j in range(HALVES)]
        qT = [s.sb(f"qT{n}", [P, BLK]) for n in range(2)]
        kT = [s.sb(f"kT{n}", [P, BLK]) for n in range(2)]
        v = [s.sb(f"v{n}", [P, CHUNKS, P]) for n in range(2)]
        q_decayed = s.sb("q_decayed", [P, CHUNKS - 1, P])
        k_decayed = s.sb("k_decayed", [P, CHUNKS - 1, P])
        weights = s.sb("weights", [P, 2, BLK])
        state = s.sb("state", [P, CHUNKS - 1, P])
        sq = [s.sb(f"sq{n}", [P, BLK]) for n in range(2)]

        ps_q, ps_k, ps_v, ps_kt = s.ps("q"), s.ps("k"), s.ps("v"), s.ps("kt")
        ps_score = [s.ps(f"score{h}") for h in range(2)]
        ps_out, ps_state = s.ps("out"), s.ps("state_sum")

        w_loaded = [s.sem(f"w_loaded{j}") for j in range(HALVES)]
        q_product, k_product, v_product = s.sem("q_product"), s.sem("k_product"), s.sem("v_product")
        q_ready, k_ready, v_ready = s.sem("q_ready"), s.sem("k_ready"), s.sem("v_ready")
        k_turned = s.sem("k_turned")
        k_decay_ready = s.sem("k_decay_ready")
        q_decay_ready = s.sem("q_decay_ready")
        scores = s.sem("scores")
        weights_ready = s.sem("weights_ready")
        state_product = s.sem("state_product")
        state_step = s.sem("state_step")
        attended = s.sem("attended")
        squared = s.sem("squared")
        gated = s.sem("gated")
        summed = s.sem("summed")
        zeroed = s.sem("zeroed")

        def done(i, k, n=1):
            return (i * UNITS + (UNITS + k + 1)) * n

        with nc.Block() as block:
            @block.sync
            def _(sp):
                with sp.Fori(0, TURNS) as i:
                    for j in range(HALVES):
                        a = i * HALVES + j
                        sp.wait_ge(gated, done(i, BATCH * (j + 1) - 1 - UNITS))
                        sp.dma_start(w[j][:, :, :],
                                     D["qkv_w"][ds(a, 1), :, :].rearrange("o p (k f) -> p (o k) f", k=KD)
                                     ).then_inc(w_loaded[j], 16)
                        sp.dma_start(tbl[j][:, :], D["decay"][ds(a, 1), :, :].rearrange("o p f -> (o p) f")
                                     ).then_inc(w_loaded[j], 16)
                        sp.dma_start(nw[j][:, :], D["norm_w"][ds(a, 1), :, :].rearrange("o p f -> (o p) f")
                                     ).then_inc(w_loaded[j], 16)

            def project(pe, i, k):
                j, b, n = k // BATCH, k % BATCH, k % 2
                if b == 0:
                    pe.wait_ge(w_loaded[j], i * 48 + 48)
                for ready, bank, done_sem, col in ((q_ready, ps_q, q_product, 0), (k_ready, ps_k, k_product, P)):
                    pe.wait_ge(ready, done(i, k - 1))
                    for c in range(KD):
                        last = nc.tensor.matmul(bank[:, :], w[j][:, c, col:col + P],
                                                M.xT[:, c, b * BLK:(b + 1) * BLK],
                                                start=(c == 0), stop=(c == KD - 1))
                    last.then_inc(done_sem, 1)
                pe.wait_ge(v_ready, done(i, k - 1))
                for t in range(CHUNKS):
                    for c in range(KD):
                        last = nc.tensor.matmul(ps_v[:, t * P:(t + 1) * P],
                                                M.xT[:, c, b * BLK + t * P:b * BLK + (t + 1) * P],
                                                w[j][:, c, 2 * P:3 * P], start=(c == 0), stop=(c == KD - 1))
                last.then_inc(v_product, 1)

            @block.tensor
            def _(pe):
                pe.wait_ge(zeroed, 1)
                with pe.Fori(0, TURNS) as i:
                    project(pe, i, 0)
                    for k in range(UNITS):
                        n = k % 2
                        pe.wait_ge(k_ready, done(i, k))
                        pe.wait_ge(k_decay_ready, done(i, k - 1))
                        for t in range(CHUNKS - 1):
                            last = nc.tensor.transpose(ps_kt[:, t * P:(t + 1) * P], kT[n][:, t * P:(t + 1) * P],
                                                       M.ident[:, :])
                        last.then_inc(k_turned, 1)
                        pe.wait_ge(q_ready, done(i, k))
                        pe.wait_ge(weights_ready, done(i, k - 1, 2))
                        for t in range(CHUNKS):
                            for h in range(2):
                                r = slice(h * HD, (h + 1) * HD)
                                last = nc.tensor.matmul(ps_score[h][:, t * P:(t + 1) * P],
                                                        kT[n][r, t * P:(t + 1) * P], qT[n][r, t * P:(t + 1) * P],
                                                        start=True, stop=True)
                        last.then_inc(scores, 1)
                        if k + 1 < UNITS:
                            project(pe, i, k + 1)
                        pe.wait_ge(k_decay_ready, done(i, k))
                        pe.wait_ge(v_ready, done(i, k))
                        pe.wait_ge(state_step, done(i, k - 1, CHUNKS - 1))
                        for t in range(CHUNKS - 1):
                            for h in range(2):
                                r = slice(h * HD, (h + 1) * HD)
                                last = nc.tensor.matmul(ps_state[r, t * P + h * HD:t * P + (h + 1) * HD],
                                                        k_decayed[:, t, r], v[n][:, t, r], start=True, stop=True)
                        last.then_inc(state_product, 1)
                        pe.wait_ge(weights_ready, done(i, k, 2))
                        pe.wait_ge(gated, done(i, k - 1))
                        for t in range(CHUNKS):
                            for h in range(2):
                                r = slice(h * HD, (h + 1) * HD)
                                last = nc.tensor.matmul(ps_out[r, t * P:(t + 1) * P], v[n][:, t, r],
                                                        weights[:, h, t * P:(t + 1) * P], start=True,
                                                        stop=(t == 0), skip_group_check=True)
                            if t == 1:
                                pe.wait_ge(state_step, done(i, k, CHUNKS - 1))
                                pe.wait_ge(q_decay_ready, done(i, k))
                            if t > 0:
                                last = nc.tensor.matmul(ps_out[:, t * P:(t + 1) * P], state[:, t - 1, :],
                                                        q_decayed[:, t - 1, :], start=False, stop=True,
                                                        skip_group_check=True)
                        last.then_inc(attended, 1)

            @block.scalar
            def _(act):
                for sem in (q_ready, k_ready, v_ready, squared):
                    act.sem_inc(sem, UNITS)

                def evacuate(i, k):
                    n = k % 2
                    act.wait_ge(k_product, done(i, k) - UNITS)
                    act.wait_ge(attended, done(i, k - 2))
                    nc.scalar.activation(kT[n][:, :], ps_k[:, :], ACT.Silu).then_inc(k_ready, 1)
                    act.wait_ge(q_product, done(i, k) - UNITS)
                    act.wait_ge(q_decay_ready, done(i, k - 2))
                    nc.scalar.activation(qT[n][:, :], ps_q[:, :], ACT.Silu).then_inc(q_ready, 1)
                    act.wait_ge(v_product, done(i, k) - UNITS)
                    nc.scalar.activation(v[n][:, :, :].rearrange("p a b -> p (a b)"), ps_v[:, :],
                                         ACT.Silu).then_inc(v_ready, 1)

                with act.Fori(0, TURNS) as i:
                    evacuate(i, 0)
                    for k in range(UNITS):
                        if k + 1 < UNITS:
                            evacuate(i, k + 1)
                        act.wait_ge(attended, done(i, k))
                        act.wait_ge(summed, done(i, k - 2))
                        nc.scalar.activation(sq[k % 2][:, :], ps_out[:, :], ACT.Square).then_inc(squared, 1)

            @block.vector
            def _(dve):
                nc.vector.memset(ps_state[:, :], 0.0).then_inc(zeroed, 1)
                dve.sem_inc(k_decay_ready, UNITS)
                dve.sem_inc(weights_ready, 2 * UNITS)
                dve.sem_inc(state_step, (CHUNKS - 1) * UNITS)
                dve.sem_inc(gated, UNITS)
                with dve.Fori(0, TURNS) as i:
                    for k in range(UNITS):
                        j, b = k // BATCH, k % BATCH
                        t_ = tbl[j]
                        if b == 0:
                            dve.wait_ge(w_loaded[j], i * 48 + 48)
                        dve.wait_ge(k_turned, done(i, k) - UNITS)
                        nc.vector.tensor_tensor(
                            k_decayed[:, :, :].rearrange("p t (h e) -> p t h e", h=2),
                            ps_kt[:, 0:(CHUNKS - 1) * P].rearrange("p (t h e) -> p t h e", t=CHUNKS - 1, h=2),
                            t_[:, 3 * P:3 * P + 2].unsqueeze(1).unsqueeze(3).broadcast_to([P, CHUNKS - 1, 2, HD]),
                            ALU.mult).then_inc(k_decay_ready, 1)
                        dve.wait_ge(scores, done(i, k) - UNITS)
                        dve.wait_ge(attended, done(i, k - 1))
                        for h in range(2):
                            nc.vector.tensor_tensor(
                                weights[:, h, :].rearrange("p (t q) -> p t q", t=CHUNKS),
                                ps_score[h][:, :].rearrange("p (t q) -> p t q", t=CHUNKS),
                                t_[:, h * P:(h + 1) * P].unsqueeze(1).broadcast_to([P, CHUNKS, P]),
                                ALU.mult).then_inc(weights_ready, 1)
                        dve.wait_ge(state_product, done(i, k) - UNITS)
                        nc.vector.tensor_copy(state[:, 0, :], ps_state[:, 0:P]).then_inc(state_step, 1)
                        for t in range(1, CHUNKS - 1):
                            dve.wait_ge(state_step, done(i, k - 1, CHUNKS - 1) + t)
                            nc.vector.scalar_tensor_tensor(state[:, t, :], state[:, t - 1, :],
                                                           t_[:, 3 * P + 2:3 * P + 3],
                                                           ps_state[:, t * P:(t + 1) * P],
                                                           ALU.mult, ALU.add).then_inc(state_step, 1)
                        dve.wait_ge(squared, done(i, k))
                        g = G[:, ds(i * HALVES + j, 1), b * BLK:(b + 1) * BLK]
                        nc.vector.scalar_tensor_tensor(g, ps_out[:, :].unsqueeze(1), nw[j][:, 0:1], g,
                                                       ALU.mult, ALU.mult).then_inc(gated, 1)

            @block.gpsimd
            def _(pool):
                nc.gpsimd.memset(squares_sum[:, :], 0.0).then_inc(summed, 1)
                pool.wait_ge(summed, 1)
                pool.sem_inc(summed, UNITS - 1)
                pool.sem_inc(q_decay_ready, UNITS)
                pool.sem_inc(attended, UNITS)
                with pool.Fori(0, TURNS) as i:
                    for k in range(UNITS):
                        j, b, n = k // BATCH, k % BATCH, k % 2
                        if b == 0:
                            pool.wait_ge(w_loaded[j], i * 48 + 48)
                        pool.wait_ge(q_ready, done(i, k))
                        pool.wait_ge(attended, done(i, k - 1))
                        nc.gpsimd.tensor_tensor(q_decayed[:, :, :],
                                                qT[n][:, P:BLK].rearrange("p (t q) -> p t q", t=CHUNKS - 1),
                                                tbl[j][:, 2 * P:3 * P].unsqueeze(1).broadcast_to([P, CHUNKS - 1, P]),
                                                ALU.mult).then_inc(q_decay_ready, 1)
                        pool.wait_ge(squared, done(i, k))
                        part = squares_sum[:, b * BLK:(b + 1) * BLK]
                        nc.gpsimd.tensor_tensor(part, part, sq[n][:, :], ALU.add).then_inc(summed, 1)


class Residual:

    TPB = BLK // P

    def __init__(self, nc, M, s, residual):
        self.nc, self.M, self.residual = nc, M, residual
        self.y = s.sb("branch", [P, KD, BLK])
        self.bank = [s.ps(f"turned{n}") for n in range(KD)]
        self.turned = s.sem("turned")
        self.added = s.sem("added")

    def tensor(self, pe, i, y_sem, y_value):
        nc = self.nc
        pe.wait_ge(y_sem, y_value)
        pe.wait_ge(self.added, i * KD + KD)
        for t in range(self.TPB):
            for c in range(KD):
                last = nc.tensor.transpose(self.bank[t // 2][:, (t % 2) * DM + c * P:(t % 2) * DM + (c + 1) * P],
                                           self.y[:, c, t * P:(t + 1) * P], self.M.ident[:, :])
            if t % 2:
                last.then_inc(self.turned, 1)

    def vector(self, dve, i):
        for h in range(KD):
            x = self.M.x[:, ds(i * self.TPB + 2 * h, 2), :]
            dve.wait_ge(self.turned, i * KD + h + 1)
            self.nc.vector.scalar_tensor_tensor(x, x, float(self.residual),
                                                self.bank[h][:, :].rearrange("p (t d) -> p t d", t=2),
                                                ALU.mult, ALU.add).then_inc(self.added, 1)


def layernorm_phase(nc, M, turn_back=True):
    with scope(nc, f"ln{M.norms}") as s:
        M.norms += 1
        stats = s.sb("stats", [P, TILES, 6])
        mv = s.sb("mv", [P, TILES, 2])
        var = s.sb("var", [P, TILES])
        rstd = s.sb("rstd", [P, TILES])
        banks = [s.ps(f"bank{n}") for n in range(4)]
        stat, aggregate, spread, root, scale = (s.sem(n) for n in ("stat", "aggregate", "spread", "root", "scale"))
        normed, turned, stored = s.sem("normed"), s.sem("turned"), s.sem("stored")
        with nc.Block() as block:
            @block.vector
            def _(dve):
                for t in range(TILES):
                    nc.vector.bn_stats(stats[:, t, :], M.x[:, t, :]).then_inc(stat, 1)
                for t in range(TILES):
                    dve.wait_ge(stat, t + 1)
                    nc.vector.bn_aggr(mv[:, t, :], stats[:, t, :]).then_inc(aggregate, 1)
                dve.wait_ge(aggregate, TILES)
                nc.vector.tensor_scalar(var[:, :], mv[:, :, 1], LN_EPS, None, ALU.add).then_inc(spread, 1)
                dve.wait_ge(root, 1)
                nc.vector.reciprocal(rstd[:, :], rstd[:, :]).then_inc(scale, 1)
                dve.wait_ge(scale, 1)
                for t in range(TILES):
                    nc.vector.tensor_scalar(M.x[:, t, :], M.x[:, t, :], mv[:, t, 0:1], rstd[:, t:t + 1],
                                            ALU.subtract, ALU.mult).then_inc(normed, 1)

            @block.scalar
            def _(act):
                act.wait_ge(spread, 1)
                nc.scalar.activation(rstd[:, :], var[:, :], ACT.Sqrt).then_inc(root, 1)
                if turn_back:
                    for t in range(0, TILES, 2):
                        act.wait_ge(turned, t + 2)
                        nc.scalar.activation(M.xT[:, :, t * P:(t + 2) * P],
                                             banks[t // 2 % 4][:, :].rearrange("p (k t) -> p k t", k=KD),
                                             ACT.Copy).then_inc(stored, 2)

            @block.tensor
            def _(pe):
                if turn_back:
                    for t in range(TILES):
                        pe.wait_ge(normed, t + 1)
                        if t >= 8:
                            pe.wait_ge(stored, t // 2 * 2 - 6)
                        for c in range(KD):
                            last = nc.tensor.transpose(
                                banks[t // 2 % 4][:, c * DM + (t % 2) * P:c * DM + (t % 2 + 1) * P],
                                M.x[:, t, c * P:(c + 1) * P], M.ident[:, :])
                        last.then_inc(turned, 1)


def projection_phase(nc, M, D, G, squares_sum):
    with scope(nc, "pr") as s:
        wo = s.sb("wo", [P, PAIRS, DM])
        rms = s.sb("rms", [P, BLK])
        inv = s.sb("inv", [P, BLK])
        eps = s.sb("eps", [P, 1])
        bank = [s.ps(f"bank{n}") for n in range(KD)]
        ps_sum = s.ps("sum")
        wo_loaded = s.sem("wo_loaded")
        ready, summed, rooted, inverted = s.sem("ready"), s.sem("summed"), s.sem("rooted"), s.sem("inverted")
        product, scaled = s.sem("product"), s.sem("scaled")
        res = Residual(nc, M, s, 1.0)

        with nc.Block() as block:
            @block.sync
            def _(sp):
                sp.dma_start(wo[:, :, :], D["out_w"].rearrange("(a p) d -> p a d", p=P)).then_inc(wo_loaded, 16)

            @block.tensor
            def _(pe):
                pe.wait_ge(wo_loaded, 16)
                with pe.Fori(0, NBLK) as i:
                    pe.wait_ge(rooted, i + 1)
                    nc.tensor.matmul(ps_sum[:, :], M.ones[:, :], squares_sum[:, ds(i * BLK, BLK)],
                                     start=True, stop=True).then_inc(summed, 1)
                    for d in range(KD):
                        pe.wait_ge(scaled, i * KD + d + 1)
                        for a in range(PAIRS):
                            last = nc.tensor.matmul(bank[d][:, :], wo[:, a, d * P:(d + 1) * P],
                                                    G[:, a, ds(i * BLK, BLK)],
                                                    start=(a == 0), stop=(a == PAIRS - 1))
                        last.then_inc(product, 1)
                    res.tensor(pe, i, scaled, i * KD + 2 * KD)

            @block.scalar
            def _(act):
                act.sem_inc(rooted, 1)
                act.wait_ge(ready, 1)
                with act.Fori(0, NBLK) as i:
                    act.wait_ge(summed, i + 1)
                    act.wait_ge(inverted, i + 1)
                    nc.scalar.activation(rms[:, :], ps_sum[:, :], ACT.Sqrt, scale=1.0 / FEAT,
                                         bias=eps[:, 0:1]).then_inc(rooted, 1)

            @block.vector
            def _(dve):
                nc.vector.memset(eps[:, :], 1e-5).then_inc(ready, 1)
                dve.sem_inc(inverted, 1)
                dve.sem_inc(scaled, KD)
                dve.sem_inc(res.added, KD)
                with dve.Fori(0, NBLK) as i:
                    dve.wait_ge(rooted, i + 2)
                    nc.vector.reciprocal(inv[:, :], rms[:, :]).then_inc(inverted, 1)
                    dve.wait_ge(inverted, i + 2)
                    for d in range(KD):
                        dve.wait_ge(product, i * KD + d + 1)
                        nc.vector.tensor_tensor(res.y[:, d, :], bank[d][:, :], inv[:, :], ALU.mult
                                                ).then_inc(scaled, 1)
                    res.vector(dve, i)


ROUTED, SHARED, FF = 16, 2, 176
TOP_K = 4
EXPERTS = ROUTED + SHARED
PARTS = 3
FTILES = -(-EXPERTS * FF // P)
LOADS = 5
FPL = FTILES // LOADS


def expert_rows():
    import numpy as np
    t = np.zeros((PARTS, EXPERTS, FTILES * P))
    for e in range(EXPERTS):
        t[:, e, e * FF:(e + 1) * FF] = 1.0
    return t.reshape(PARTS * EXPERTS, FTILES * P).astype(np.uint16) * ONE_BITS


def router_phase(nc, M, D, gates, gate_parts):
    with scope(nc, "ro") as s:
        cent = s.sb("cent", [P, KD, ROUTED])
        bias = s.sb("bias", [P, ROUTED])
        score = s.sb("score", [P, TILES, ROUTED])
        top = s.sb("top", [P, TILES, 8])
        kept = s.sb("kept", [P, TILES, ROUTED])
        total = s.sb("total", [P, TILES])
        g = s.sb("g", [P, TILES, EXPERTS])
        parts = s.sb("parts", [P, TILES, PARTS, EXPERTS], BF16)
        rest = [s.sb(f"rest{n}", [P, TILES, EXPERTS]) for n in range(PARTS - 1)]
        ps_score = s.ps("score")
        ps_gate = [s.ps(f"gate{n}") for n in range(NBLK)]
        ps_part = [s.ps(f"part{n}", (P, 1024), BF16) for n in range(2)]
        loaded, product, squashed, step = s.sem("loaded"), s.sem("product"), s.sem("squashed"), s.sem("step")
        g_ready, parts_ready, turned = s.sem("g_ready"), s.sem("parts_ready"), s.sem("turned")
        with nc.Block() as block:
            @block.sync
            def _(sp):
                sp.dma_start(cent[:, :, :], D["centroids"].rearrange("(k p) e -> p k e", p=P)).then_inc(loaded, 16)
                sp.dma_start(bias[:, :], D["route_bias"].partition_broadcast(P)).then_inc(loaded, 16)

            @block.tensor
            def _(pe):
                pe.wait_ge(loaded, 32)
                for t in range(TILES):
                    for c in range(KD):
                        last = nc.tensor.matmul(ps_score[:, t * ROUTED:(t + 1) * ROUTED],
                                                M.xT[:, c, t * P:(t + 1) * P], cent[:, c, :],
                                                start=(c == 0), stop=(c == KD - 1))
                last.then_inc(product, 1)
                pe.wait_ge(g_ready, 1)
                for t in range(TILES):
                    last = nc.tensor.transpose(ps_gate[t // 4][0:EXPERTS, t % 4 * P:(t % 4 + 1) * P],
                                               g[:, t, :], M.ident[:, :])
                    if t % 4 == 3:
                        last.then_inc(turned, 1)
                pe.wait_ge(parts_ready, PARTS)
                for t in range(TILES):
                    last = nc.tensor.transpose(ps_part[t // 8][0:PARTS * EXPERTS, t % 8 * P:(t % 8 + 1) * P],
                                               parts[:, t, :, :].rearrange("p a e -> p (a e)"), M.ident16[:, :])
                    if t % 8 == 7:
                        last.then_inc(turned, 1)

            @block.scalar
            def _(act):
                act.wait_ge(product, 1)
                nc.scalar.activation(score[:, :, :].rearrange("p t e -> p (t e)"),
                                     ps_score[:, 0:TILES * ROUTED], ACT.Sigmoid).then_inc(squashed, 1)
                for n in range(NBLK):
                    act.wait_ge(turned, n + 1)
                    nc.scalar.activation(gates[:, n * BLK:(n + 1) * BLK], ps_gate[n][0:EXPERTS, :], ACT.Copy)
                for n in range(2):
                    act.wait_ge(turned, NBLK + n + 1)
                    nc.scalar.activation(gate_parts[:, n * 1024:(n + 1) * 1024],
                                         ps_part[n][0:PARTS * EXPERTS, :], ACT.Copy)

            @block.vector
            def _(dve):
                def wide(ap):
                    return ap.broadcast_to([P, TILES, ROUTED])

                nc.vector.memset(g[:, :, ROUTED:EXPERTS], 1.0)
                dve.wait_ge(loaded, 32)
                dve.wait_ge(squashed, 1)
                nc.vector.tensor_tensor(score[:, :, :], score[:, :, :], wide(bias[:, :].unsqueeze(1)),
                                        ALU.add).then_inc(step, 1)
                dve.wait_ge(step, 1)
                for t in range(TILES):
                    last = nc.vector.max(top[:, t, :], score[:, t, :])
                last.then_inc(step, 1)
                dve.wait_ge(step, 2)
                nc.vector.tensor_tensor(kept[:, :, :], score[:, :, :], wide(top[:, :, TOP_K - 1:TOP_K]),
                                        ALU.is_ge).then_inc(step, 1)
                dve.wait_ge(step, 3)
                nc.vector.tensor_tensor(kept[:, :, :], kept[:, :, :], score[:, :, :], ALU.mult).then_inc(step, 1)
                dve.wait_ge(step, 4)
                nc.vector.tensor_reduce(total[:, :], kept[:, :, :], AX.X, ALU.add).then_inc(step, 1)
                dve.wait_ge(step, 5)
                nc.vector.tensor_scalar(total[:, :], total[:, :], 1e-8, None, ALU.max).then_inc(step, 1)
                dve.wait_ge(step, 6)
                nc.vector.reciprocal(total[:, :], total[:, :]).then_inc(step, 1)
                dve.wait_ge(step, 7)
                nc.vector.tensor_tensor(g[:, :, 0:ROUTED], kept[:, :, :], wide(total[:, :].unsqueeze(2)),
                                        ALU.mult).then_inc(g_ready, 1)
                dve.wait_ge(g_ready, 1)
                whole = g
                for n in range(PARTS):
                    nc.vector.tensor_copy(parts[:, :, n, :], whole[:, :, :]).then_inc(parts_ready, 1)
                    if n < PARTS - 1:
                        dve.wait_ge(parts_ready, n + 1)
                        nc.vector.tensor_tensor(rest[n][:, :, :], whole[:, :, :], parts[:, :, n, :],
                                                ALU.subtract).then_inc(step, 1)
                        dve.wait_ge(step, 8 + n)
                        whole = rest[n]


def experts_phase(nc, M, D):
    with scope(nc, "mo") as s:
        gates = s.sb("gates", [EXPERTS, TOKENS])
        gate_parts = s.sb("gate_parts", [PARTS * EXPERTS, TOKENS], BF16)
        router_phase(nc, M, D, gates, gate_parts)
        w1 = s.sb("w1", [P, KD, FTILES * P])
        w2 = s.sb("w2", [P, FTILES, DM])
        b1 = s.sb("b1", [P, FTILES])
        b2 = s.sb("b2", [EXPERTS, DM])
        rows = s.sb("rows", [PARTS * EXPERTS, FTILES * P], BF16)
        NH = 3
        hidden = [s.sb(f"hidden{n}", [P, BLK]) for n in range(2)]
        gated = [s.sb(f"gated{n}", [P, BLK]) for n in range(NH)]
        ps_h = [s.ps(f"h{n}") for n in range(2)]
        ps_g = [s.ps(f"g{n}") for n in range(2)]
        acc = [s.ps(f"acc{n}") for n in range(KD)]
        small_loaded = s.sem("small_loaded")
        w_loaded = [s.sem(f"w_loaded{n}") for n in range(LOADS)]
        h_product, g_product, relu_ready = s.sem("h_product"), s.sem("g_product"), s.sem("relu_ready")
        gated_ready, used = s.sem("gated_ready"), s.sem("used")
        product, y_ready = s.sem("product"), s.sem("y_ready")
        res = Residual(nc, M, s, 2.0)

        def done(i, f):
            return i * FTILES + (FTILES + f + 1)

        with nc.Block() as block:
            @block.sync
            def _(sp):
                sp.dma_start(b1[:, :], D["b1"]).then_inc(small_loaded, 16)
                sp.dma_start(b2[:, :], D["b2"]).then_inc(small_loaded, 16)
                sp.dma_start(rows[:, :], D["expert_rows"].bitcast(BF16)).then_inc(small_loaded, 16)
                for n in range(LOADS):
                    c = slice(n * FPL * P, (n + 1) * FPL * P)
                    sp.dma_start(w1[:, :, c], D["w1"].rearrange("(k p) f -> p k f", p=P)[:, :, c]
                                 ).then_inc(w_loaded[n], 16)
                    sp.dma_start(w2[:, n * FPL:(n + 1) * FPL, :],
                                 D["w2"].rearrange("(f p) d -> p f d", p=P)[:, n * FPL:(n + 1) * FPL, :]
                                 ).then_inc(w_loaded[n], 16)

            @block.tensor
            def _(pe):
                pe.sem_inc(used, FTILES)
                pe.wait_ge(small_loaded, 48)
                with pe.Fori(0, NBLK) as i:
                    for f in range(FTILES + 2):
                        if f < FTILES:
                            if f % FPL == 0:
                                pe.wait_ge(w_loaded[f // FPL], 32)
                            fs = slice(f * P, (f + 1) * P)
                            pe.wait_ge(relu_ready, done(i, f - 2))
                            for c in range(KD):
                                last = nc.tensor.matmul(ps_h[f % 2][:, :], w1[:, c, fs],
                                                        M.xT[:, c, ds(i * BLK, BLK)],
                                                        start=(c == 0), stop=(c == KD - 1))
                            last.then_inc(h_product, 1)
                            wait_apart(pe, gated_ready, done(i, f - 2), M.passed)
                            nc.tensor.matmul(ps_g[f % 2][:, :], rows[:, fs], gate_parts[:, ds(i * BLK, BLK)],
                                             start=True, stop=True).then_inc(g_product, 1)
                        if f == 0:
                            pe.wait_ge(y_ready, i * KD + KD)
                            for d in range(KD):
                                nc.tensor.matmul(acc[d][:, :], b2[:, d * P:(d + 1) * P],
                                                 gates[:, ds(i * BLK, BLK)], start=True, stop=False)
                        if f >= 2:
                            g = f - 2
                            pe.wait_ge(gated_ready, done(i, g))
                            for d in range(KD):
                                last = nc.tensor.matmul(acc[d][:, :], w2[:, g, d * P:(d + 1) * P],
                                                        gated[g % NH][:, :], start=False,
                                                        stop=(g == FTILES - 1))
                            last.then_inc(used, 1)
                    res.tensor(pe, i, y_ready, i * KD + 2 * KD)

            @block.scalar
            def _(act):
                act.sem_inc(relu_ready, FTILES)
                act.sem_inc(y_ready, KD)
                act.wait_ge(small_loaded, 48)
                with act.Fori(0, NBLK) as i:
                    for f in range(FTILES):
                        act.wait_ge(h_product, done(i, f) - FTILES)
                        act.wait_ge(gated_ready, done(i, f - 2))
                        nc.scalar.activation(hidden[f % 2][:, :], ps_h[f % 2][:, :], ACT.Relu,
                                             bias=b1[:, f:f + 1]).then_inc(relu_ready, 1)
                    act.wait_ge(used, done(i, FTILES - 1))
                    for d in range(KD):
                        nc.scalar.activation(res.y[:, d, :], acc[d][:, :], ACT.Copy).then_inc(y_ready, 1)

            @block.vector
            def _(dve):
                dve.sem_inc(gated_ready, FTILES)
                dve.sem_inc(res.added, KD)
                with dve.Fori(0, NBLK) as i:
                    for f in range(FTILES):
                        dve.wait_ge(relu_ready, done(i, f))
                        dve.wait_ge(g_product, done(i, f) - FTILES)
                        dve.wait_ge(used, done(i, f - NH))
                        nc.vector.tensor_tensor(gated[f % NH][:, :], hidden[f % 2][:, :], ps_g[f % 2][:, :],
                                                ALU.mult).then_inc(gated_ready, 1)
                    res.vector(dve, i)


STATES, DT_RANK = 16, 128
BC = 2 * STATES
HALF = 2 * SEQ
SEQ_HALF = HALF // SEQ


def state_rows():
    import numpy as np
    t = np.zeros((PARTS, BC, BC, P))
    t[:, np.arange(BC), np.arange(BC), :] = 1.0
    return t.reshape(PARTS * BC, BC * P).astype(np.uint16) * ONE_BITS


def step_phase(nc, M, D, dt, dtx, bc_parts, decay):
    with scope(nc, "dt") as s:
        wx = s.sb("wx", [P, KD, DT_RANK + PARTS * BC])
        wdt = s.sb("wdt", [P, DM])
        bx = s.sb("bx", [P, 1])
        bbc = s.sb("bbc", [PARTS * BC, 1])
        bdt = s.sb("bdt", [P, KD])
        rank = s.sb("rank", [P, BLK])
        bc = s.sb("bc", [PARTS * BC, BLK])
        high = s.sb("high", [PARTS * BC, BLK], BF16)
        rest = s.sb("rest", [PARTS * BC, BLK])
        mid = s.sb("mid", [PARTS * BC, BLK], BF16)
        rest2 = s.sb("rest2", [PARTS * BC, BLK])
        size = [s.sb(f"size{d}", [P, BLK]) for d in range(KD)]
        e = [s.sb(f"e{d}", [P, BLK]) for d in range(KD)]
        log = [s.sb(f"log{d}", [P, BLK]) for d in range(KD)]
        one_e = [s.sb(f"one_e{d}", [P, BLK]) for d in range(KD)]
        lost = [s.sb(f"lost{d}", [P, BLK]) for d in range(KD)]
        positive = [s.sb(f"positive{d}", [P, BLK]) for d in range(KD)]
        ps_rank, ps_bc = s.ps("rank"), s.ps("bc")
        ps_dt = [s.ps(f"dt{d}") for d in range(KD)]
        loaded, rank_product, bc_product, dt_product = (s.sem(n) for n in ("loaded", "rank_product", "bc_product", "dt_product"))
        rank_ready, bc_ready, bc_step = s.sem("rank_ready"), s.sem("bc_ready"), s.sem("bc_step")
        size_ready, e_ready, log_ready, dt_step = s.sem("size_ready"), s.sem("e_ready"), s.sem("log_ready"), s.sem("dt_step")
        bc_kept = s.sem("bc_kept")
        a_step = s.sem("a_step")
        LOADED = 7 * 16
        VS = 6
        with nc.Block() as block:
            @block.sync
            def _(sp):
                for to, of in ((wx[:, :, :], D["wx"].rearrange("(k p) r -> p k r", p=P)), (wdt[:, :], D["wdt"]),
                               (bx[:, :], D["bx"][0:DT_RANK, :]), (bbc[:, :], D["bx"][DT_RANK:, :]),
                               (bdt[:, :], D["bdt"]), (decay[:, :, :], D["a_log"]),
                               (M.state_rows[:, :], D["state_rows"].bitcast(BF16))):
                    sp.dma_start(to, of).then_inc(loaded, 16)

            @block.tensor
            def _(pe):
                pe.wait_ge(loaded, LOADED)
                with pe.Fori(0, NBLK) as i:
                    for to, cols, sem, free in ((ps_rank[:, :], slice(0, DT_RANK), rank_product, rank_ready),
                                                (ps_bc[0:PARTS * BC, :], slice(DT_RANK, DT_RANK + PARTS * BC),
                                                 bc_product, bc_ready)):
                        pe.wait_ge(free, i + 1)
                        for c in range(KD):
                            last = nc.tensor.matmul(to, wx[:, c, cols], M.xT[:, c, ds(i * BLK, BLK)],
                                                    start=(c == 0), stop=(c == KD - 1))
                        last.then_inc(sem, 1)
                    pe.wait_ge(rank_ready, i + 2)
                    pe.wait_ge(dt_step, i * KD * VS + 1)
                    for d in range(KD):
                        nc.tensor.matmul(ps_dt[d][:, :], wdt[:, d * P:(d + 1) * P], rank[:, :],
                                         start=True, stop=True).then_inc(dt_product, 1)

            @block.scalar
            def _(act):
                act.sem_inc(rank_ready, 1)
                act.sem_inc(bc_ready, 1)
                act.wait_ge(loaded, LOADED)
                nc.scalar.activation(decay[:, :, :], decay[:, :, :], ACT.Exp).then_inc(a_step, 1)
                with act.Fori(0, NBLK) as i:
                    act.wait_ge(rank_product, i + 1)
                    nc.scalar.activation(rank[:, :], ps_rank[:, :], ACT.Identity, bias=bx[:, 0:1]).then_inc(rank_ready, 1)
                    act.wait_ge(bc_product, i + 1)
                    act.wait_ge(bc_kept, i + 1)
                    nc.scalar.activation(bc[:, :], ps_bc[0:PARTS * BC, :], ACT.Identity, bias=bbc[:, 0:1]
                                         ).then_inc(bc_ready, 1)
                    for d in range(KD):
                        act.wait_ge(dt_product, i * KD + d + 1)
                        act.wait_ge(dt_step, i * KD * VS + 1)
                        nc.scalar.activation(size[d][:, :], ps_dt[d][:, :], ACT.Abs, bias=bdt[:, d:d + 1]
                                             ).then_inc(size_ready, 1)
                    for d in range(KD):
                        act.wait_ge(size_ready, i * KD + d + 1)
                        nc.scalar.activation(e[d][:, :], size[d][:, :], ACT.Exp, scale=-1.0).then_inc(e_ready, 1)
                    for d in range(KD):
                        act.wait_ge(e_ready, i * KD + d + 1)
                        nc.scalar.activation(log[d][:, :], e[d][:, :], ACT.Ln, bias=1.0).then_inc(log_ready, 1)

            @block.vector
            def _(dve):
                dve.sem_inc(dt_step, 1)
                dve.wait_ge(a_step, 1)
                nc.vector.tensor_scalar(decay[:, :, :], decay[:, :, :], -1.0, None, ALU.mult).then_inc(a_step, 1)
                dve.wait_ge(loaded, LOADED)
                dve.sem_inc(bc_kept, 1)
                with dve.Fori(0, NBLK) as i:
                    def keep(n, of):
                        rows = slice(n * BC, (n + 1) * BC)
                        return nc.vector.tensor_copy(bc_parts[rows, ds(i * BLK, BLK)], of[rows, :])

                    wait_apart(dve, bc_ready, i + 2, M.passed)
                    nc.vector.tensor_copy(high[:, :], bc[:, :]).then_inc(bc_step, 1)
                    keep(0, bc)
                    dve.wait_ge(bc_step, i * 4 + 1)
                    nc.vector.tensor_tensor(rest[:, :], bc[:, :], high[:, :], ALU.subtract).then_inc(bc_step, 1)
                    wait_apart(dve, bc_step, i * 4 + 2, M.passed)
                    nc.vector.tensor_copy(mid[:, :], rest[:, :]).then_inc(bc_step, 1)
                    keep(1, rest)
                    dve.wait_ge(bc_step, i * 4 + 3)
                    nc.vector.tensor_tensor(rest2[:, :], rest[:, :], mid[:, :], ALU.subtract).then_inc(bc_step, 1)
                    wait_apart(dve, bc_step, i * 4 + 4, M.passed)
                    keep(2, rest2).then_inc(bc_kept, 1)
                    for d in range(KD):
                        at = lambda n: i * KD * VS + (d * VS + n + 1)
                        dt_out, x_in = dt[:, d:d + 1, ds(i * BLK, BLK)], M.xT[:, d:d + 1, ds(i * BLK, BLK)]
                        dtx_out = dtx[:, d:d + 1, ds(i * BLK, BLK)]
                        dve.wait_ge(size_ready, i * KD + d + 1)
                        nc.vector.tensor_scalar(positive[d][:, :], ps_dt[d][:, :], bdt[:, d:d + 1], 0.0,
                                                ALU.add, ALU.max).then_inc(dt_step, 1)
                        dve.wait_ge(e_ready, i * KD + d + 1)
                        nc.vector.tensor_scalar(one_e[d][:, :], e[d][:, :], 1.0, None, ALU.add).then_inc(dt_step, 1)
                        dve.wait_ge(dt_step, at(2))
                        nc.vector.scalar_tensor_tensor(lost[d][:, :], one_e[d][:, :], 1.0, e[d][:, :],
                                                       ALU.subtract, ALU.subtract).then_inc(dt_step, 1)
                        dve.wait_ge(log_ready, i * KD + d + 1)
                        dve.wait_ge(dt_step, at(3))
                        nc.vector.tensor_tensor(log[d][:, :], log[d][:, :], lost[d][:, :], ALU.subtract
                                                ).then_inc(dt_step, 1)
                        dve.wait_ge(dt_step, at(4))
                        nc.vector.tensor_tensor(dt_out, log[d][:, :].unsqueeze(1), positive[d][:, :].unsqueeze(1),
                                                ALU.add).then_inc(dt_step, 1)
                        dve.wait_ge(dt_step, at(5))
                        nc.vector.tensor_tensor(dtx_out, dt_out, x_in, ALU.mult).then_inc(dt_step, 1)

def scan_phase(nc, M, D):
    with scope(nc, "sc") as s:
        dt = s.sb("dt", [P, KD, TOKENS])
        dtx = s.sb("dtx", [P, KD, TOKENS])
        bc_parts = s.sb("bc_parts", [PARTS * BC, TOKENS], BF16)
        decay = s.sb("decay", [P, KD, STATES])
        M.state_rows = s.sb("state_rows", [PARTS * BC, BC * P], BF16)
        y = s.sb("y", [P, KD, TOKENS])
        step_phase(nc, M, D, dt, dtx, bc_parts, decay)
        bs = [s.sb(f"bs{n}", [P, HALF]) for n in range(2)]
        a = [[s.sb(f"a{n}{d}", [P, HALF]) for d in range(KD)] for n in range(2)]
        bx = [[s.sb(f"bx{n}{d}", [P, HALF]) for d in range(KD)] for n in range(2)]
        h = [s.sb(f"h{d}", [P, HALF]) for d in range(KD)]
        hc = [[s.sb(f"hc{n}{d}", [P, HALF]) for d in range(KD)] for n in range(2)]
        with scope(nc, "s2") as q:
            ps_b, ps_c = q.ps("b", (P, HALF)), q.ps("c", (P, HALF))
            ps_y = [q.ps(f"y{d}", (P, HALF)) for d in range(KD)]
            b_product, c_product, y_sum = q.sem("b_product"), q.sem("c_product"), q.sem("y_sum")
            b_ready, a_ready, bx_ready = q.sem("b_ready"), q.sem("a_ready"), q.sem("bx_ready")
            scanned, hc_ready, y_ready = q.sem("scanned"), q.sem("hc_ready"), q.sem("y_ready")

            def done(i, n):
                return i * STATES + (STATES + n + 1)

            def done2(i, n, d=KD - 1):
                return i * (STATES * KD) + (STATES + n) * KD + d + 1

            with nc.Block() as block:
                def spread(i, to, row):
                    for t in range(HALF // BLK):
                        last = nc.tensor.matmul(to[:, t * BLK:(t + 1) * BLK],
                                                M.state_rows[:, row * P:(row + 1) * P],
                                                bc_parts[:, ds(i * HALF + t * BLK, BLK)], start=True, stop=True)
                    return last

                @block.tensor
                def _(pe):
                    pe.sem_inc(y_sum, STATES * KD)
                    with pe.Fori(0, TOKENS // HALF) as i:
                        for n in range(STATES + 1):
                            if n < STATES:
                                wait_apart(pe, b_ready, done(i, n - 1), M.passed)
                                spread(i, ps_b, n).then_inc(b_product, 1)
                                wait_apart(pe, hc_ready, done2(i, n - 1), M.passed)
                                spread(i, ps_c, STATES + n).then_inc(c_product, 1)
                            if n == 1:
                                pe.wait_ge(y_ready, i * KD + KD)
                            if n >= 1:
                                for d in range(KD):
                                    pe.wait_ge(hc_ready, done2(i, n - 1, d))
                                    for t in range(HALF // BLK):
                                        last = nc.tensor.matmul(ps_y[d][:, t * BLK:(t + 1) * BLK], M.ident[:, :],
                                                                hc[(n - 1) % 2][d][:, t * BLK:(t + 1) * BLK],
                                                                start=(n == 1), stop=(n == STATES))
                                    last.then_inc(y_sum, 1)

                @block.scalar
                def _(act):
                    act.sem_inc(b_ready, STATES)
                    act.sem_inc(y_ready, KD)
                    with act.Fori(0, TOKENS // HALF) as i:
                        for n in range(STATES):
                            act.wait_ge(b_product, done(i, n) - STATES)
                            act.wait_ge(bx_ready, done2(i, n - 2))
                            nc.scalar.activation(bs[n % 2][:, :], ps_b[:, :], ACT.Copy).then_inc(b_ready, 1)
                            for d in range(KD):
                                wait_apart(act, scanned, done2(i, n - 2, d), M.passed)
                                nc.scalar.activation(a[n % 2][d][:, :].unsqueeze(1),
                                                     dt[:, d:d + 1, ds(i * HALF, HALF)], ACT.Exp,
                                                     scale=decay[:, d, n:n + 1]).then_inc(a_ready, 1)
                        for d in range(KD):
                            act.wait_ge(y_sum, done2(i, STATES - 1, d))
                            nc.scalar.activation(y[:, d:d + 1, ds(i * HALF, HALF)], ps_y[d][:, :].unsqueeze(1),
                                                 ACT.Copy).then_inc(y_ready, 1)

                @block.gpsimd
                def _(pool):
                    pool.sem_inc(bx_ready, STATES * KD)
                    with pool.Fori(0, TOKENS // HALF) as i:
                        for n in range(STATES):
                            wait_apart(pool, b_ready, done(i, n), M.passed)
                            for d in range(KD):
                                wait_apart(pool, scanned, done2(i, n - 2, d), M.passed)
                                nc.gpsimd.tensor_tensor(bx[n % 2][d][:, :].unsqueeze(1),
                                                        dtx[:, d:d + 1, ds(i * HALF, HALF)],
                                                        bs[n % 2][:, :].unsqueeze(1), ALU.mult).then_inc(bx_ready, 1)

                @block.vector
                def _(dve):
                    dve.sem_inc(scanned, STATES * KD)
                    dve.sem_inc(hc_ready, STATES * KD)
                    with dve.Fori(0, TOKENS // HALF) as i:
                        for n in range(STATES):
                            for d in range(KD):
                                dve.wait_ge(a_ready, done2(i, n, d) - STATES * KD)
                                dve.wait_ge(bx_ready, done2(i, n, d))
                                dve.wait_ge(hc_ready, done2(i, n - 1, d))
                                for q_ in range(SEQ_HALF):
                                    t = slice(q_ * SEQ, (q_ + 1) * SEQ)
                                    last = nc.vector.tensor_tensor_scan(h[d][:, t], a[n % 2][d][:, t],
                                                                        bx[n % 2][d][:, t], 0.0, ALU.mult, ALU.add)
                                last.then_inc(scanned, 1)
                            for d in range(KD):
                                dve.wait_ge(scanned, done2(i, n, d))
                                dve.wait_ge(c_product, done(i, n) - STATES)
                                dve.wait_ge(y_sum, done2(i, n - 2, d))
                                nc.vector.tensor_tensor(hc[n % 2][d][:, :], h[d][:, :], ps_c[:, :], ALU.mult
                                                        ).then_inc(hc_ready, 1)
        with scope(nc, "s3") as q:
            res = Residual(nc, M, q, 1.0)
            copied = q.sem("copied")
            with nc.Block() as block:
                @block.tensor
                def _(pe):
                    with pe.Fori(0, NBLK) as i:
                        res.tensor(pe, i, copied, i + 1)

                @block.scalar
                def _(act):
                    with act.Fori(0, NBLK) as i:
                        act.wait_ge(res.added, i * KD + KD)
                        nc.scalar.activation(res.y[:, :, :], y[:, :, ds(i * BLK, BLK)], ACT.Copy).then_inc(copied, 1)

                @block.vector
                def _(dve):
                    dve.sem_inc(res.added, KD)
                    with dve.Fori(0, NBLK) as i:
                        res.vector(dve, i)


CROSS, PRIV, RETR = 1024, 128, 128
RHEADS, K_HEAD = 8, 8
KEYS = 45
KHD = RETR // 2
PAIRED = KEYS * KEYS
COLS = PAIRED + PAIRED % 2
EBLK = -(-COLS // P)
CUT = [(0, 1024), (1024, COLS)]
NEVER = -1.0e30
REPLACED = -3.0e38


def pair_rows():
    import numpy as np
    col = np.arange(COLS)
    e = np.minimum(col, PAIRED - 1)
    t = np.zeros((2 * KEYS, COLS), np.float32)
    t[e // KEYS, col] = 1.0
    t[KEYS + e % KEYS, col] = 1.0
    return t


def need(eng, sem, value):
    if not (isinstance(value, int) and value <= 0):
        eng.wait_ge(sem, value)


def need_apart(eng, sem, value, passed):
    if isinstance(value, int):
        need(eng, sem, value)
    else:
        wait_apart(eng, sem, value, passed)


def private_phase(nc, M, D, h, wk):
    UPT = CROSS // P
    with scope(nc, "pv") as s:
        wu = s.sb("wu", [P, KD, CROSS])
        wd = s.sb("wd", [P, UPT, PRIV])
        bu = s.sb("bu", [P, UPT])
        bd = s.sb("bd", [P, 1])
        wq = s.sb("wq", [KHD, 2 * RHEADS, PRIV])
        keys = s.sb("keys", [KHD, 2 * RHEADS, KEYS])
        up = [s.sb(f"up{n}", [P, BLK]) for n in range(2)]
        ps_up = [s.ps(f"up{n}") for n in range(2)]
        ps_h = s.ps("h")
        ps_k = [s.ps(f"k{n}") for n in range(2)]
        loaded, up_product, up_ready, up_used = s.sem("loaded"), s.sem("up_product"), s.sem("up_ready"), s.sem("up_used")
        h_product, h_ready, k_product = s.sem("h_product"), s.sem("h_ready"), s.sem("k_product")

        def done(i, m):
            return i * UPT + (UPT + m + 1)

        with nc.Block() as block:
            @block.sync
            def _(sp):
                for to, of in ((wu[:, :, :], D["w_up"].rearrange("(k p) c -> p k c", p=P)), (bu[:, :], D["b_up"]),
                               (wd[:, :, :], D["w_down"].rearrange("(m p) r -> p m r", p=P)), (bd[:, :], D["b_down"]),
                               (wq[:, :, :], D["w_q"]), (keys[:, :, :], D["keys"])):
                    sp.dma_start(to, of).then_inc(loaded, 16)

            @block.tensor
            def _(pe):
                pe.sem_inc(up_used, UPT)
                pe.wait_ge(loaded, 6 * 16)
                for n in range(2 * RHEADS):
                    last = nc.tensor.matmul(ps_k[n // RHEADS][:, n % RHEADS * KEYS:(n % RHEADS + 1) * KEYS],
                                            wq[:, n, :], keys[:, n, :], start=True, stop=True)
                last.then_inc(k_product, 1)
                with pe.Fori(0, NBLK) as i:
                    for m in range(UPT + 1):
                        if m < UPT:
                            pe.wait_ge(up_ready, done(i, m - 2))
                            for c in range(KD):
                                last = nc.tensor.matmul(ps_up[m % 2][:, :], wu[:, c, m * P:(m + 1) * P],
                                                        M.xT[:, c, ds(i * BLK, BLK)],
                                                        start=(c == 0), stop=(c == KD - 1))
                            last.then_inc(up_product, 1)
                        if m == 1:
                            pe.wait_ge(h_ready, i + 1)
                        if m >= 1:
                            pe.wait_ge(up_ready, done(i, m - 1))
                            last = nc.tensor.matmul(ps_h[:, :], wd[:, m - 1, :], up[(m - 1) % 2][:, :],
                                                    start=(m == 1), stop=(m == UPT))
                            last.then_inc(up_used, 1)

            @block.scalar
            def _(act):
                act.sem_inc(up_ready, UPT)
                act.sem_inc(h_ready, 1)
                act.wait_ge(loaded, 6 * 16)
                act.wait_ge(k_product, 1)
                for n in range(2):
                    nc.scalar.activation(wk[:, n * RHEADS * KEYS:(n + 1) * RHEADS * KEYS],
                                         ps_k[n][:, 0:RHEADS * KEYS], ACT.Copy)
                with act.Fori(0, NBLK) as i:
                    for m in range(UPT):
                        act.wait_ge(up_product, done(i, m) - UPT)
                        act.wait_ge(up_used, done(i, m - 2))
                        nc.scalar.activation(up[m % 2][:, :], ps_up[m % 2][:, :], ACT.Silu,
                                             bias=bu[:, m:m + 1]).then_inc(up_ready, 1)
                    wait_apart(act, up_used, done(i, UPT - 1), M.passed)
                    nc.scalar.activation(h[:, ds(i * BLK, BLK)], ps_h[:, :], ACT.Identity,
                                         bias=bd[:, 0:1]).then_inc(h_ready, 1)


def retrieval_phase(nc, M, D):
    with scope(nc, "re") as s:
        h = s.sb("h", [P, TOKENS])
        wk = s.sb("wk", [P, RHEADS * 2 * KEYS])
        private_phase(nc, M, D, h, wk)
        down = s.sb("down", [P, COLS])
        up = s.sb("up", [P, EBLK, DM])
        pairs = s.sb("pairs", [2 * KEYS, COLS], FP32R)
        hs = [s.sb(f"hs{n}", [P, P]) for n in range(2)]
        z = s.sb("z", [P, COLS])
        sim = s.sb("sim", [P, 2 * RHEADS, KEYS])
        top = s.sb("top", [P, 2 * RHEADS, K_HEAD])
        left = s.sb("left", [P, 2 * RHEADS, KEYS])
        kept = s.sb("kept", [P, 2 * RHEADS, KEYS])
        cand = s.sb("cand", [P, RHEADS, K_HEAD, K_HEAD])
        best = s.sb("best", [P, RHEADS, 8])
        cand2 = s.sb("cand2", [P, RHEADS, K_HEAD * K_HEAD])
        ninth = s.sb("ninth", [P, RHEADS, 8])
        soft = s.sb("soft", [P, RHEADS, 8])
        thr = [s.sb(f"thr{n}", [P, RHEADS]) for n in range(2)]
        shift = [s.sb(f"shift{n}", [P, RHEADS]) for n in range(2)]
        total = [s.sb(f"total{n}", [P, RHEADS]) for n in range(2)]
        keptH = s.sb("keptH", [2 * KEYS, RHEADS, P], FP32R)
        keptL = s.sb("keptL", [2 * KEYS, RHEADS, P], FP32R)
        NE = 4
        ex = [s.sb(f"ex{n}", [P, 1024]) for n in range(NE)]
        u = s.sb("u", [P, RHEADS, COLS])
        Z = [M.xT[:, n, 0:COLS] for n in range(2)]
        ZT = s.sb("ZT", [P, EBLK, P])
        NR = 3
        ring = [s.ps(f"ring{n}", (P, 1024)) for n in range(NR)]
        misc = [s.ps(f"misc{n}") for n in range(2)]

        names = ("loaded hs_ready filled z_ready sim_product sim_ready kept_ready kept_turned keptT_ready "
                 "prep ex_ready masked weighted silu_ready summed z_turned zT_ready out_product out_added "
                 "soft_in soft_ready total_ready prep_step cand_ready high_ready pairs_ready").split()
        S = {n: s.sem(n) for n in names}
        UPT_ = 18
        NU = 2 * RHEADS

        def ring_wait(pe, T, r):
            q = r - NR
            if q < 0:
                q += UPT_
                T = T - 1
            if q < 2:
                need(pe, S["z_ready"], T * 2 + (q + 1))
            else:
                need(pe, S["masked"], T * NU + (q - 1))

        def pe_turn(pe, T, n, live, ahead, behind):
            if ahead:
                need(pe, S["hs_ready"], T + 2)
                need(pe, S["keptT_ready"], T * 2 + 2)
                for m in range(2):
                    nc.tensor.matmul(misc[m][:, 0:RHEADS * KEYS], hs[1 - n][:, :],
                                     wk[:, m * RHEADS * KEYS:(m + 1) * RHEADS * KEYS],
                                     start=True, stop=True).then_inc(S["sim_product"], 1)
            if live:
                for m, (a, b) in enumerate(CUT):
                    ring_wait(pe, T, m)
                    for c in range(a, b, 512):
                        e = min(c + 512, b)
                        last = nc.tensor.matmul(ring[m][:, c - a:e - a], hs[n][:, :], down[:, c:e],
                                                start=True, stop=True)
                    last.then_inc(S["filled"], 1)
            for k in range(RHEADS):
                if live:
                    if k == 0:
                        need(pe, S["keptT_ready"], T * 2 + 2)
                    for m, (a, b) in enumerate(CUT):
                        r = 2 + 2 * k + m
                        ring_wait(pe, T, r)
                        for c in range(a, b, 512):
                            e = min(c + 512, b)
                            nc.tensor.matmul(ring[r % NR][:, c - a:e - a], keptH[:, k, :], pairs[:, c:e],
                                             start=True, stop=False)
                            last = nc.tensor.matmul(ring[r % NR][:, c - a:e - a], keptL[:, k, :], pairs[:, c:e],
                                                    start=False, stop=True)
                        last.then_inc(S["filled"], 1)
                if behind and k < 2:
                    if k == 0:
                        need(pe, S["summed"], (T - 1) * (RHEADS - 1))
                    for m in range(2):
                        g = 2 * k + m
                        if g < 2 and ahead:
                            need(pe, S["sim_ready"], T * 2 + 4)
                        elif g < 2:
                            need(pe, S["keptT_ready"], 2 * TILES)
                            need(pe, S["out_added"], T - 2)
                        else:
                            need(pe, S["zT_ready"], (T - 2) * 4 + (g - 1))
                        for q in range(4):
                            blk = 4 * g + q
                            w = min(P, COLS - blk * P)
                            last = nc.tensor.transpose(misc[m][0:w, q * P:(q + 1) * P],
                                                       Z[n][:, blk * P:blk * P + w], M.ident[:, :])
                        last.then_inc(S["z_turned"], 1)
                if behind and k == 2:
                    need(pe, S["zT_ready"], (T - 2) * 4 + 4)
                    for blk in range(EBLK):
                        w = min(P, COLS - blk * P)
                        last = nc.tensor.matmul(misc[0][:, 0:DM], ZT[0:w, blk, :], up[0:w, blk, :],
                                                start=(blk == 0), stop=(blk == EBLK - 1))
                    last.then_inc(S["out_product"], 1)
            if ahead:
                need(pe, S["kept_ready"], T + 2)
                if behind:
                    need(pe, S["out_added"], T - 1)
                if not behind:
                    need(pe, S["sim_ready"], T * 2 + 4)
                for k in range(RHEADS):
                    last = nc.tensor.transpose(misc[k // 4][0:2 * KEYS, k % 4 * P:(k % 4 + 1) * P],
                                               kept[:, 2 * k:2 * k + 2, :].rearrange("p a k -> p (a k)"),
                                               M.ident[:, :])
                    if k % 4 == 3:
                        last.then_inc(S["kept_turned"], 1)

        def act_turn(act, T, n, live, last_silus, ahead, behind):
            def hs_copy(T, n):
                need_apart(act, S["z_ready"], (T - 1) * 2, M.passed)
                nc.scalar.activation(hs[n][:, :], h[:, ds(T * P, P)], ACT.Copy).then_inc(S["hs_ready"], 1)

            def exps(k):
                for m, (a, b) in enumerate(CUT):
                    i = 2 * k + m
                    need(act, S["filled"], T * UPT_ + (3 + i))
                    need(act, S["masked"], T * NU + (i + 1 - NE))
                    nc.scalar.activation(ex[i % NE][:, 0:b - a], ring[(2 + i) % NR][:, 0:b - a], ACT.Exp,
                                         bias=shift[n][:, k:k + 1]).then_inc(S["ex_ready"], 1)

            def silus(T, n, heads):
                for k in heads:
                    need(act, S["weighted"], T * NU + (2 * k + 2))
                    nc.scalar.activation(u[:, k, :], u[:, k, :], ACT.Silu, scale=total[n][:, k:k + 1]
                                         ).then_inc(S["silu_ready"], 1)

            if ahead:
                hs_copy(T + 1, 1 - n)
            if live:
                for m, (a, b) in enumerate(CUT):
                    need(act, S["filled"], T * UPT_ + (m + 1))
                    need(act, S["weighted"], T * NU)
                    nc.scalar.activation(z[:, a:b], ring[m][:, 0:b - a], ACT.Copy).then_inc(S["z_ready"], 1)
                need(act, S["prep"], T + 1)
            for k in range(RHEADS):
                if live:
                    exps(k)
                if ahead and k == 0:
                    for m in range(2):
                        need(act, S["sim_product"], T * 2 + (3 + m))
                        need(act, S["kept_ready"], T + 1)
                        nc.scalar.activation(sim[:, m * RHEADS:(m + 1) * RHEADS, :].rearrange("p a k -> p (a k)"),
                                             misc[m][:, 0:RHEADS * KEYS], ACT.Copy).then_inc(S["sim_ready"], 1)
                if behind and k < 2:
                    for m in range(2):
                        g = 2 * k + m
                        need(act, S["z_turned"], (T - 2) * 4 + (g + 1))
                        need(act, S["out_product"], T - 2)
                        full = min(4, (COLS - 4 * g * P) // P)
                        last = nc.scalar.activation(ZT[:, 4 * g:4 * g + full, :].rearrange("p a t -> p (a t)"),
                                             misc[m][:, 0:full * P], ACT.Copy)
                        if full < 4:
                            w = COLS % P
                            last = nc.scalar.activation(ZT[0:w, 4 * g + full, :],
                                                        misc[m][0:w, full * P:(full + 1) * P], ACT.Copy)
                        last.then_inc(S["zT_ready"], 1)
                if last_silus and k == 3:
                    need(act, S["total_ready"], T)
                    silus(T - 1, 1 - n, range(4, RHEADS))
            if live:
                need(act, S["total_ready"], T + 1)
                silus(T, n, range(0, 4))
            if ahead:
                need(act, S["soft_in"], T + 2)
                nc.scalar.activation(soft[:, :, :], soft[:, :, :], ACT.Exp).then_inc(S["soft_ready"], 1)
                for m in range(2):
                    need(act, S["kept_turned"], T * 2 + (3 + m))
                    nc.scalar.activation(keptH[:, 4 * m:4 * m + 4, :].rearrange("k h t -> k (h t)"),
                                         misc[m][0:2 * KEYS, :], ACT.Copy).then_inc(S["high_ready"], 1)

        CH = 9

        def dve_turn(dve, T, n, live, ahead, behind):
            def chain(c):
                return (T + 1) * CH + c

            def mask(i):
                k, m = i // 2, i % 2
                a, b = CUT[m]
                need(dve, S["ex_ready"], T * NU + (i + 1))
                if m == 0:
                    need(dve, S["summed"], (T - 1) * (RHEADS - 1) + max(k, 1))
                nc.vector.scalar_tensor_tensor(u[:, k, a:b], ring[(2 + i) % NR][:, 0:b - a], thr[n][:, k:k + 1],
                                               ex[i % NE][:, 0:b - a], ALU.is_ge, ALU.mult).then_inc(S["masked"], 1)

            def weigh(i):
                k, m = i // 2, i % 2
                a, b = CUT[m]
                need(dve, S["masked"], T * NU + (i + 1))
                nc.vector.tensor_tensor(u[:, k, a:b], u[:, k, a:b], z[:, a:b], ALU.mult).then_inc(S["weighted"], 1)

            if live:
                need(dve, S["z_ready"], T * 2 + 2)
            for k in range(RHEADS):
                if live:
                    for i in (2 * k, 2 * k + 1):
                        mask(i)
                        if i:
                            weigh(i - 1)
                if behind and k == 2:
                    need(dve, S["out_product"], T - 1)
                    x = M.x[:, ds(T - 2, 1), :]
                    nc.vector.tensor_tensor(x, misc[0][:, 0:DM].unsqueeze(1), x, ALU.add).then_inc(S["out_added"], 1)
                if ahead and k == 3:
                    need_apart(dve, S["sim_ready"], T * 2 + 4, M.passed)
                    for q in range(2 * RHEADS):
                        last = nc.vector.max(top[:, q, :], sim[:, q, :])
                    last.then_inc(S["prep_step"], 1)
                    need_apart(dve, S["prep_step"], chain(1), M.passed)
                    for q in range(2 * RHEADS):
                        last = nc.vector.match_replace(out=left[:, q, :], in_to_replace=top[:, q, :],
                                                       in_values=sim[:, q, :], imm_value=REPLACED)
                    last.then_inc(S["prep_step"], 1)
                    nc.vector.tensor_tensor(
                        cand[:, :, :, :],
                        top[:, :, :].rearrange("p (h a) k -> p h a k", a=2)[:, :, 0, :].unsqueeze(3)
                        .broadcast_to([P, RHEADS, K_HEAD, K_HEAD]),
                        top[:, :, :].rearrange("p (h a) k -> p h a k", a=2)[:, :, 1, :].unsqueeze(2)
                        .broadcast_to([P, RHEADS, K_HEAD, K_HEAD]), ALU.add).then_inc(S["cand_ready"], 1)
                    need(dve, S["prep_step"], chain(2))
                    nc.vector.tensor_tensor(left[:, :, :], left[:, :, :], sim[:, :, :], ALU.is_equal
                                            ).then_inc(S["prep_step"], 1)
                    need_apart(dve, S["cand_ready"], T + 2, M.passed)
                    for q in range(RHEADS):
                        last = nc.vector.max(best[:, q, :], cand[:, q, :, :].rearrange("p a b -> p (a b)"))
                    last.then_inc(S["prep_step"], 1)
                    need(dve, S["prep_step"], chain(3))
                    need(dve, S["kept_turned"], T * 2 + 2)
                    nc.vector.scalar_tensor_tensor(kept[:, :, :], left[:, :, :], NEVER, sim[:, :, :],
                                                   ALU.mult, ALU.add).then_inc(S["kept_ready"], 1)
                    need_apart(dve, S["prep_step"], chain(4), M.passed)
                    for q in range(RHEADS):
                        last = nc.vector.match_replace(out=cand2[:, q, :], in_to_replace=best[:, q, :],
                                                       in_values=cand[:, q, :, :].rearrange("p a b -> p (a b)"),
                                                       imm_value=REPLACED)
                    last.then_inc(S["prep_step"], 1)
                    nc.vector.tensor_scalar(shift[1 - n][:, :], best[:, :, 0], -1.0, None, ALU.mult
                                            ).then_inc(S["prep_step"], 1)
                    need_apart(dve, S["prep_step"], chain(5), M.passed)
                    for q in range(RHEADS):
                        last = nc.vector.max(ninth[:, q, :], cand2[:, q, :])
                    last.then_inc(S["prep_step"], 1)
                    need(dve, S["prep_step"], chain(6))
                    nc.vector.tensor_tensor(soft[:, :, :], best[:, :, :],
                                            shift[1 - n][:, :].unsqueeze(2).broadcast_to([P, RHEADS, 8]),
                                            ALU.add).then_inc(S["soft_in"], 1)
                    need(dve, S["prep_step"], chain(7))
                    nc.vector.tensor_tensor(thr[1 - n][:, :], best[:, :, K_HEAD - 1], ninth[:, :, 0], ALU.add
                                            ).then_inc(S["prep_step"], 1)
                    need(dve, S["prep_step"], chain(8))
                    nc.vector.tensor_scalar(thr[1 - n][:, :], thr[1 - n][:, :], 0.5, None, ALU.mult
                                            ).then_inc(S["prep"], 1)
            if live:
                weigh(NU - 1)
            if ahead:
                need(dve, S["soft_ready"], T + 2)
                need(dve, S["silu_ready"], T * RHEADS)
                nc.vector.tensor_reduce(total[1 - n][:, :], soft[:, :, :], AX.X, ALU.add).then_inc(S["prep_step"], 1)
                need(dve, S["prep_step"], chain(9))
                nc.vector.reciprocal(total[1 - n][:, :], total[1 - n][:, :]).then_inc(S["total_ready"], 1)
                for m in range(2):
                    need(dve, S["high_ready"], T * 2 + (3 + m))
                    four = slice(4 * m, 4 * m + 4)
                    nc.vector.tensor_tensor(keptL[:, four, :], misc[m][0:2 * KEYS, :].rearrange("k (h t) -> k h t", h=4),
                                            keptH[:, four, :].bitcast(FP32), ALU.subtract).then_inc(S["keptT_ready"], 1)

        def pool_turn(pool, T, n, live, last_silus):
            def add(T, n, k):
                j = T * (RHEADS - 1) + k
                need(pool, S["silu_ready"], T * RHEADS + (k + 1))
                if k == 1:
                    need(pool, S["z_turned"], (T - 1) * 4)
                else:
                    need(pool, S["summed"], j - 1)
                nc.gpsimd.tensor_tensor(Z[n], u[:, 0, :] if k == 1 else Z[n], u[:, k, :], ALU.add
                                        ).then_inc(S["summed"], 1)

            if last_silus:
                for k in range(4, RHEADS):
                    add(T - 1, 1 - n, k)
            if live:
                for k in range(1, 4):
                    add(T, n, k)

        def turns(eng, turn):
            for T in (-1, 0, 1):
                turn(T, T % 2, T >= 0, T >= 1, True, False)
            with eng.Fori(0, (TILES - 4) // 2) as i:
                for n in range(2):
                    turn(i * 2 + (2 + n), n, True, True, True, True)
            for T in range(TILES - 2, TILES + 2):
                turn(T, T % 2, T < TILES, T <= TILES, T < TILES - 1, True)

        with nc.Block() as block:
            @block.sync
            def _(sp):
                sp.dma_start(down[:, :], D["down"]).then_inc(S["loaded"], 16)
                sp.dma_start(u[0:2 * KEYS, 0, :], D["pairs"]).then_inc(S["loaded"], 16)
                sp.dma_start(up[:, 0:EBLK - 1, :],
                             D["up"][0:(EBLK - 1) * P, :].rearrange("(a p) d -> p a d", p=P)).then_inc(S["loaded"], 16)
                sp.dma_start(up[0:COLS % P, EBLK - 1, :], D["up"][(EBLK - 1) * P:COLS, :]).then_inc(S["loaded"], 16)

            @block.tensor
            def _(pe):
                pe.wait_ge(S["loaded"], 64)
                pe.wait_ge(S["pairs_ready"], 1)
                turns(pe, lambda T, n, live, last, ahead, behind: pe_turn(pe, T, n, live, ahead, behind))

            @block.scalar
            def _(act):
                turns(act, lambda T, n, live, last, ahead, behind: act_turn(act, T, n, live, last, ahead, behind))

            @block.vector
            def _(dve):
                dve.wait_ge(S["loaded"], 64)
                nc.vector.tensor_copy(pairs[:, :], u[0:2 * KEYS, 0, :]).then_inc(S["pairs_ready"], 1)
                turns(dve, lambda T, n, live, last, ahead, behind: dve_turn(dve, T, n, live, ahead, behind))

            @block.gpsimd
            def _(pool):
                turns(pool, lambda T, n, live, last, ahead, behind: pool_turn(pool, T, n, live, last))


def store_phase(nc, M, D):
    with scope(nc, "st") as s:
        stored = s.sem("stored")
        with nc.Block() as block:
            @block.sync
            def _(sp):
                sp.dma_start(D["out"].rearrange("b s d -> (b s) d").rearrange("(n p) d -> p n d", p=P), M.x[:, :, :]).then_inc(stored, 16)
                sp.wait_ge(stored, 16)


class Memory:
    pass


def build(nc, D):
    M = Memory()
    M.norms = 0
    with scope(nc, "all") as s:
        M.xT = s.sb("xT", [P, KD, TOKENS])
        M.x = s.sb("x", [P, TILES, DM])
        M.ident = s.sb("ident", [P, P])
        M.passed = s.sem("passed")
        M.ident16 = s.sb("ident16", [P, P], BF16)
        M.ones = s.sb("ones", [P, P])
        load_phase(nc, M, D)
        with scope(nc, "g") as g:
            G = g.sb("gated", [P, PAIRS, TOKENS])
            squares_sum = g.sb("squares_sum", [P, TOKENS])
            gate_phase(nc, M, D, G)
            attention_phase(nc, M, D, G, squares_sum)
            projection_phase(nc, M, D, G, squares_sum)
        layernorm_phase(nc, M)
        experts_phase(nc, M, D)
        layernorm_phase(nc, M)
        scan_phase(nc, M, D)
        layernorm_phase(nc, M)
        retrieval_phase(nc, M, D)
        layernorm_phase(nc, M, turn_back=False)
        store_phase(nc, M, D)


def kernel(**inputs):
    import numpy as np
    import concourse.bacc as bacc
    from concourse.bass_utils import run_bass_kernel_spmd as run

    I = {k: np.asarray(v) for k, v in inputs.items()}
    x = I["L0_attn_hidden_states"].reshape(TOKENS, DM)
    qkv = I["L0_attn_qkv_w"].reshape(PAIRS, 2, 3, HD, DM)
    qkv = qkv.transpose(0, 4, 2, 1, 3).reshape(PAIRS, KD, P, 3 * P).transpose(0, 2, 1, 3)
    gate = I["L0_attn_gate_w"].reshape(PAIRS, P, KD, P).transpose(0, 3, 2, 1)
    A = dict(
        x=x, xT=x.T,
        qkv_w=qkv.reshape(PAIRS, P, KD * 3 * P),
        gate_w=gate.reshape(PAIRS, P, KD * P),
        norm_w=I["L0_attn_norm_w"].reshape(PAIRS, P, 1),
        decay=decay_table(),
        out_w=I["L0_attn_out_w"].T,
    )
    wq = I["L1_ffn_W_q"].reshape(2, RHEADS, KHD, PRIV)
    pad_experts = lambda a: np.pad(a[:PAIRED], ((0, COLS - PAIRED), (0, 0)))
    keys = I["L1_ffn_keys"]
    A.update(
        w_up=I["L1_ffn_W_up"].T, b_up=I["L1_ffn_b_up"].reshape(-1, P).T,
        w_down=I["L1_ffn_W_down"].T, b_down=I["L1_ffn_b_down"][:, None],
        w_q=wq.transpose(2, 1, 0, 3).reshape(KHD, 2 * RHEADS, PRIV),
        keys=keys.transpose(3, 0, 2, 1).reshape(KHD, 2 * RHEADS, KEYS),
        down=pad_experts(I["L1_ffn_down_embed"]).T, up=pad_experts(I["L1_ffn_up_embed"]),
        pairs=pair_rows(),
    )
    pad = FTILES * P - EXPERTS * FF

    def hidden_rows(routed, shared, axis):
        a = np.concatenate([routed, shared], 0)
        a = a.transpose(1, 0, 2).reshape(DM, EXPERTS * FF) if axis == 1 else a.reshape(EXPERTS * FF, -1)
        return np.pad(a, ((0, 0), (0, pad)) if axis == 1 else ((0, pad), (0, 0)))

    A.update(
        centroids=I["L0_ffn_centroids"].T, route_bias=I["L0_ffn_bias"],
        w1=hidden_rows(I["L0_ffn_routed_w1"], I["L0_ffn_shared_w1"], 1),
        w2=hidden_rows(I["L0_ffn_routed_w2"], I["L0_ffn_shared_w2"], 0),
        b1=hidden_rows(I["L0_ffn_routed_b1"], I["L0_ffn_shared_b1"], 0).reshape(FTILES, P).T,
        b2=np.concatenate([I["L0_ffn_routed_b2"], I["L0_ffn_shared_b2"]], 0),
        expert_rows=expert_rows(),
    )
    wx, bx = I["L1_attn_W_xproj"].T, I["L1_attn_b_xproj"][:, None]
    A.update(
        wx=np.concatenate([wx[:, :DT_RANK]] + [wx[:, DT_RANK:]] * PARTS, 1),
        bx=np.concatenate([bx[:DT_RANK]] + [bx[DT_RANK:]] * PARTS, 0),
        wdt=I["L1_attn_W_dt"].T, bdt=I["L1_attn_b_dt"].reshape(KD, P).T,
        a_log=I["L1_attn_A_log"].reshape(KD, P, STATES).transpose(1, 0, 2),
        state_rows=state_rows(),
    )
    nc = bacc.Bacc("TRN2", target_bir_lowering=False, num_devices=1)
    D, arrays = {}, {}
    for name, a in A.items():
        a = np.ascontiguousarray(a)
        arrays[f"in_{name}_dram"] = a
        D[name] = nc.dram_tensor(f"in_{name}_dram", a.shape, mybir.dt.from_np(a.dtype),
                                 kind="ExternalInput").ap()
    D["out"] = nc.dram_tensor("out_0_dram", (BATCH, SEQ, DM), FP32, kind="ExternalOutput").ap()
    build(nc, D)
    r = run(nc, [arrays], core_ids=[0])
    return r.results[0]["out_0_dram"]
```

```python
import concourse.bass as bass
from concourse import mybir
from contextlib import ExitStack, contextmanager

FP32 = mybir.dt.float32
FP32R = mybir.dt.float32r
BF16 = mybir.dt.bfloat16
ALU = mybir.AluOpType
ACT = mybir.ActivationFunctionType
AX = mybir.AxisListType
ds = bass.ds

P = 128
BATCH, SEQ, DM = 4, 512, 256
TOKENS = BATCH * SEQ
TILES = TOKENS // P
BLK = 512
NBLK = TOKENS // BLK
KD = DM // P
LN_EPS = 1e-5
ONE_BITS = 0x3F80


def wait_apart(eng, sem, value, passed):
    eng.wait_ge(sem, value)
    eng.sem_inc(passed, 1)


def need(eng, sem, value):
    if not (isinstance(value, int) and value <= 0):
        eng.wait_ge(sem, value)


def need_apart(eng, sem, value, passed):
    if isinstance(value, int):
        need(eng, sem, value)
    else:
        wait_apart(eng, sem, value, passed)


class Scope:

    def __init__(self, nc, prefix, ctx):
        self.nc, self.prefix, self.ctx = nc, prefix, ctx

    def sb(self, name, shape, dt=FP32):
        return self.ctx.enter_context(self.nc.sbuf_tensor(f"{self.prefix}_sb_{name}", shape, dt))

    def sb_both(self, name, shape):
        start = self.nc.sbuf_base
        whole = self.sb(name, shape)
        end = self.nc.sbuf_base
        self.ctx.callback(self.set_base, end)
        self.set_base(start)
        part = self.sb(f"{name}_part", shape, FP32R)
        assert self.nc.sbuf_base == end
        return whole, part

    def set_base(self, base):
        self.nc.sbuf_base = base

    def ps(self, name, shape=(P, 512), dt=FP32):
        return self.ctx.enter_context(self.nc.psum_tensor(f"{self.prefix}_ps_{name}", list(shape), dt))

    def sem(self, name):
        return self.ctx.enter_context(self.nc.semaphore(f"{self.prefix}_{name}"))


@contextmanager
def scope(nc, prefix):
    with ExitStack() as ctx:
        yield Scope(nc, prefix, ctx)


def load_phase(nc, M, D):
    with scope(nc, "ld") as s:
        loaded = s.sem("loaded")
        zeroed = s.sem("zeroed")
        with nc.Block() as block:
            @block.sync
            def _(sp):
                sp.dma_start(M.xT[:, :, :], D["xT"].rearrange("(k p) t -> p k t", p=P)).then_inc(loaded, 16)
                sp.wait_ge(loaded, 16)

            @block.gpsimd
            def _(pool):
                nc.gpsimd.memset(M.ident[:, :], 0.0).then_inc(zeroed, 1)
                nc.gpsimd.memset(M.ones[:, :], 1.0)
                nc.gpsimd.memset(M.ident16[:, :], 0.0).then_inc(zeroed, 1)
                pool.wait_ge(zeroed, 2)
                nc.gpsimd.affine_select(out=M.ident16[:, :], in_=M.ident16[:, :], compare_op=ALU.not_equal,
                                        fill=1.0, base=0, pattern=[[-1, P]], channel_multiplier=1)
                nc.gpsimd.affine_select(out=M.ident[:, :], in_=M.ident[:, :], compare_op=ALU.not_equal,
                                        fill=1.0, base=0, pattern=[[-1, P]],
                                        channel_multiplier=1).then_inc(zeroed, 1)


HEADS, HD = 32, 64
FEAT = HEADS * HD
PAIRS = HEADS // 2
CHUNKS = SEQ // P
HALVES = 2
UNITS = HALVES * BATCH
TURNS = PAIRS // HALVES


def gate_phase(nc, M, D, G):
    with scope(nc, "gt") as s:
        w = [s.sb(f"w{j}", [P, KD, P]) for j in range(HALVES)]
        wH = [s.sb(f"wH{j}", [P, KD, P], FP32R) for j in range(HALVES)]
        wL = [s.sb(f"wL{j}", [P, KD, P], FP32R) for j in range(HALVES)]
        bank = [s.ps(f"bank{n}") for n in range(4)]
        w_loaded = [s.sem(f"w_loaded{j}") for j in range(HALVES)]
        x_high, x_low = s.sem("x_high"), s.sem("x_low")
        w_high, w_low = s.sem("w_high"), s.sem("w_low")
        product = s.sem("product")
        gate = s.sem("gate")

        def done(i, k):
            return i * UNITS + (UNITS + k + 1)

        with nc.Block() as block:
            @block.sync
            def _(sp):
                sp.sem_inc(w_low, HALVES)
                with sp.Fori(0, TURNS) as i:
                    for j in range(HALVES):
                        sp.wait_ge(w_low, i * HALVES + j + 1)
                        sp.dma_start(w[j][:, :, :],
                                     D["gate_w"][ds(i * HALVES + j, 1), :, :].rearrange("o p (k f) -> p (o k) f", k=KD)
                                     ).then_inc(w_loaded[j], 16)

            @block.gpsimd
            def _(pool):
                with pool.Fori(0, TURNS) as i:
                    for j in range(HALVES):
                        pool.wait_ge(w_loaded[j], i * 16 + 16)
                        wait_apart(pool, product, done(i, BATCH * (j + 1) - 1 - UNITS), M.passed)
                        nc.gpsimd.tensor_copy(wH[j][:, :, :], w[j][:, :, :]).then_inc(w_high, 1)
                        wait_apart(pool, w_high, i * HALVES + j + 1, M.passed)
                        nc.gpsimd.tensor_tensor(wL[j][:, :, :], w[j][:, :, :], wH[j][:, :, :].bitcast(FP32),
                                                ALU.subtract).then_inc(w_low, 1)

            @block.vector
            def _(dve):
                for b in range(BATCH):
                    t = slice(b * BLK, (b + 1) * BLK)
                    dve.wait_ge(x_high, b + 1)
                    nc.vector.tensor_tensor(M.xL[:, :, t], M.xT[:, :, t], M.xH[:, :, t].bitcast(FP32),
                                            ALU.subtract).then_inc(x_low, 1)

            @block.tensor
            def _(pe):
                pe.sem_inc(product, UNITS)
                with pe.Fori(0, TURNS) as i:
                    for j in range(HALVES):
                        pe.wait_ge(w_low, i * HALVES + (HALVES + j + 1))
                        for b in range(BATCH):
                            k = j * BATCH + b
                            t = slice(b * BLK, (b + 1) * BLK)
                            pe.wait_ge(x_low, b + 1)
                            pe.wait_ge(gate, done(i, k - 4))
                            for c in range(KD):
                                nc.tensor.matmul(bank[k % 4][:, :], wH[j][:, c, :], M.xH[:, c, t],
                                                 start=(c == 0), stop=False)
                                nc.tensor.matmul(bank[k % 4][:, :], wH[j][:, c, :], M.xL[:, c, t],
                                                 start=False, stop=False)
                                last = nc.tensor.matmul(bank[k % 4][:, :], wL[j][:, c, :], M.xH[:, c, t],
                                                        start=False, stop=(c == KD - 1))
                            last.then_inc(product, 1)

            @block.scalar
            def _(act):
                for b in range(BATCH):
                    t = slice(b * BLK, (b + 1) * BLK)
                    nc.scalar.activation(M.xH[:, :, t], M.xT[:, :, t], ACT.Copy).then_inc(x_high, 1)
                act.sem_inc(gate, UNITS)
                with act.Fori(0, TURNS) as i:
                    for j in range(HALVES):
                        for b in range(BATCH):
                            k = j * BATCH + b
                            act.wait_ge(product, done(i, k))
                            nc.scalar.activation(G[:, ds(i * HALVES + j, 1), b * BLK:(b + 1) * BLK],
                                                 bank[k % 4][:, :].unsqueeze(1), ACT.Sigmoid).then_inc(gate, 1)


TBL = 2 * P + P + 2 + 1


def decay_table():
    import numpy as np
    base = 1.0 / 2.0 ** (8.0 / HEADS)
    slope = base ** (np.arange(HEADS) + 1.0) * (1.0 + 1e-5)
    r = np.arange(P, dtype=np.float64)
    t = np.zeros((PAIRS, P, TBL))
    for a in range(PAIRS):
        for h in range(2):
            m = slope[2 * a + h]
            dist = r[None, :] - r[:, None]
            t[a, :, h * P:(h + 1) * P] = np.where(dist >= 0, np.exp(-m * np.maximum(dist, 0)), 0.0)
            t[a, h * HD:(h + 1) * HD, 2 * P:3 * P] = np.exp(-m * (r + 1))[None, :]
            t[a, :, 3 * P + h] = np.exp(-m * (P - 1 - r))
            t[a, h * HD:(h + 1) * HD, 3 * P + 2] = np.exp(-m * P)
    return t.astype(np.float32)


def attention_phase(nc, M, D, G, squares_sum):
    with scope(nc, "at") as s:
        w, wL = zip(*(s.sb_both(f"w{j}", [P, KD, 3 * P]) for j in range(HALVES)))
        wH = [s.sb(f"wH{j}", [P, KD, 3 * P], FP32R) for j in range(HALVES)]
        tbl = [s.sb(f"tbl{j}", [P, TBL]) for j in range(HALVES)]
        nw = [s.sb(f"nw{j}", [P, 1]) for j in range(HALVES)]
        qT = [s.sb(f"qT{n}", [P, BLK]) for n in range(2)]
        kT = [s.sb(f"kT{n}", [P, BLK]) for n in range(2)]
        v = [s.sb(f"v{n}", [P, CHUNKS, P]) for n in range(2)]
        q_decayed = s.sb("q_decayed", [P, CHUNKS - 1, P])
        k_decayed = s.sb("k_decayed", [P, CHUNKS - 1, P])
        weights = s.sb("weights", [P, 2, BLK])
        state = s.sb("state", [P, CHUNKS - 1, P])
        sq = s.sb("sq", [P, BLK])

        ps_q, ps_k, ps_v, ps_kt = s.ps("q"), s.ps("k"), s.ps("v"), s.ps("kt")
        ps_score = [s.ps(f"score{h}") for h in range(2)]
        ps_out, ps_state = s.ps("out"), s.ps("state_sum")

        w_loaded = [s.sem(f"w_loaded{j}") for j in range(HALVES)]
        w_high, w_low = s.sem("w_high"), s.sem("w_low")
        q_product, k_product, v_product = s.sem("q_product"), s.sem("k_product"), s.sem("v_product")
        q_ready, k_ready, v_ready = s.sem("q_ready"), s.sem("k_ready"), s.sem("v_ready")
        k_turned = s.sem("k_turned")
        k_decay_ready = s.sem("k_decay_ready")
        q_decay_ready = s.sem("q_decay_ready")
        scores = s.sem("scores")
        weights_ready = s.sem("weights_ready")
        state_product = s.sem("state_product")
        state_step = s.sem("state_step")
        attended = s.sem("attended")
        squared = s.sem("squared")
        gated = s.sem("gated")
        summed = s.sem("summed")
        zeroed = s.sem("zeroed")

        def done(i, k, n=1):
            return (i * UNITS + (UNITS + k + 1)) * n

        with nc.Block() as block:
            @block.sync
            def _(sp):
                def load(j, a):
                    for to, name in ((w[j][:, :, :], "qkv_w"), (tbl[j][:, :], "decay"), (nw[j][:, :], "norm_w")):
                        of = D[name][ds(a, 1), :, :]
                        of = of.rearrange("o p (k f) -> p (o k) f", k=KD) if name == "qkv_w" else of.rearrange(
                            "o p f -> (o p) f")
                        sp.dma_start(to, of).then_inc(w_loaded[j], 16)

                load(0, 0)
                with sp.Fori(0, TURNS) as i:
                    sp.wait_ge(gated, done(i, -1))
                    load(1, i * HALVES + 1)
                    sp.wait_ge(gated, done(i, BATCH - 1))
                    load(0, i * HALVES + 2)

            def project(pe, i, k):
                j, b, n = k // BATCH, k % BATCH, k % 2
                if b == 0:
                    pe.wait_ge(w_low, i * HALVES + j + 1)
                for ready, bank, done_sem, col in ((q_ready, ps_q, q_product, 0), (k_ready, ps_k, k_product, P)):
                    pe.wait_ge(ready, done(i, k - 1))
                    t = slice(b * BLK, (b + 1) * BLK)
                    for c in range(KD):
                        nc.tensor.matmul(bank[:, :], wH[j][:, c, col:col + P], M.xH[:, c, t], start=(c == 0), stop=False)
                        nc.tensor.matmul(bank[:, :], wH[j][:, c, col:col + P], M.xL[:, c, t], start=False, stop=False)
                        last = nc.tensor.matmul(bank[:, :], wL[j][:, c, col:col + P], M.xH[:, c, t],
                                                start=False, stop=(c == KD - 1))
                    last.then_inc(done_sem, 1)
                pe.wait_ge(v_ready, done(i, k - 1))
                for t in range(CHUNKS):
                    of, tokens = ps_v[:, t * P:(t + 1) * P], slice(b * BLK + t * P, b * BLK + (t + 1) * P)
                    for c in range(KD):
                        nc.tensor.matmul(of, M.xH[:, c, tokens], wH[j][:, c, 2 * P:3 * P], start=(c == 0), stop=False)
                        nc.tensor.matmul(of, M.xH[:, c, tokens], wL[j][:, c, 2 * P:3 * P], start=False, stop=False)
                        last = nc.tensor.matmul(of, M.xL[:, c, tokens], wH[j][:, c, 2 * P:3 * P],
                                                start=False, stop=(c == KD - 1))
                last.then_inc(v_product, 1)

            @block.tensor
            def _(pe):
                pe.wait_ge(zeroed, 1)
                with pe.Fori(0, TURNS) as i:
                    project(pe, i, 0)
                    for k in range(UNITS):
                        n = k % 2
                        pe.wait_ge(k_ready, done(i, k))
                        pe.wait_ge(k_decay_ready, done(i, k - 1))
                        for t in range(CHUNKS - 1):
                            last = nc.tensor.transpose(ps_kt[:, t * P:(t + 1) * P], kT[n][:, t * P:(t + 1) * P],
                                                       M.ident[:, :])
                        last.then_inc(k_turned, 1)
                        pe.wait_ge(q_ready, done(i, k))
                        pe.wait_ge(weights_ready, done(i, k - 1, 2))
                        for t in range(CHUNKS):
                            for h in range(2):
                                r = slice(h * HD, (h + 1) * HD)
                                last = nc.tensor.matmul(ps_score[h][:, t * P:(t + 1) * P],
                                                        kT[n][r, t * P:(t + 1) * P], qT[n][r, t * P:(t + 1) * P],
                                                        start=True, stop=True)
                        last.then_inc(scores, 1)
                        if k + 1 < UNITS:
                            project(pe, i, k + 1)
                        pe.wait_ge(k_decay_ready, done(i, k))
                        pe.wait_ge(v_ready, done(i, k))
                        pe.wait_ge(state_step, done(i, k - 1, CHUNKS - 1))
                        for t in range(CHUNKS - 1):
                            for h in range(2):
                                r = slice(h * HD, (h + 1) * HD)
                                last = nc.tensor.matmul(ps_state[r, t * P + h * HD:t * P + (h + 1) * HD],
                                                        k_decayed[:, t, r], v[n][:, t, r], start=True, stop=True)
                        last.then_inc(state_product, 1)
                        pe.wait_ge(weights_ready, done(i, k, 2))
                        pe.wait_ge(gated, done(i, k - 1))
                        for t in range(CHUNKS):
                            for h in range(2):
                                r = slice(h * HD, (h + 1) * HD)
                                last = nc.tensor.matmul(ps_out[r, t * P:(t + 1) * P], v[n][:, t, r],
                                                        weights[:, h, t * P:(t + 1) * P], start=True,
                                                        stop=(t == 0), skip_group_check=True)
                            if t == 1:
                                pe.wait_ge(state_step, done(i, k, CHUNKS - 1))
                                pe.wait_ge(q_decay_ready, done(i, k))
                            if t > 0:
                                last = nc.tensor.matmul(ps_out[:, t * P:(t + 1) * P], state[:, t - 1, :],
                                                        q_decayed[:, t - 1, :], start=False, stop=True,
                                                        skip_group_check=True)
                        last.then_inc(attended, 1)

            @block.scalar
            def _(act):
                for sem in (q_ready, k_ready, v_ready, squared):
                    act.sem_inc(sem, UNITS)

                def evacuate(i, k):
                    n = k % 2
                    act.wait_ge(k_product, done(i, k) - UNITS)
                    act.wait_ge(attended, done(i, k - 2))
                    nc.scalar.activation(kT[n][:, :], ps_k[:, :], ACT.Silu).then_inc(k_ready, 1)
                    act.wait_ge(q_product, done(i, k) - UNITS)
                    act.wait_ge(q_decay_ready, done(i, k - 2))
                    nc.scalar.activation(qT[n][:, :], ps_q[:, :], ACT.Silu).then_inc(q_ready, 1)
                    act.wait_ge(v_product, done(i, k) - UNITS)
                    nc.scalar.activation(v[n][:, :, :].rearrange("p a b -> p (a b)"), ps_v[:, :],
                                         ACT.Silu).then_inc(v_ready, 1)

                with act.Fori(0, TURNS) as i:
                    evacuate(i, 0)
                    for k in range(UNITS):
                        if k + 1 < UNITS:
                            evacuate(i, k + 1)
                        act.wait_ge(attended, done(i, k))
                        act.wait_ge(summed, done(i, k - 1))
                        nc.scalar.activation(sq[:, :], ps_out[:, :], ACT.Square).then_inc(squared, 1)

            @block.vector
            def _(dve):
                nc.vector.memset(ps_state[:, :], 0.0).then_inc(zeroed, 1)
                dve.sem_inc(k_decay_ready, UNITS)
                dve.sem_inc(weights_ready, 2 * UNITS)
                dve.sem_inc(state_step, (CHUNKS - 1) * UNITS)
                dve.sem_inc(gated, UNITS)
                with dve.Fori(0, TURNS) as i:
                    for k in range(UNITS):
                        j, b = k // BATCH, k % BATCH
                        t_ = tbl[j]
                        if b == 0:
                            dve.wait_ge(w_loaded[j], i * 48 + 48)
                        dve.wait_ge(k_turned, done(i, k) - UNITS)
                        nc.vector.tensor_tensor(
                            k_decayed[:, :, :].rearrange("p t (h e) -> p t h e", h=2),
                            ps_kt[:, 0:(CHUNKS - 1) * P].rearrange("p (t h e) -> p t h e", t=CHUNKS - 1, h=2),
                            t_[:, 3 * P:3 * P + 2].unsqueeze(1).unsqueeze(3).broadcast_to([P, CHUNKS - 1, 2, HD]),
                            ALU.mult).then_inc(k_decay_ready, 1)
                        dve.wait_ge(scores, done(i, k) - UNITS)
                        dve.wait_ge(attended, done(i, k - 1))
                        for h in range(2):
                            nc.vector.tensor_tensor(
                                weights[:, h, :].rearrange("p (t q) -> p t q", t=CHUNKS),
                                ps_score[h][:, :].rearrange("p (t q) -> p t q", t=CHUNKS),
                                t_[:, h * P:(h + 1) * P].unsqueeze(1).broadcast_to([P, CHUNKS, P]),
                                ALU.mult).then_inc(weights_ready, 1)
                        dve.wait_ge(state_product, done(i, k) - UNITS)
                        nc.vector.tensor_copy(state[:, 0, :], ps_state[:, 0:P]).then_inc(state_step, 1)
                        for t in range(1, CHUNKS - 1):
                            dve.wait_ge(state_step, done(i, k - 1, CHUNKS - 1) + t)
                            nc.vector.scalar_tensor_tensor(state[:, t, :], state[:, t - 1, :],
                                                           t_[:, 3 * P + 2:3 * P + 3],
                                                           ps_state[:, t * P:(t + 1) * P],
                                                           ALU.mult, ALU.add).then_inc(state_step, 1)
                        dve.wait_ge(squared, done(i, k))
                        g = G[:, ds(i * HALVES + j, 1), b * BLK:(b + 1) * BLK]
                        nc.vector.scalar_tensor_tensor(g, ps_out[:, :].unsqueeze(1), nw[j][:, 0:1], g,
                                                       ALU.mult, ALU.mult).then_inc(gated, 1)

            @block.gpsimd
            def _(pool):
                nc.gpsimd.memset(squares_sum[:, :], 0.0).then_inc(summed, 1)
                pool.wait_ge(summed, 1)
                pool.sem_inc(summed, UNITS - 1)
                pool.sem_inc(q_decay_ready, UNITS)
                pool.sem_inc(attended, UNITS)

                def cut(j, loads, pair):
                    need_apart(pool, w_loaded[j], loads * 48, M.passed)
                    nc.gpsimd.tensor_copy(wH[j][:, :, :], w[j][:, :, :]).then_inc(w_high, 1)
                    need_apart(pool, w_high, pair + 1, M.passed)
                    nc.gpsimd.tensor_tensor(wL[j][:, :, :], w[j][:, :, :], wH[j][:, :, :].bitcast(FP32),
                                            ALU.subtract).then_inc(w_low, 1)

                cut(0, 1, 0)
                with pool.Fori(0, TURNS) as i:
                    for k in range(UNITS):
                        if k % BATCH == 2:
                            j = 1 - k // BATCH
                            cut(j, i + 2 - j, i * HALVES + k // BATCH + 1)
                        j, b, n = k // BATCH, k % BATCH, k % 2
                        if b == 0:
                            pool.wait_ge(w_loaded[j], i * 48 + 48)
                        pool.wait_ge(q_ready, done(i, k))
                        pool.wait_ge(attended, done(i, k - 1))
                        nc.gpsimd.tensor_tensor(q_decayed[:, :, :],
                                                qT[n][:, P:BLK].rearrange("p (t q) -> p t q", t=CHUNKS - 1),
                                                tbl[j][:, 2 * P:3 * P].unsqueeze(1).broadcast_to([P, CHUNKS - 1, P]),
                                                ALU.mult).then_inc(q_decay_ready, 1)
                        pool.wait_ge(squared, done(i, k))
                        part = squares_sum[:, b * BLK:(b + 1) * BLK]
                        nc.gpsimd.tensor_tensor(part, part, sq[:, :], ALU.add).then_inc(summed, 1)


class Residual:

    TPB = BLK // P

    def __init__(self, nc, M, s, residual):
        self.nc, self.M, self.residual = nc, M, residual
        self.y = s.sb("branch", [P, KD, BLK])
        self.bank = [s.ps(f"turned{n}") for n in range(KD)]
        self.turned = s.sem("turned")
        self.added = s.sem("added")

    def tensor(self, pe, i, y_sem, y_value):
        nc = self.nc
        pe.wait_ge(y_sem, y_value)
        pe.wait_ge(self.added, i * KD + KD)
        for t in range(self.TPB):
            for c in range(KD):
                last = nc.tensor.transpose(self.bank[t // 2][:, (t % 2) * DM + c * P:(t % 2) * DM + (c + 1) * P],
                                           self.y[:, c, t * P:(t + 1) * P], self.M.ident[:, :])
            if t % 2:
                last.then_inc(self.turned, 1)

    def vector(self, dve, i):
        for h in range(KD):
            x = self.M.x[:, ds(i * self.TPB + 2 * h, 2), :]
            dve.wait_ge(self.turned, i * KD + h + 1)
            self.nc.vector.scalar_tensor_tensor(x, x, float(self.residual),
                                                self.bank[h][:, :].rearrange("p (t d) -> p t d", t=2),
                                                ALU.mult, ALU.add).then_inc(self.added, 1)


NORM_SEMS = ("stat", "aggregate", "spread", "root", "scale", "normed", "turned")


def layernorm_phase(nc, M, out=None):
    GROUP = 4
    GROUPS = TILES // GROUP
    with scope(nc, f"ln{M.norms}") as s:
        before_t, before_g = M.norms * TILES, M.norms * GROUPS
        M.norms += 1
        stats = s.sb("stats", [P, TILES, 6])
        mv = s.sb("mv", [P, TILES, 2])
        var = s.sb("var", [P, TILES])
        rstd = s.sb("rstd", [P, TILES])
        banks = [s.ps(f"bank{n}") for n in range(8)]
        stat, aggregate, spread, root, scale, normed, turned = (M.norm_sems[n] for n in NORM_SEMS)

        def tiles(g):
            return range(g * GROUP, (g + 1) * GROUP)

        def part(g):
            return slice(g * GROUP, (g + 1) * GROUP)

        with nc.Block() as block:
            @block.vector
            def _(dve):
                def spreads(g):
                    for t in tiles(g):
                        nc.vector.bn_stats(stats[:, t, :], M.x[:, t, :]).then_inc(stat, 1)
                    for t in tiles(g):
                        dve.wait_ge(stat, before_t + t + 1)
                        nc.vector.bn_aggr(mv[:, t, :], stats[:, t, :]).then_inc(aggregate, 1)
                    dve.wait_ge(aggregate, before_t + (g + 1) * GROUP)
                    nc.vector.tensor_scalar(var[:, part(g)], mv[:, part(g), 1], LN_EPS, None, ALU.add
                                            ).then_inc(spread, 1)

                def normalize(g):
                    dve.wait_ge(root, before_g + g + 1)
                    nc.vector.reciprocal(rstd[:, part(g)], rstd[:, part(g)]).then_inc(scale, 1)
                    dve.wait_ge(scale, before_g + g + 1)
                    for t in tiles(g):
                        nc.vector.tensor_scalar(M.x[:, t, :], M.x[:, t, :], mv[:, t, 0:1], rstd[:, t:t + 1],
                                                ALU.subtract, ALU.mult).then_inc(normed, 1)

                for g in range(GROUPS):
                    spreads(g)
                    if g:
                        normalize(g - 1)
                normalize(GROUPS - 1)

            @block.scalar
            def _(act):
                def copies(g):
                    for t in range(g * GROUP, (g + 1) * GROUP, 2):
                        act.wait_ge(turned, before_t + t + 2)
                        nc.scalar.activation(M.xT[:, :, t * P:(t + 2) * P],
                                             banks[t // 2][:, :].rearrange("p (k t) -> p k t", k=KD), ACT.Copy)

                for g in range(GROUPS):
                    act.wait_ge(spread, before_g + g + 1)
                    nc.scalar.activation(rstd[:, part(g)], var[:, part(g)], ACT.Sqrt).then_inc(root, 1)
                    if g and out is None:
                        copies(g - 1)
                if out is None:
                    copies(GROUPS - 1)

            @block.tensor
            def _(pe):
                if out is None:
                    for t in range(TILES):
                        pe.wait_ge(normed, before_t + t + 1)
                        for c in range(KD):
                            last = nc.tensor.transpose(
                                banks[t // 2][:, c * DM + (t % 2) * P:c * DM + (t % 2 + 1) * P],
                                M.x[:, t, c * P:(c + 1) * P], M.ident[:, :])
                        last.then_inc(turned, 1)

            @block.sync
            def _(sp):
                if out is not None:
                    rows = out.rearrange("b s d -> (b s) d").rearrange("(n p) d -> p n d", p=P)
                    for g in range(GROUPS):
                        sp.wait_ge(normed, before_t + (g + 1) * GROUP)
                        sp.dma_start(rows[:, part(g), :], M.x[:, part(g), :]).then_inc(M.stored, 16)
                    sp.wait_ge(M.stored, GROUPS * 16)


def projection_phase(nc, M, D, G, squares_sum):
    with scope(nc, "pr") as s:
        wo = s.sb("wo", [P, PAIRS, DM])
        rms = s.sb("rms", [P, BLK])
        inv = s.sb("inv", [P, BLK])
        eps = s.sb("eps", [P, 1])
        bank = [s.ps(f"bank{n}") for n in range(KD)]
        ps_sum = s.ps("sum")
        wo_loaded, x_loaded = s.sem("wo_loaded"), s.sem("x_loaded")
        ready, summed, rooted, inverted = s.sem("ready"), s.sem("summed"), s.sem("rooted"), s.sem("inverted")
        product, scaled = s.sem("product"), s.sem("scaled")
        res = Residual(nc, M, s, 1.0)

        with nc.Block() as block:
            @block.sync
            def _(sp):
                sp.dma_start(wo[:, :, :], D["out_w"].rearrange("(a p) d -> p a d", p=P)).then_inc(wo_loaded, 16)
                sp.dma_start(M.x[:, :, :], D["x"].rearrange("(n p) d -> p n d", p=P)).then_inc(x_loaded, 16)

            @block.tensor
            def _(pe):
                pe.wait_ge(wo_loaded, 16)
                with pe.Fori(0, NBLK) as i:
                    pe.wait_ge(rooted, i + 1)
                    nc.tensor.matmul(ps_sum[:, :], M.ones[:, :], squares_sum[:, ds(i * BLK, BLK)],
                                     start=True, stop=True).then_inc(summed, 1)
                    for d in range(KD):
                        pe.wait_ge(scaled, i * KD + d + 1)
                        for a in range(PAIRS):
                            last = nc.tensor.matmul(bank[d][:, :], wo[:, a, d * P:(d + 1) * P],
                                                    G[:, a, ds(i * BLK, BLK)],
                                                    start=(a == 0), stop=(a == PAIRS - 1))
                        last.then_inc(product, 1)
                    res.tensor(pe, i, scaled, i * KD + 2 * KD)

            @block.scalar
            def _(act):
                act.sem_inc(rooted, 1)
                act.wait_ge(ready, 1)
                with act.Fori(0, NBLK) as i:
                    act.wait_ge(summed, i + 1)
                    act.wait_ge(inverted, i + 1)
                    nc.scalar.activation(rms[:, :], ps_sum[:, :], ACT.Sqrt, scale=1.0 / FEAT,
                                         bias=eps[:, 0:1]).then_inc(rooted, 1)

            @block.vector
            def _(dve):
                nc.vector.memset(eps[:, :], 1e-5).then_inc(ready, 1)
                dve.sem_inc(inverted, 1)
                dve.sem_inc(scaled, KD)
                dve.sem_inc(res.added, KD)
                dve.wait_ge(x_loaded, 16)
                with dve.Fori(0, NBLK) as i:
                    dve.wait_ge(rooted, i + 2)
                    nc.vector.reciprocal(inv[:, :], rms[:, :]).then_inc(inverted, 1)
                    dve.wait_ge(inverted, i + 2)
                    for d in range(KD):
                        dve.wait_ge(product, i * KD + d + 1)
                        nc.vector.tensor_tensor(res.y[:, d, :], bank[d][:, :], inv[:, :], ALU.mult
                                                ).then_inc(scaled, 1)
                    res.vector(dve, i)


ROUTED, SHARED, FF = 16, 2, 176
TOP_K = 4
EXPERTS = ROUTED + SHARED
PARTS = 3
FTILES = -(-EXPERTS * FF // P)
LOADS = 5
FPL = FTILES // LOADS


def expert_rows():
    import numpy as np
    t = np.zeros((PARTS, EXPERTS, FTILES * P))
    for e in range(EXPERTS):
        t[:, e, e * FF:(e + 1) * FF] = 1.0
        t[:, e, EXPERTS * FF + e] = 1.0
    return t.reshape(PARTS * EXPERTS, FTILES * P).astype(np.uint16) * ONE_BITS


def router_phase(nc, M, D, gate_parts, load_weights):
    with scope(nc, "ro") as s:
        cent = s.sb("cent", [P, KD, ROUTED])
        bias = s.sb("bias", [P, ROUTED])
        score = s.sb("score", [P, TILES, ROUTED])
        top = s.sb("top", [P, TILES, 8])
        kept = s.sb("kept", [P, TILES, ROUTED])
        total = s.sb("total", [P, TILES])
        g = s.sb("g", [P, TILES, EXPERTS])
        parts = s.sb("parts", [P, TILES, PARTS, EXPERTS], BF16)
        rest = [s.sb(f"rest{n}", [P, TILES, EXPERTS]) for n in range(PARTS - 1)]
        ps_score = s.ps("score")
        ps_part = [s.ps(f"part{n}", (P, 1024), BF16) for n in range(2)]
        loaded, product, squashed, step = s.sem("loaded"), s.sem("product"), s.sem("squashed"), s.sem("step")
        g_ready, parts_ready, turned = s.sem("g_ready"), s.sem("parts_ready"), s.sem("turned")
        with nc.Block() as block:
            @block.sync
            def _(sp):
                sp.dma_start(cent[:, :, :], D["centroids"].rearrange("(k p) e -> p k e", p=P)).then_inc(loaded, 16)
                sp.dma_start(bias[:, :], D["route_bias"].partition_broadcast(P)).then_inc(loaded, 16)
                load_weights(sp)

            @block.tensor
            def _(pe):
                pe.wait_ge(loaded, 32)
                for t in range(TILES):
                    for c in range(KD):
                        last = nc.tensor.matmul(ps_score[:, t * ROUTED:(t + 1) * ROUTED],
                                                M.xT[:, c, t * P:(t + 1) * P], cent[:, c, :],
                                                start=(c == 0), stop=(c == KD - 1))
                last.then_inc(product, 1)
                pe.wait_ge(parts_ready, PARTS)
                for t in range(TILES):
                    last = nc.tensor.transpose(ps_part[t // 8][0:PARTS * EXPERTS, t % 8 * P:(t % 8 + 1) * P],
                                               parts[:, t, :, :].rearrange("p a e -> p (a e)"), M.ident16[:, :])
                    if t % 8 == 7:
                        last.then_inc(turned, 1)

            @block.scalar
            def _(act):
                act.wait_ge(product, 1)
                nc.scalar.activation(score[:, :, :].rearrange("p t e -> p (t e)"),
                                     ps_score[:, 0:TILES * ROUTED], ACT.Sigmoid).then_inc(squashed, 1)
                for n in range(2):
                    act.wait_ge(turned, n + 1)
                    nc.scalar.activation(gate_parts[:, n * 1024:(n + 1) * 1024],
                                         ps_part[n][0:PARTS * EXPERTS, :], ACT.Copy)

            @block.vector
            def _(dve):
                def wide(ap):
                    return ap.broadcast_to([P, TILES, ROUTED])

                nc.vector.memset(g[:, :, ROUTED:EXPERTS], 1.0)
                dve.wait_ge(loaded, 32)
                dve.wait_ge(squashed, 1)
                nc.vector.tensor_tensor(score[:, :, :], score[:, :, :], wide(bias[:, :].unsqueeze(1)),
                                        ALU.add).then_inc(step, 1)
                dve.wait_ge(step, 1)
                for t in range(TILES):
                    last = nc.vector.max(top[:, t, :], score[:, t, :])
                last.then_inc(step, 1)
                dve.wait_ge(step, 2)
                nc.vector.tensor_tensor(kept[:, :, :], score[:, :, :], wide(top[:, :, TOP_K - 1:TOP_K]),
                                        ALU.is_ge).then_inc(step, 1)
                dve.wait_ge(step, 3)
                nc.vector.tensor_tensor(kept[:, :, :], kept[:, :, :], score[:, :, :], ALU.mult).then_inc(step, 1)
                dve.wait_ge(step, 4)
                nc.vector.tensor_reduce(total[:, :], kept[:, :, :], AX.X, ALU.add).then_inc(step, 1)
                dve.wait_ge(step, 5)
                nc.vector.tensor_scalar(total[:, :], total[:, :], 1e-8, None, ALU.max).then_inc(step, 1)
                dve.wait_ge(step, 6)
                nc.vector.reciprocal(total[:, :], total[:, :]).then_inc(step, 1)
                dve.wait_ge(step, 7)
                nc.vector.tensor_tensor(g[:, :, 0:ROUTED], kept[:, :, :], wide(total[:, :].unsqueeze(2)),
                                        ALU.mult).then_inc(g_ready, 1)
                dve.wait_ge(g_ready, 1)
                whole = g
                for n in range(PARTS):
                    nc.vector.tensor_copy(parts[:, :, n, :], whole[:, :, :]).then_inc(parts_ready, 1)
                    if n < PARTS - 1:
                        dve.wait_ge(parts_ready, n + 1)
                        nc.vector.tensor_tensor(rest[n][:, :, :], whole[:, :, :], parts[:, :, n, :],
                                                ALU.subtract).then_inc(step, 1)
                        dve.wait_ge(step, 8 + n)
                        whole = rest[n]


def experts_phase(nc, M, D):
    with scope(nc, "mo") as s:
        gate_parts = s.sb("gate_parts", [PARTS * EXPERTS, TOKENS], BF16)
        w1, w1L = s.sb_both("w1", [P, KD, FTILES * P])
        w2, w2L = s.sb_both("w2", [P, FTILES, DM])
        w_loaded = [s.sem(f"w_loaded{n}") for n in range(LOADS)]

        def load_weights(sp):
            for n in range(LOADS):
                c = slice(n * FPL * P, (n + 1) * FPL * P)
                sp.dma_start(w1[:, :, c], D["w1"].rearrange("(k p) f -> p k f", p=P)[:, :, c]
                             ).then_inc(w_loaded[n], 16)
                sp.dma_start(w2[:, n * FPL:(n + 1) * FPL, :],
                             D["w2"].rearrange("(f p) d -> p f d", p=P)[:, n * FPL:(n + 1) * FPL, :]
                             ).then_inc(w_loaded[n], 16)

        router_phase(nc, M, D, gate_parts, load_weights)
        w1H = s.sb("w1H", [P, KD, FTILES * P], FP32R)
        w2H = s.sb("w2H", [P, FTILES, DM], FP32R)
        xH = s.sb("xH", [P, KD, TOKENS], FP32R)
        xL = M.xL
        b1 = s.sb("b1", [P, FTILES])
        rows = s.sb("rows", [PARTS * EXPERTS, FTILES * P], BF16)
        NH = 3
        hidden = [s.sb(f"hidden{n}", [P, BLK]) for n in range(2)]
        gated = [s.sb(f"gated{n}", [P, BLK]) for n in range(2)]
        gatedH = [s.sb(f"gatedH{n}", [P, BLK], FP32R) for n in range(NH)]
        gatedL = [s.sb(f"gatedL{n}", [P, BLK], FP32R) for n in range(NH)]
        ps_h = [s.ps(f"h{n}") for n in range(2)]
        ps_g = [s.ps(f"g{n}") for n in range(2)]
        acc = [s.ps(f"acc{n}") for n in range(KD)]
        small_loaded = s.sem("small_loaded")
        w_high, w_low, x_high, x_low = s.sem("w_high"), s.sem("w_low"), s.sem("x_high"), s.sem("x_low")
        high_ready, low_ready = s.sem("high_ready"), s.sem("low_ready")
        h_product, g_product, relu_ready = s.sem("h_product"), s.sem("g_product"), s.sem("relu_ready")
        gated_ready, used = s.sem("gated_ready"), s.sem("used")
        product, y_ready = s.sem("product"), s.sem("y_ready")
        res = Residual(nc, M, s, 2.0)

        def done(i, f):
            return i * FTILES + (FTILES + f + 1)

        with nc.Block() as block:
            @block.sync
            def _(sp):
                sp.dma_start(b1[:, :], D["b1"]).then_inc(small_loaded, 16)
                sp.dma_start(rows[:, :], D["expert_rows"].bitcast(BF16)).then_inc(small_loaded, 16)

            @block.tensor
            def _(pe):
                pe.sem_inc(used, FTILES)
                pe.wait_ge(small_loaded, 32)
                with pe.Fori(0, NBLK) as i:
                    pe.wait_ge(x_low, i + 1)
                    for f in range(FTILES + 2):
                        if f < FTILES:
                            fs = slice(f * P, (f + 1) * P)
                            pe.wait_ge(w_low, 2 * f + 2)
                            pe.wait_ge(relu_ready, done(i, f - 2))
                            for c in range(KD):
                                xs = (slice(None), c, ds(i * BLK, BLK))
                                nc.tensor.matmul(ps_h[f % 2][:, :], w1H[:, c, fs], xH[xs], start=(c == 0), stop=False)
                                nc.tensor.matmul(ps_h[f % 2][:, :], w1H[:, c, fs], xL[xs], start=False, stop=False)
                                last = nc.tensor.matmul(ps_h[f % 2][:, :], w1L[:, c, fs], xH[xs],
                                                        start=False, stop=(c == KD - 1))
                            last.then_inc(h_product, 1)
                            wait_apart(pe, gated_ready, done(i, f - 2), M.passed)
                            nc.tensor.matmul(ps_g[f % 2][:, :], rows[:, fs], gate_parts[:, ds(i * BLK, BLK)],
                                             start=True, stop=True).then_inc(g_product, 1)
                        if f == 1:
                            pe.wait_ge(y_ready, i * KD + KD)
                        if f >= 2:
                            g = f - 2
                            pe.wait_ge(low_ready, done(i, g))
                            for d in range(KD):
                                of = slice(d * P, (d + 1) * P)
                                nc.tensor.matmul(acc[d][:, :], w2H[:, g, of], gatedH[g % NH][:, :],
                                                 start=(g == 0), stop=False)
                                nc.tensor.matmul(acc[d][:, :], w2H[:, g, of], gatedL[g % NH][:, :],
                                                 start=False, stop=False)
                                last = nc.tensor.matmul(acc[d][:, :], w2L[:, g, of], gatedH[g % NH][:, :],
                                                        start=False, stop=(g == FTILES - 1))
                            last.then_inc(used, 1)
                    res.tensor(pe, i, y_ready, i * KD + 2 * KD)

            @block.gpsimd
            def _(pool):
                for f in range(FTILES):
                    if f % FPL == 0:
                        pool.wait_ge(w_loaded[f // FPL], 32)
                    fs = slice(f * P, (f + 1) * P)
                    nc.gpsimd.tensor_copy(w1H[:, :, fs], w1[:, :, fs]).then_inc(w_high, 1)
                    nc.gpsimd.tensor_copy(w2H[:, f, :], w2[:, f, :]).then_inc(w_high, 1)
                    pool.wait_ge(w_high, 2 * f + 1)
                    nc.gpsimd.tensor_tensor(w1L[:, :, fs], w1[:, :, fs], w1H[:, :, fs].bitcast(FP32), ALU.subtract
                                            ).then_inc(w_low, 1)
                    pool.wait_ge(w_high, 2 * f + 2)
                    nc.gpsimd.tensor_tensor(w2L[:, f, :], w2[:, f, :], w2H[:, f, :].bitcast(FP32), ALU.subtract
                                            ).then_inc(w_low, 1)

            @block.scalar
            def _(act):
                act.sem_inc(relu_ready, FTILES)
                act.sem_inc(high_ready, FTILES)
                act.sem_inc(y_ready, KD)
                for n in range(NBLK):
                    nc.scalar.activation(xH[:, :, n * BLK:(n + 1) * BLK], M.xT[:, :, n * BLK:(n + 1) * BLK], ACT.Copy
                                         ).then_inc(x_high, 1)
                act.wait_ge(small_loaded, 32)

                def high(i, f):
                    act.wait_ge(gated_ready, done(i, f))
                    act.wait_ge(used, done(i, f - NH))
                    nc.scalar.activation(gatedH[f % NH][:, :], gated[f % 2][:, :], ACT.Copy).then_inc(high_ready, 1)

                with act.Fori(0, NBLK) as i:
                    for f in range(FTILES):
                        act.wait_ge(h_product, done(i, f) - FTILES)
                        act.wait_ge(gated_ready, done(i, f - 2))
                        nc.scalar.activation(hidden[f % 2][:, :], ps_h[f % 2][:, :], ACT.Relu,
                                             bias=b1[:, f:f + 1]).then_inc(relu_ready, 1)
                        if f >= 1:
                            high(i, f - 1)
                    high(i, FTILES - 1)
                    act.wait_ge(used, done(i, FTILES - 1))
                    for d in range(KD):
                        nc.scalar.activation(res.y[:, d, :], acc[d][:, :], ACT.Copy).then_inc(y_ready, 1)

            @block.vector
            def _(dve):
                dve.sem_inc(gated_ready, FTILES)
                dve.sem_inc(low_ready, FTILES)
                dve.sem_inc(res.added, KD)
                for n in range(NBLK):
                    b = slice(n * BLK, (n + 1) * BLK)
                    dve.wait_ge(x_high, n + 1)
                    nc.vector.tensor_tensor(xL[:, :, b], M.xT[:, :, b], xH[:, :, b].bitcast(FP32), ALU.subtract
                                            ).then_inc(x_low, 1)

                def low(i, f):
                    dve.wait_ge(high_ready, done(i, f))
                    nc.vector.tensor_tensor(gatedL[f % NH][:, :], gated[f % 2][:, :], gatedH[f % NH][:, :].bitcast(FP32),
                                            ALU.subtract).then_inc(low_ready, 1)

                with dve.Fori(0, NBLK) as i:
                    for f in range(FTILES):
                        dve.wait_ge(relu_ready, done(i, f))
                        dve.wait_ge(g_product, done(i, f) - FTILES)
                        dve.wait_ge(low_ready, done(i, f - 2))
                        nc.vector.tensor_tensor(gated[f % 2][:, :], hidden[f % 2][:, :], ps_g[f % 2][:, :],
                                                ALU.mult).then_inc(gated_ready, 1)
                        if f >= 1:
                            low(i, f - 1)
                    low(i, FTILES - 1)
                    res.vector(dve, i)


STATES, DT_RANK = 16, 128
BC = 2 * STATES
HALF = 2 * SEQ
SEQ_HALF = HALF // SEQ


def state_rows():
    import numpy as np
    t = np.zeros((PARTS, BC, BC, P))
    t[:, np.arange(BC), np.arange(BC), :] = 1.0
    return t.reshape(PARTS * BC, BC * P).astype(np.uint16) * ONE_BITS


def step_phase(nc, M, D, dt, dtx, bc_parts, decay):
    with scope(nc, "dt") as s:
        wx = s.sb("wx", [P, KD, DT_RANK + PARTS * BC])
        wdt = s.sb("wdt", [P, DM])
        bx = s.sb("bx", [P, 1])
        bbc = s.sb("bbc", [PARTS * BC, 1])
        bdt = s.sb("bdt", [P, KD])
        rank = s.sb("rank", [P, BLK])
        bc = s.sb("bc", [PARTS * BC, BLK])
        high = s.sb("high", [PARTS * BC, BLK], BF16)
        rest = s.sb("rest", [PARTS * BC, BLK])
        mid = s.sb("mid", [PARTS * BC, BLK], BF16)
        rest2 = s.sb("rest2", [PARTS * BC, BLK])
        size = [s.sb(f"size{d}", [P, BLK]) for d in range(KD)]
        e = [s.sb(f"e{d}", [P, BLK]) for d in range(KD)]
        log = [s.sb(f"log{d}", [P, BLK]) for d in range(KD)]
        one_e = [s.sb(f"one_e{d}", [P, BLK]) for d in range(KD)]
        lost = [s.sb(f"lost{d}", [P, BLK]) for d in range(KD)]
        positive = [s.sb(f"positive{d}", [P, BLK]) for d in range(KD)]
        ps_rank, ps_bc = s.ps("rank"), s.ps("bc")
        ps_dt = [s.ps(f"dt{d}") for d in range(KD)]
        loaded, rank_product, bc_product, dt_product = (s.sem(n) for n in ("loaded", "rank_product", "bc_product", "dt_product"))
        rank_ready, bc_ready, bc_step = s.sem("rank_ready"), s.sem("bc_ready"), s.sem("bc_step")
        size_ready, e_ready, log_ready, dt_step = s.sem("size_ready"), s.sem("e_ready"), s.sem("log_ready"), s.sem("dt_step")
        bc_kept = s.sem("bc_kept")
        a_step = s.sem("a_step")
        LOADED = 7 * 16
        VS = 6
        with nc.Block() as block:
            @block.sync
            def _(sp):
                for to, of in ((wx[:, :, :], D["wx"].rearrange("(k p) r -> p k r", p=P)), (wdt[:, :], D["wdt"]),
                               (bx[:, :], D["bx"][0:DT_RANK, :]), (bbc[:, :], D["bx"][DT_RANK:, :]),
                               (bdt[:, :], D["bdt"]), (decay[:, :, :], D["a_log"]),
                               (M.state_rows[:, :], D["state_rows"].bitcast(BF16))):
                    sp.dma_start(to, of).then_inc(loaded, 16)

            @block.tensor
            def _(pe):
                pe.wait_ge(loaded, LOADED)
                with pe.Fori(0, NBLK) as i:
                    for to, cols, sem, free in ((ps_rank[:, :], slice(0, DT_RANK), rank_product, rank_ready),
                                                (ps_bc[0:PARTS * BC, :], slice(DT_RANK, DT_RANK + PARTS * BC),
                                                 bc_product, bc_ready)):
                        pe.wait_ge(free, i + 1)
                        for c in range(KD):
                            last = nc.tensor.matmul(to, wx[:, c, cols], M.xT[:, c, ds(i * BLK, BLK)],
                                                    start=(c == 0), stop=(c == KD - 1))
                        last.then_inc(sem, 1)
                    pe.wait_ge(rank_ready, i + 2)
                    pe.wait_ge(dt_step, i * KD * VS + 1)
                    for d in range(KD):
                        nc.tensor.matmul(ps_dt[d][:, :], wdt[:, d * P:(d + 1) * P], rank[:, :],
                                         start=True, stop=True).then_inc(dt_product, 1)

            @block.scalar
            def _(act):
                act.sem_inc(rank_ready, 1)
                act.sem_inc(bc_ready, 1)
                act.wait_ge(loaded, LOADED)
                nc.scalar.activation(decay[:, :, :], decay[:, :, :], ACT.Exp).then_inc(a_step, 1)
                with act.Fori(0, NBLK) as i:
                    act.wait_ge(rank_product, i + 1)
                    nc.scalar.activation(rank[:, :], ps_rank[:, :], ACT.Identity, bias=bx[:, 0:1]).then_inc(rank_ready, 1)
                    act.wait_ge(bc_product, i + 1)
                    act.wait_ge(bc_kept, i + 1)
                    nc.scalar.activation(bc[:, :], ps_bc[0:PARTS * BC, :], ACT.Identity, bias=bbc[:, 0:1]
                                         ).then_inc(bc_ready, 1)
                    for d in range(KD):
                        act.wait_ge(dt_product, i * KD + d + 1)
                        act.wait_ge(dt_step, i * KD * VS + 1)
                        nc.scalar.activation(size[d][:, :], ps_dt[d][:, :], ACT.Abs, bias=bdt[:, d:d + 1]
                                             ).then_inc(size_ready, 1)
                    for d in range(KD):
                        act.wait_ge(size_ready, i * KD + d + 1)
                        nc.scalar.activation(e[d][:, :], size[d][:, :], ACT.Exp, scale=-1.0).then_inc(e_ready, 1)
                    for d in range(KD):
                        act.wait_ge(e_ready, i * KD + d + 1)
                        nc.scalar.activation(log[d][:, :], e[d][:, :], ACT.Ln, bias=1.0).then_inc(log_ready, 1)

            @block.vector
            def _(dve):
                dve.sem_inc(dt_step, 1)
                dve.wait_ge(a_step, 1)
                nc.vector.tensor_scalar(decay[:, :, :], decay[:, :, :], -1.0, None, ALU.mult).then_inc(a_step, 1)
                dve.wait_ge(loaded, LOADED)
                dve.sem_inc(bc_kept, 1)
                with dve.Fori(0, NBLK) as i:
                    def keep(n, of):
                        rows = slice(n * BC, (n + 1) * BC)
                        return nc.vector.tensor_copy(bc_parts[rows, ds(i * BLK, BLK)], of[rows, :])

                    wait_apart(dve, bc_ready, i + 2, M.passed)
                    nc.vector.tensor_copy(high[:, :], bc[:, :]).then_inc(bc_step, 1)
                    keep(0, bc)
                    dve.wait_ge(bc_step, i * 4 + 1)
                    nc.vector.tensor_tensor(rest[:, :], bc[:, :], high[:, :], ALU.subtract).then_inc(bc_step, 1)
                    wait_apart(dve, bc_step, i * 4 + 2, M.passed)
                    nc.vector.tensor_copy(mid[:, :], rest[:, :]).then_inc(bc_step, 1)
                    keep(1, rest)
                    dve.wait_ge(bc_step, i * 4 + 3)
                    nc.vector.tensor_tensor(rest2[:, :], rest[:, :], mid[:, :], ALU.subtract).then_inc(bc_step, 1)
                    wait_apart(dve, bc_step, i * 4 + 4, M.passed)
                    keep(2, rest2).then_inc(bc_kept, 1)
                    for d in range(KD):
                        at = lambda n: i * KD * VS + (d * VS + n + 1)
                        dt_out, x_in = dt[:, d:d + 1, ds(i * BLK, BLK)], M.xT[:, d:d + 1, ds(i * BLK, BLK)]
                        dtx_out = dtx[:, d:d + 1, ds(i * BLK, BLK)]
                        dve.wait_ge(size_ready, i * KD + d + 1)
                        nc.vector.tensor_scalar(positive[d][:, :], ps_dt[d][:, :], bdt[:, d:d + 1], 0.0,
                                                ALU.add, ALU.max).then_inc(dt_step, 1)
                        dve.wait_ge(e_ready, i * KD + d + 1)
                        nc.vector.tensor_scalar(one_e[d][:, :], e[d][:, :], 1.0, None, ALU.add).then_inc(dt_step, 1)
                        dve.wait_ge(dt_step, at(2))
                        nc.vector.scalar_tensor_tensor(lost[d][:, :], one_e[d][:, :], 1.0, e[d][:, :],
                                                       ALU.subtract, ALU.subtract).then_inc(dt_step, 1)
                        dve.wait_ge(log_ready, i * KD + d + 1)
                        dve.wait_ge(dt_step, at(3))
                        nc.vector.tensor_tensor(log[d][:, :], log[d][:, :], lost[d][:, :], ALU.subtract
                                                ).then_inc(dt_step, 1)
                        dve.wait_ge(dt_step, at(4))
                        nc.vector.tensor_tensor(dt_out, log[d][:, :].unsqueeze(1), positive[d][:, :].unsqueeze(1),
                                                ALU.add).then_inc(dt_step, 1)
                        dve.wait_ge(dt_step, at(5))
                        nc.vector.tensor_tensor(dtx_out, dt_out, x_in, ALU.mult).then_inc(dt_step, 1)

def scan_phase(nc, M, D):
    with scope(nc, "sc") as s:
        dt = s.sb("dt", [P, KD, TOKENS])
        dtx = s.sb("dtx", [P, KD, TOKENS])
        bc_parts = s.sb("bc_parts", [PARTS * BC, TOKENS], BF16)
        decay = s.sb("decay", [P, KD, STATES])
        M.state_rows = s.sb("state_rows", [PARTS * BC, BC * P], BF16)
        y = s.sb("y", [P, KD, TOKENS])
        step_phase(nc, M, D, dt, dtx, bc_parts, decay)
        bs = [s.sb(f"bs{n}", [P, HALF]) for n in range(2)]
        a = [[s.sb(f"a{n}{d}", [P, HALF]) for d in range(KD)] for n in range(2)]
        bx = [[s.sb(f"bx{n}{d}", [P, HALF]) for d in range(KD)] for n in range(2)]
        h = [s.sb(f"h{d}", [P, HALF]) for d in range(KD)]
        hc = [[s.sb(f"hc{n}{d}", [P, HALF]) for d in range(KD)] for n in range(2)]
        with scope(nc, "s2") as q:
            ps_b, ps_c = q.ps("b", (P, HALF)), q.ps("c", (P, HALF))
            ps_y = [q.ps(f"y{d}", (P, HALF)) for d in range(KD)]
            b_product, c_product, y_sum = q.sem("b_product"), q.sem("c_product"), q.sem("y_sum")
            b_ready, a_ready, bx_ready = q.sem("b_ready"), q.sem("a_ready"), q.sem("bx_ready")
            scanned, hc_ready, y_ready = q.sem("scanned"), q.sem("hc_ready"), q.sem("y_ready")

            def done(i, n):
                return i * STATES + (STATES + n + 1)

            def done2(i, n, d=KD - 1):
                return i * (STATES * KD) + (STATES + n) * KD + d + 1

            with nc.Block() as block:
                def spread(i, to, row):
                    for t in range(HALF // BLK):
                        last = nc.tensor.matmul(to[:, t * BLK:(t + 1) * BLK],
                                                M.state_rows[:, row * P:(row + 1) * P],
                                                bc_parts[:, ds(i * HALF + t * BLK, BLK)], start=True, stop=True)
                    return last

                @block.tensor
                def _(pe):
                    pe.sem_inc(y_sum, STATES * KD)
                    with pe.Fori(0, TOKENS // HALF) as i:
                        for n in range(STATES + 1):
                            if n < STATES:
                                wait_apart(pe, b_ready, done(i, n - 1), M.passed)
                                spread(i, ps_b, n).then_inc(b_product, 1)
                                wait_apart(pe, hc_ready, done2(i, n - 1), M.passed)
                                spread(i, ps_c, STATES + n).then_inc(c_product, 1)
                            if n == 1:
                                pe.wait_ge(y_ready, i * KD + KD)
                            if n >= 1:
                                for d in range(KD):
                                    pe.wait_ge(hc_ready, done2(i, n - 1, d))
                                    for t in range(HALF // BLK):
                                        last = nc.tensor.matmul(ps_y[d][:, t * BLK:(t + 1) * BLK], M.ident[:, :],
                                                                hc[(n - 1) % 2][d][:, t * BLK:(t + 1) * BLK],
                                                                start=(n == 1), stop=(n == STATES))
                                    last.then_inc(y_sum, 1)

                @block.scalar
                def _(act):
                    act.sem_inc(b_ready, STATES)
                    act.sem_inc(y_ready, KD)
                    with act.Fori(0, TOKENS // HALF) as i:
                        for n in range(STATES):
                            act.wait_ge(b_product, done(i, n) - STATES)
                            act.wait_ge(bx_ready, done2(i, n - 2))
                            nc.scalar.activation(bs[n % 2][:, :], ps_b[:, :], ACT.Copy).then_inc(b_ready, 1)
                            for d in range(KD):
                                wait_apart(act, scanned, done2(i, n - 2, d), M.passed)
                                nc.scalar.activation(a[n % 2][d][:, :].unsqueeze(1),
                                                     dt[:, d:d + 1, ds(i * HALF, HALF)], ACT.Exp,
                                                     scale=decay[:, d, n:n + 1]).then_inc(a_ready, 1)
                        for d in range(KD):
                            act.wait_ge(y_sum, done2(i, STATES - 1, d))
                            nc.scalar.activation(y[:, d:d + 1, ds(i * HALF, HALF)], ps_y[d][:, :].unsqueeze(1),
                                                 ACT.Copy).then_inc(y_ready, 1)

                @block.gpsimd
                def _(pool):
                    pool.sem_inc(bx_ready, STATES * KD)
                    with pool.Fori(0, TOKENS // HALF) as i:
                        for n in range(STATES):
                            wait_apart(pool, b_ready, done(i, n), M.passed)
                            for d in range(KD):
                                wait_apart(pool, scanned, done2(i, n - 2, d), M.passed)
                                nc.gpsimd.tensor_tensor(bx[n % 2][d][:, :].unsqueeze(1),
                                                        dtx[:, d:d + 1, ds(i * HALF, HALF)],
                                                        bs[n % 2][:, :].unsqueeze(1), ALU.mult).then_inc(bx_ready, 1)

                @block.vector
                def _(dve):
                    dve.sem_inc(scanned, STATES * KD)
                    dve.sem_inc(hc_ready, STATES * KD)
                    with dve.Fori(0, TOKENS // HALF) as i:
                        for n in range(STATES):
                            for d in range(KD):
                                dve.wait_ge(a_ready, done2(i, n, d) - STATES * KD)
                                dve.wait_ge(bx_ready, done2(i, n, d))
                                dve.wait_ge(hc_ready, done2(i, n - 1, d))
                                for q_ in range(SEQ_HALF):
                                    t = slice(q_ * SEQ, (q_ + 1) * SEQ)
                                    last = nc.vector.tensor_tensor_scan(h[d][:, t], a[n % 2][d][:, t],
                                                                        bx[n % 2][d][:, t], 0.0, ALU.mult, ALU.add)
                                last.then_inc(scanned, 1)
                            for d in range(KD):
                                dve.wait_ge(scanned, done2(i, n, d))
                                dve.wait_ge(c_product, done(i, n) - STATES)
                                dve.wait_ge(y_sum, done2(i, n - 2, d))
                                nc.vector.tensor_tensor(hc[n % 2][d][:, :], h[d][:, :], ps_c[:, :], ALU.mult
                                                        ).then_inc(hc_ready, 1)
        with scope(nc, "s3") as q:
            res = Residual(nc, M, q, 1.0)
            copied = q.sem("copied")
            with nc.Block() as block:
                @block.tensor
                def _(pe):
                    with pe.Fori(0, NBLK) as i:
                        res.tensor(pe, i, copied, i + 1)

                @block.scalar
                def _(act):
                    with act.Fori(0, NBLK) as i:
                        act.wait_ge(res.added, i * KD + KD)
                        nc.scalar.activation(res.y[:, :, :], y[:, :, ds(i * BLK, BLK)], ACT.Copy).then_inc(copied, 1)

                @block.vector
                def _(dve):
                    dve.sem_inc(res.added, KD)
                    with dve.Fori(0, NBLK) as i:
                        res.vector(dve, i)


CROSS, PRIV, RETR = 1024, 128, 128
RHEADS, K_HEAD = 8, 8
KEYS = 45
KHD = RETR // 2
PAIRED = KEYS * KEYS
COLS = PAIRED + PAIRED % 2
EBLK = -(-COLS // P)
CUT = [(0, 1024), (1024, COLS)]
CUT_IN_THREE = (2, 6)
CUT3 = ((0, 676), (676, 1352), (1352, COLS))
QUARTER = tuple((a, min(a + 512, COLS)) for a in range(0, COLS, 512))
NEVER = -1.0e30
REPLACED = -3.0e38


def pair_rows():
    import numpy as np
    col = np.arange(COLS)
    e = np.minimum(col, PAIRED - 1)
    t = np.zeros((2 * KEYS, COLS), np.float32)
    t[e // KEYS, col] = 1.0
    t[KEYS + e % KEYS, col] = 1.0
    return t


def private_phase(nc, M, D, h, wk):
    UPT = CROSS // P
    with scope(nc, "pv") as s:
        wu = s.sb("wu", [P, KD, CROSS])
        wd = s.sb("wd", [P, UPT, PRIV])
        bu = s.sb("bu", [P, UPT])
        bd = s.sb("bd", [P, 1])
        wq = s.sb("wq", [KHD, 2 * RHEADS, PRIV])
        keys = s.sb("keys", [KHD, 2 * RHEADS, KEYS])
        up = [s.sb(f"up{n}", [P, BLK]) for n in range(2)]
        ps_up = [s.ps(f"up{n}") for n in range(2)]
        ps_h = s.ps("h")
        ps_k = [s.ps(f"k{n}") for n in range(2)]
        loaded, up_product, up_ready, up_used = s.sem("loaded"), s.sem("up_product"), s.sem("up_ready"), s.sem("up_used")
        h_product, h_ready, k_product = s.sem("h_product"), s.sem("h_ready"), s.sem("k_product")

        def done(i, m):
            return i * UPT + (UPT + m + 1)

        with nc.Block() as block:
            @block.sync
            def _(sp):
                for to, of in ((wu[:, :, :], D["w_up"].rearrange("(k p) c -> p k c", p=P)), (bu[:, :], D["b_up"]),
                               (wd[:, :, :], D["w_down"].rearrange("(m p) r -> p m r", p=P)), (bd[:, :], D["b_down"]),
                               (wq[:, :, :], D["w_q"]), (keys[:, :, :], D["keys"])):
                    sp.dma_start(to, of).then_inc(loaded, 16)

            @block.tensor
            def _(pe):
                pe.sem_inc(up_used, UPT)
                pe.wait_ge(loaded, 6 * 16)
                for n in range(2 * RHEADS):
                    last = nc.tensor.matmul(ps_k[n // RHEADS][:, n % RHEADS * KEYS:(n % RHEADS + 1) * KEYS],
                                            wq[:, n, :], keys[:, n, :], start=True, stop=True)
                last.then_inc(k_product, 1)
                with pe.Fori(0, NBLK) as i:
                    for m in range(UPT + 1):
                        if m < UPT:
                            pe.wait_ge(up_ready, done(i, m - 2))
                            for c in range(KD):
                                last = nc.tensor.matmul(ps_up[m % 2][:, :], wu[:, c, m * P:(m + 1) * P],
                                                        M.xT[:, c, ds(i * BLK, BLK)],
                                                        start=(c == 0), stop=(c == KD - 1))
                            last.then_inc(up_product, 1)
                        if m == 1:
                            pe.wait_ge(h_ready, i + 1)
                        if m >= 1:
                            pe.wait_ge(up_ready, done(i, m - 1))
                            last = nc.tensor.matmul(ps_h[:, :], wd[:, m - 1, :], up[(m - 1) % 2][:, :],
                                                    start=(m == 1), stop=(m == UPT))
                            last.then_inc(up_used, 1)

            @block.scalar
            def _(act):
                act.sem_inc(up_ready, UPT)
                act.sem_inc(h_ready, 1)
                act.wait_ge(loaded, 6 * 16)
                act.wait_ge(k_product, 1)
                for n in range(2):
                    nc.scalar.activation(wk[:, n * RHEADS * KEYS:(n + 1) * RHEADS * KEYS],
                                         ps_k[n][:, 0:RHEADS * KEYS], ACT.Copy)
                with act.Fori(0, NBLK) as i:
                    for m in range(UPT):
                        act.wait_ge(up_product, done(i, m) - UPT)
                        act.wait_ge(up_used, done(i, m - 2))
                        nc.scalar.activation(up[m % 2][:, :], ps_up[m % 2][:, :], ACT.Silu,
                                             bias=bu[:, m:m + 1]).then_inc(up_ready, 1)
                    wait_apart(act, up_used, done(i, UPT - 1), M.passed)
                    nc.scalar.activation(h[:, ds(i * BLK, BLK)], ps_h[:, :], ACT.Identity,
                                         bias=bd[:, 0:1]).then_inc(h_ready, 1)


PE_STEPS = """
    sums:0 turn_Z:0 sums:1 sums:2 turn_Z:1 turn_Z:2 sums:3 sums:4 fill_z:0 sums:5 sums:6 scores:0
    sums:7 fill_z:1 sums:8 turn_Z:3 sums:9 turn_kept:0 scores:1 sums:10 sums:11 sums:12 fill_z:2
    sums:13 fill_z:3 sums:14 sums:15 sums:16 sums:17 turn_kept:1 product:0 product:1 product:2
    product:3
""".split()
ACT_STEPS = """
    exps:0 copy_Z:0 exps:1 exps:2 copy_Z:1 exps:3 exps:4 copy_Z:2 copy_z:0 copy_h exps:5 exps:6
    silus:6 copy_scores:0 silus:7 copy_z:1 exps:7 copy_Z:3 exps:8 copy_scores:1 exps:9 copy_kept:0
    soften exps:10 exps:11 exps:12 copy_z:2 exps:13 exps:14 exps:15 copy_z:3 exps:16 exps:17 silus:0
    silus:1 copy_kept:1 silus:2 silus:3 silus:4 silus:5
""".split()
DVE_STEPS = """
    top_eights replace mask:0 mask:1 mask:2 mask:3 candidates mask:4 weigh:0 mask:5 keep mask:6
    bests weigh:2 replace_bests ninths thresholds mask:7 mask:8 mask:9 low_parts:0 totals mask:10
    mask:11 weigh:3 mask:12 mask:13 weigh:4 mask:14 mask:15 weigh:6 mask:16 weigh:7 weigh:10
    weigh:14 mask:17 weigh:16 add_out low_parts:1 weigh:17
""".split()
POOL_STEPS = """
    add:6 weigh:1 add:7 weigh:5 weigh:8 weigh:9 weigh:11 weigh:12 add:1 add:2 weigh:13 weigh:15
    add:3 add:4 add:5
""".split()


def take(steps, do):
    for step in steps:
        name, _, n = step.partition(":")
        do[name](int(n)) if n else do[name]()


def retrieval_phase(nc, M, D):
    with scope(nc, "re") as s:
        h = s.sb("h", [P, TOKENS])
        wk = s.sb("wk", [P, RHEADS * 2 * KEYS])
        private_phase(nc, M, D, h, wk)
        down = s.sb("down", [P, COLS])
        up = s.sb("up", [P, EBLK, DM])
        pairs = s.sb("pairs", [2 * KEYS, COLS], FP32R)
        hs = [s.sb(f"hs{n}", [P, P]) for n in range(2)]
        z = [s.sb(f"z{n}", [P, COLS]) for n in range(2)]
        sim = s.sb("sim", [P, 2 * RHEADS, KEYS])
        top = s.sb("top", [P, 2 * RHEADS, K_HEAD])
        left = s.sb("left", [P, 2 * RHEADS, KEYS])
        kept = s.sb("kept", [P, 2 * RHEADS, KEYS])
        cand = s.sb("cand", [P, RHEADS, K_HEAD, K_HEAD])
        best = s.sb("best", [P, RHEADS, 8])
        ninth = top[:, 0:RHEADS, :]
        soft = s.sb("soft", [P, RHEADS, 8])
        thr = [s.sb(f"thr{n}", [P, RHEADS]) for n in range(2)]
        shift = [s.sb(f"shift{n}", [P, RHEADS]) for n in range(2)]
        total = [s.sb(f"total{n}", [P, RHEADS]) for n in range(2)]
        keptH = [s.sb(f"keptH{n}", [2 * KEYS, RHEADS, P], FP32R) for n in range(2)]
        keptL = [s.sb(f"keptL{n}", [2 * KEYS, RHEADS, P], FP32R) for n in range(2)]
        NE = 4
        ex = [s.sb(f"ex{n}", [P, 1024]) for n in range(NE)]
        u = s.sb("u", [P, RHEADS, COLS])
        Z = [M.xT[:, n, 0:COLS] for n in range(2)]
        ZT = s.sb("ZT", [P, EBLK, P])
        NR = 3
        ring = [s.ps(f"ring{n}", (P, 1024)) for n in range(NR)]
        misc = [s.ps(f"misc{n}") for n in range(2)]

        names = ("loaded hs_ready filled z_filled z_ready sim_product sim_ready kept_ready kept_turned keptT_ready "
                 "prep ex_ready masked weighted pool_weighted silu_ready summed z_turned zT_ready out_product "
                 "out_added soft_in soft_ready total_ready prep_step cand_ready high_ready pairs_ready").split()
        S = {n: s.sem(n) for n in names}
        UNITS = [(k, a, b) for k in range(RHEADS) for a, b in (CUT3 if k in CUT_IN_THREE else CUT)]
        NU = len(UNITS)
        FIRST = 6
        HEAD_END = [max(i for i in range(NU) if UNITS[i][0] == k) + 1 for k in range(RHEADS)]
        ON_POOL = [int(step[6:]) for step in POOL_STEPS if step[:6] == "weigh:"]
        ON_DVE = [i for i in range(NU) if i not in ON_POOL]

        def weighs_before(T, unit, mine):
            return T * len(mine) + sum(i < unit for i in mine)

        kinds = {"turn_Z": "Z", "turn_kept": "kept", "scores": "sim", "fill_z": "z"}
        USES = [("product", 0) if step == "product:0" else (kinds[step.partition(":")[0]], int(step.partition(":")[2]))
                for step in PE_STEPS if step == "product:0" or step.partition(":")[0] in kinds]
        TILE = {"Z": -2, "kept": 1, "sim": 2, "z": 1, "product": -2}
        READ = {"Z": ("zT_ready", 4), "kept": ("keptT_ready", 2), "sim": ("sim_ready", 2),
                "z": ("z_ready", 4), "product": ("out_added", 1)}

        def bank(kind, j):
            return misc[USES.index((kind, j)) % 2]

        def bank_wait(pe, T, kind, j):
            i = USES.index((kind, j))
            t, last = T, i - 2
            while True:
                if last < 0:
                    t, last = t - 1, (len(USES) - 1 if i % 2 == 0 else len(USES) - 2)
                before, b = USES[last]
                tile = t + TILE[before]
                if not isinstance(t, int) or 0 <= tile < TILES:
                    break
                if t < -2:
                    return
                last -= 2
            name, each = READ[before]
            need(pe, S[name], tile * each + (b + 1) + (before == "product"))
            if before == "product" and not isinstance(t, int):
                before, b = USES[last - 2]
                name, each = READ[before]
                need(pe, S[name], (t + TILE[before]) * each + (b + 1))

        def pe_turn(pe, T, n, live, ahead, behind, scored):
            def sums(i):
                if not live:
                    return
                k, a, b = UNITS[i]
                need(pe, S["masked"], T * NU + (i - NR + 1))
                need(pe, S["keptT_ready"], T * 2 + (1 + k // 4))
                for c in range(a, b, 512):
                    e = min(c + 512, b)
                    nc.tensor.matmul(ring[i % NR][:, c - a:e - a], keptH[n][:, k, :], pairs[:, c:e],
                                     start=True, stop=False)
                    last = nc.tensor.matmul(ring[i % NR][:, c - a:e - a], keptL[n][:, k, :], pairs[:, c:e],
                                            start=False, stop=True)
                last.then_inc(S["filled"], 1)

            def turn_Z(g):
                if not behind:
                    return
                if g == 0:
                    need(pe, S["summed"], (T - 1) * (RHEADS - 1))
                bank_wait(pe, T, "Z", g)
                for q in range(4):
                    blk = 4 * g + q
                    w = min(P, COLS - blk * P)
                    last = nc.tensor.transpose(bank("Z", g)[0:w, q * P:(q + 1) * P],
                                               Z[n][:, blk * P:blk * P + w], M.ident[:, :])
                last.then_inc(S["z_turned"], 1)

            def turn_kept(m):
                if not ahead:
                    return
                need(pe, S["kept_ready"], T + 2)
                bank_wait(pe, T, "kept", m)
                for q in range(4):
                    k = 4 * m + q
                    last = nc.tensor.transpose(bank("kept", m)[0:2 * KEYS, q * P:(q + 1) * P],
                                               kept[:, 2 * k:2 * k + 2, :].rearrange("p a k -> p (a k)"),
                                               M.ident[:, :])
                last.then_inc(S["kept_turned"], 1)

            def scores(m):
                if not scored:
                    return
                need(pe, S["hs_ready"], T + 3)
                bank_wait(pe, T, "sim", m)
                nc.tensor.matmul(bank("sim", m)[:, 0:RHEADS * KEYS], hs[n][:, :],
                                 wk[:, m * RHEADS * KEYS:(m + 1) * RHEADS * KEYS],
                                 start=True, stop=True).then_inc(S["sim_product"], 1)

            def fill_z(j):
                if not ahead:
                    return
                bank_wait(pe, T, "z", j)
                a, b = QUARTER[j]
                nc.tensor.matmul(bank("z", j)[:, 0:b - a], hs[1 - n][:, :], down[:, a:b],
                                 start=True, stop=True).then_inc(S["z_filled"], 1)

            def product(part):
                if not behind:
                    return
                if part == 0:
                    need(pe, S["zT_ready"], (T - 2) * 4 + 4)
                    bank_wait(pe, T, "product", 0)
                for blk in range(part * EBLK // 4, (part + 1) * EBLK // 4):
                    w = min(P, COLS - blk * P)
                    last = nc.tensor.matmul(bank("product", 0)[:, 0:DM], ZT[0:w, blk, :], up[0:w, blk, :],
                                            start=(blk == 0), stop=(blk == EBLK - 1))
                if part == 3:
                    last.then_inc(S["out_product"], 1)

            take(PE_STEPS, dict(sums=sums, turn_Z=turn_Z, turn_kept=turn_kept, scores=scores, fill_z=fill_z,
                                product=product))

        def act_turn(act, T, n, live, last_silus, ahead, behind, scored):
            def exps(i):
                if not live:
                    return
                k, a, b = UNITS[i]
                if i == 0:
                    need(act, S["prep"], T + 1)
                need(act, S["filled"], T * NU + (i + 1))
                need(act, S["masked"], T * NU + (i + 1 - NE))
                nc.scalar.activation(ex[(n * NU + i) % NE][:, 0:b - a], ring[i % NR][:, 0:b - a], ACT.Exp,
                                     bias=shift[n][:, k:k + 1]).then_inc(S["ex_ready"], 1)

            def silus(k):
                t, b = (T, n) if k < FIRST else (T - 1, 1 - n)
                if not (live if k < FIRST else last_silus):
                    return
                need(act, S["total_ready"], t + 1)
                need(act, S["weighted"], weighs_before(t, HEAD_END[k], ON_DVE))
                need(act, S["pool_weighted"], weighs_before(t, HEAD_END[k], ON_POOL))
                nc.scalar.activation(u[:, k, :], u[:, k, :], ACT.Silu, scale=total[b][:, k:k + 1]
                                     ).then_inc(S["silu_ready"], 1)

            def copy_h():
                if not scored:
                    return
                nc.scalar.activation(hs[n][:, :], h[:, ds((T + 2) * P, P)], ACT.Copy).then_inc(S["hs_ready"], 1)

            def copy_Z(g):
                if not behind:
                    return
                need(act, S["z_turned"], (T - 2) * 4 + (g + 1))
                need(act, S["out_product"], T - 1)
                full = min(4, (COLS - 4 * g * P) // P)
                last = nc.scalar.activation(ZT[:, 4 * g:4 * g + full, :].rearrange("p a t -> p (a t)"),
                                            bank("Z", g)[:, 0:full * P], ACT.Copy)
                if full < 4:
                    w = COLS % P
                    last = nc.scalar.activation(ZT[0:w, 4 * g + full, :],
                                                bank("Z", g)[0:w, full * P:(full + 1) * P], ACT.Copy)
                last.then_inc(S["zT_ready"], 1)

            def copy_kept(m):
                if not ahead:
                    return
                need(act, S["kept_turned"], T * 2 + (3 + m))
                nc.scalar.activation(keptH[1 - n][:, 4 * m:4 * m + 4, :].rearrange("k h t -> k (h t)"),
                                     bank("kept", m)[0:2 * KEYS, :], ACT.Copy).then_inc(S["high_ready"], 1)

            def copy_scores(m):
                if not scored:
                    return
                need(act, S["sim_product"], T * 2 + (5 + m))
                need(act, S["kept_ready"], T + 2)
                nc.scalar.activation(sim[:, m * RHEADS:(m + 1) * RHEADS, :].rearrange("p a k -> p (a k)"),
                                     bank("sim", m)[:, 0:RHEADS * KEYS], ACT.Copy).then_inc(S["sim_ready"], 1)

            def copy_z(j):
                if not ahead:
                    return
                need(act, S["z_filled"], T * 4 + (5 + j))
                if j == 0:
                    need(act, S["weighted"], weighs_before(T, 0, ON_DVE))
                    need(act, S["pool_weighted"], weighs_before(T, 0, ON_POOL))
                a, b = QUARTER[j]
                nc.scalar.activation(z[1 - n][:, a:b], bank("z", j)[:, 0:b - a], ACT.Copy).then_inc(S["z_ready"], 1)

            def soften():
                if not ahead:
                    return
                need(act, S["soft_in"], T + 2)
                nc.scalar.activation(soft[:, :, :], soft[:, :, :], ACT.Exp).then_inc(S["soft_ready"], 1)

            take(ACT_STEPS, dict(copy_h=copy_h, exps=exps, silus=silus, copy_Z=copy_Z, copy_kept=copy_kept,
                                 copy_scores=copy_scores, copy_z=copy_z, soften=soften))

        CH = 9

        def dve_turn(dve, T, n, live, ahead, behind):
            def chain(c):
                return (T + 1) * CH + c

            def mask(i):
                if not live:
                    return
                k, a, b = UNITS[i]
                need(dve, S["ex_ready"], T * NU + (i + 1))
                if a == 0:
                    need(dve, S["summed"], (T - 1) * (RHEADS - 1) + max(k, 1))
                nc.vector.scalar_tensor_tensor(u[:, k, a:b], ring[i % NR][:, 0:b - a], thr[n][:, k:k + 1],
                                               ex[(n * NU + i) % NE][:, 0:b - a], ALU.is_ge, ALU.mult
                                               ).then_inc(S["masked"], 1)

            def weigh(i):
                if not live:
                    return
                k, a, b = UNITS[i]
                need(dve, S["z_ready"], T * 4 + 4)
                need(dve, S["masked"], T * NU + (i + 1))
                nc.vector.tensor_tensor(u[:, k, a:b], u[:, k, a:b], z[n][:, a:b], ALU.mult).then_inc(S["weighted"], 1)

            def top_eights():
                if not ahead:
                    return
                need_apart(dve, S["sim_ready"], T * 2 + 4, M.passed)
                for q in range(2 * RHEADS):
                    last = nc.vector.max(top[:, q, :], sim[:, q, :])
                last.then_inc(S["prep_step"], 1)

            def replace():
                if not ahead:
                    return
                need_apart(dve, S["prep_step"], chain(1), M.passed)
                for q in range(2 * RHEADS):
                    last = nc.vector.match_replace(out=left[:, q, :], in_to_replace=top[:, q, :],
                                                   in_values=sim[:, q, :], imm_value=REPLACED)
                last.then_inc(S["prep_step"], 1)

            def candidates():
                if not ahead:
                    return
                nc.vector.tensor_tensor(
                    cand[:, :, :, :],
                    top[:, :, :].rearrange("p (h a) k -> p h a k", a=2)[:, :, 0, :].unsqueeze(3)
                    .broadcast_to([P, RHEADS, K_HEAD, K_HEAD]),
                    top[:, :, :].rearrange("p (h a) k -> p h a k", a=2)[:, :, 1, :].unsqueeze(2)
                    .broadcast_to([P, RHEADS, K_HEAD, K_HEAD]), ALU.add).then_inc(S["cand_ready"], 1)
                need(dve, S["prep_step"], chain(2))
                nc.vector.tensor_tensor(left[:, :, :], left[:, :, :], sim[:, :, :], ALU.is_equal
                                        ).then_inc(S["prep_step"], 1)

            def keep():
                if not ahead:
                    return
                need(dve, S["prep_step"], chain(3))
                need(dve, S["kept_turned"], T * 2 + 2)
                nc.vector.scalar_tensor_tensor(kept[:, :, :], left[:, :, :], NEVER, sim[:, :, :],
                                               ALU.mult, ALU.add).then_inc(S["kept_ready"], 1)

            def bests():
                if not ahead:
                    return
                need_apart(dve, S["cand_ready"], T + 2, M.passed)
                for q in range(RHEADS):
                    last = nc.vector.max(best[:, q, :], cand[:, q, :, :].rearrange("p a b -> p (a b)"))
                last.then_inc(S["prep_step"], 1)

            def replace_bests():
                if not ahead:
                    return
                need_apart(dve, S["prep_step"], chain(4), M.passed)
                for q in range(RHEADS):
                    last = nc.vector.match_replace(out=cand[:, q, :, :].rearrange("p a b -> p (a b)"), in_to_replace=best[:, q, :],
                                                   in_values=cand[:, q, :, :].rearrange("p a b -> p (a b)"),
                                                   imm_value=REPLACED)
                last.then_inc(S["prep_step"], 1)
                nc.vector.tensor_scalar(shift[1 - n][:, :], best[:, :, 0], -1.0, None, ALU.mult
                                        ).then_inc(S["prep_step"], 1)

            def ninths():
                if not ahead:
                    return
                need_apart(dve, S["prep_step"], chain(5), M.passed)
                for q in range(RHEADS):
                    last = nc.vector.max(ninth[:, q, :], cand[:, q, :, :].rearrange("p a b -> p (a b)"))
                last.then_inc(S["prep_step"], 1)

            def thresholds():
                if not ahead:
                    return
                need(dve, S["prep_step"], chain(6))
                nc.vector.tensor_tensor(soft[:, :, :], best[:, :, :],
                                        shift[1 - n][:, :].unsqueeze(2).broadcast_to([P, RHEADS, 8]),
                                        ALU.add).then_inc(S["soft_in"], 1)
                need(dve, S["prep_step"], chain(7))
                nc.vector.tensor_tensor(thr[1 - n][:, :], best[:, :, K_HEAD - 1], ninth[:, :, 0], ALU.add
                                        ).then_inc(S["prep_step"], 1)
                need(dve, S["prep_step"], chain(8))
                nc.vector.tensor_scalar(thr[1 - n][:, :], thr[1 - n][:, :], 0.5, None, ALU.mult
                                        ).then_inc(S["prep"], 1)

            def totals():
                if not ahead:
                    return
                need(dve, S["soft_ready"], T + 2)
                need(dve, S["silu_ready"], T * RHEADS)
                nc.vector.tensor_reduce(total[1 - n][:, :], soft[:, :, :], AX.X, ALU.add).then_inc(S["prep_step"], 1)
                need(dve, S["prep_step"], chain(9))
                nc.vector.reciprocal(total[1 - n][:, :], total[1 - n][:, :]).then_inc(S["total_ready"], 1)

            def low_parts(m):
                if not ahead:
                    return
                need(dve, S["high_ready"], T * 2 + (3 + m))
                four = slice(4 * m, 4 * m + 4)
                nc.vector.tensor_tensor(keptL[1 - n][:, four, :],
                                        bank("kept", m)[0:2 * KEYS, :].rearrange("k (h t) -> k h t", h=4),
                                        keptH[1 - n][:, four, :].bitcast(FP32), ALU.subtract).then_inc(S["keptT_ready"], 1)

            def add_out():
                if not behind:
                    return
                need(dve, S["out_product"], T)
                x = M.x[:, ds(T - 2, 1), :]
                nc.vector.tensor_tensor(x, bank("product", 0)[:, 0:DM].unsqueeze(1), x, ALU.add
                                        ).then_inc(S["out_added"], 1)

            take(DVE_STEPS, dict(mask=mask, weigh=weigh, top_eights=top_eights, replace=replace,
                                 candidates=candidates, keep=keep, bests=bests, replace_bests=replace_bests,
                                 ninths=ninths, thresholds=thresholds, totals=totals, low_parts=low_parts,
                                 add_out=add_out))

        def pool_turn(pool, T, n, live, last_silus):
            def add(k):
                t, b = (T, n) if k < FIRST else (T - 1, 1 - n)
                if not (live if k < FIRST else last_silus):
                    return
                need(pool, S["silu_ready"], t * RHEADS + (k + 1))
                if k == 1:
                    need(pool, S["z_turned"], (t - 1) * 4)
                else:
                    need(pool, S["summed"], t * (RHEADS - 1) + (k - 1))
                nc.gpsimd.tensor_tensor(Z[b], u[:, 0, :] if k == 1 else Z[b], u[:, k, :], ALU.add
                                        ).then_inc(S["summed"], 1)

            def weigh(i):
                if not live:
                    return
                k, a, b = UNITS[i]
                need(pool, S["z_ready"], T * 4 + 4)
                need_apart(pool, S["masked"], T * NU + (i + 1), M.passed)
                nc.gpsimd.tensor_tensor(u[:, k, a:b], u[:, k, a:b], z[n][:, a:b], ALU.mult
                                        ).then_inc(S["pool_weighted"], 1)

            take(POOL_STEPS, dict(add=add, weigh=weigh))

        def turns(eng, turn):
            for T in (-2, -1, 0, 1):
                turn(T, T % 2, T >= 0, T >= 1, T >= -1, False, True)
            with eng.Fori(0, (TILES - 4) // 2) as i:
                for n in range(2):
                    turn(i * 2 + (2 + n), n, True, True, True, True, True)
            for T in range(TILES - 2, TILES + 2):
                turn(T, T % 2, T < TILES, T <= TILES, T < TILES - 1, True, False)

        with nc.Block() as block:
            @block.sync
            def _(sp):
                sp.dma_start(down[:, :], D["down"]).then_inc(S["loaded"], 16)
                sp.dma_start(u[0:2 * KEYS, 0, :], D["pairs"]).then_inc(S["loaded"], 16)
                sp.dma_start(up[:, 0:EBLK - 1, :],
                             D["up"][0:(EBLK - 1) * P, :].rearrange("(a p) d -> p a d", p=P)).then_inc(S["loaded"], 16)
                sp.dma_start(up[0:COLS % P, EBLK - 1, :], D["up"][(EBLK - 1) * P:COLS, :]).then_inc(S["loaded"], 16)

            @block.tensor
            def _(pe):
                pe.wait_ge(S["loaded"], 64)
                pe.wait_ge(S["pairs_ready"], 1)
                pe.sem_inc(S["out_product"], 1)
                turns(pe, lambda T, n, live, last, ahead, behind, scored: pe_turn(pe, T, n, live, ahead, behind, scored))

            @block.scalar
            def _(act):
                turns(act, lambda T, n, live, last, ahead, behind, scored: act_turn(act, T, n, live, last, ahead, behind, scored))

            @block.vector
            def _(dve):
                dve.wait_ge(S["loaded"], 64)
                nc.vector.tensor_copy(pairs[:, :], u[0:2 * KEYS, 0, :]).then_inc(S["pairs_ready"], 1)
                dve.sem_inc(S["out_added"], 1)
                turns(dve, lambda T, n, live, last, ahead, behind, scored: dve_turn(dve, T, n, live, ahead, behind))

            @block.gpsimd
            def _(pool):
                turns(pool, lambda T, n, live, last, ahead, behind, scored: pool_turn(pool, T, n, live, last))


class Memory:
    pass


def build(nc, D):
    M = Memory()
    M.norms = 0
    with scope(nc, "all") as s:
        M.xT, M.xL = s.sb_both("xT", [P, KD, TOKENS])
        M.x, xH = s.sb_both("x", [P, TILES, DM])
        M.xH = xH[:, :, :].rearrange("p n d -> p (n d)").rearrange("p (k t) -> p k t", k=KD)
        M.ident = s.sb("ident", [P, P])
        M.passed = s.sem("passed")
        M.norm_sems = {n: s.sem(f"norm_{n}") for n in NORM_SEMS}
        M.stored = s.sem("stored")
        M.ident16 = s.sb("ident16", [P, P], BF16)
        M.ones = s.sb("ones", [P, P])
        load_phase(nc, M, D)
        with scope(nc, "g") as g:
            G = g.sb("gated", [P, PAIRS, TOKENS])
            squares_sum = g.sb("squares_sum", [P, TOKENS])
            gate_phase(nc, M, D, G)
            attention_phase(nc, M, D, G, squares_sum)
            projection_phase(nc, M, D, G, squares_sum)
        layernorm_phase(nc, M)
        experts_phase(nc, M, D)
        layernorm_phase(nc, M)
        scan_phase(nc, M, D)
        layernorm_phase(nc, M)
        retrieval_phase(nc, M, D)
        layernorm_phase(nc, M, D["out"])


def kernel(**inputs):
    import numpy as np
    import concourse.bacc as bacc
    from concourse.bass_utils import run_bass_kernel_spmd as run

    I = {k: np.asarray(v) for k, v in inputs.items()}
    x = I["L0_attn_hidden_states"].reshape(TOKENS, DM)
    qkv = I["L0_attn_qkv_w"].reshape(PAIRS, 2, 3, HD, DM)
    qkv = qkv.transpose(0, 4, 2, 1, 3).reshape(PAIRS, KD, P, 3 * P).transpose(0, 2, 1, 3)
    gate = I["L0_attn_gate_w"].reshape(PAIRS, P, KD, P).transpose(0, 3, 2, 1)
    A = dict(
        x=x, xT=x.T,
        qkv_w=np.pad(qkv.reshape(PAIRS, P, KD * 3 * P), ((0, 1), (0, 0), (0, 0))),
        gate_w=gate.reshape(PAIRS, P, KD * P),
        norm_w=np.pad(I["L0_attn_norm_w"].reshape(PAIRS, P, 1), ((0, 1), (0, 0), (0, 0))),
        decay=np.pad(decay_table(), ((0, 1), (0, 0), (0, 0))),
        out_w=I["L0_attn_out_w"].T,
    )
    wq = I["L1_ffn_W_q"].reshape(2, RHEADS, KHD, PRIV)
    pad_experts = lambda a: np.pad(a[:PAIRED], ((0, COLS - PAIRED), (0, 0)))
    keys = I["L1_ffn_keys"]
    A.update(
        w_up=I["L1_ffn_W_up"].T, b_up=I["L1_ffn_b_up"].reshape(-1, P).T,
        w_down=I["L1_ffn_W_down"].T, b_down=I["L1_ffn_b_down"][:, None],
        w_q=wq.transpose(2, 1, 0, 3).reshape(KHD, 2 * RHEADS, PRIV),
        keys=keys.transpose(3, 0, 2, 1).reshape(KHD, 2 * RHEADS, KEYS),
        down=pad_experts(I["L1_ffn_down_embed"]).T, up=pad_experts(I["L1_ffn_up_embed"]),
        pairs=pair_rows(),
    )
    pad = FTILES * P - EXPERTS * FF

    def hidden_rows(routed, shared, axis):
        a = np.concatenate([routed, shared], 0)
        a = a.transpose(1, 0, 2).reshape(DM, EXPERTS * FF) if axis == 1 else a.reshape(EXPERTS * FF, -1)
        return np.pad(a, ((0, 0), (0, pad)) if axis == 1 else ((0, pad), (0, 0)))

    second = hidden_rows(I["L0_ffn_routed_w2"], I["L0_ffn_shared_w2"], 0)
    second[EXPERTS * FF:EXPERTS * (FF + 1)] = np.concatenate([I["L0_ffn_routed_b2"], I["L0_ffn_shared_b2"]], 0)
    first_bias = hidden_rows(I["L0_ffn_routed_b1"], I["L0_ffn_shared_b1"], 0)
    first_bias[EXPERTS * FF:EXPERTS * (FF + 1)] = 1.0
    A.update(
        centroids=I["L0_ffn_centroids"].T, route_bias=I["L0_ffn_bias"],
        w1=hidden_rows(I["L0_ffn_routed_w1"], I["L0_ffn_shared_w1"], 1),
        w2=second, b1=first_bias.reshape(FTILES, P).T,
        expert_rows=expert_rows(),
    )
    wx, bx = I["L1_attn_W_xproj"].T, I["L1_attn_b_xproj"][:, None]
    A.update(
        wx=np.concatenate([wx[:, :DT_RANK]] + [wx[:, DT_RANK:]] * PARTS, 1),
        bx=np.concatenate([bx[:DT_RANK]] + [bx[DT_RANK:]] * PARTS, 0),
        wdt=I["L1_attn_W_dt"].T, bdt=I["L1_attn_b_dt"].reshape(KD, P).T,
        a_log=I["L1_attn_A_log"].reshape(KD, P, STATES).transpose(1, 0, 2),
        state_rows=state_rows(),
    )
    nc = bacc.Bacc("TRN2", target_bir_lowering=False, num_devices=1)
    D, arrays = {}, {}
    for name, a in A.items():
        a = np.ascontiguousarray(a)
        arrays[f"in_{name}_dram"] = a
        D[name] = nc.dram_tensor(f"in_{name}_dram", a.shape, mybir.dt.from_np(a.dtype),
                                 kind="ExternalInput").ap()
    D["out"] = nc.dram_tensor("out_0_dram", (BATCH, SEQ, DM), FP32, kind="ExternalOutput").ap()
    build(nc, D)
    r = run(nc, [arrays], core_ids=[0])
    return r.results[0]["out_0_dram"]
```

```python
import concourse.bass as bass
from concourse import mybir
from contextlib import ExitStack, contextmanager

FP32 = mybir.dt.float32
FP32R = mybir.dt.float32r
BF16 = mybir.dt.bfloat16
ALU = mybir.AluOpType
ACT = mybir.ActivationFunctionType
AX = mybir.AxisListType
ds = bass.ds

P = 128
BATCH, SEQ, DM = 4, 512, 256
TOKENS = BATCH * SEQ
TILES = TOKENS // P
BLK = 512
NBLK = TOKENS // BLK
KD = DM // P
LN_EPS = 1e-5
ONE_BITS = 0x3F80


def wait_apart(eng, sem, value, passed):
    eng.wait_ge(sem, value)
    eng.sem_inc(passed, 1)


def need(eng, sem, value):
    if not (isinstance(value, int) and value <= 0):
        eng.wait_ge(sem, value)


def need_apart(eng, sem, value, passed):
    if isinstance(value, int):
        need(eng, sem, value)
    else:
        wait_apart(eng, sem, value, passed)


class Scope:

    def __init__(self, nc, prefix, ctx):
        self.nc, self.prefix, self.ctx = nc, prefix, ctx

    def sb(self, name, shape, dt=FP32):
        return self.ctx.enter_context(self.nc.sbuf_tensor(f"{self.prefix}_sb_{name}", shape, dt))

    def sb_both(self, name, shape):
        start = self.nc.sbuf_base
        whole = self.sb(name, shape)
        end = self.nc.sbuf_base
        self.ctx.callback(self.set_base, end)
        self.set_base(start)
        part = self.sb(f"{name}_part", shape, FP32R)
        assert self.nc.sbuf_base == end
        return whole, part

    def set_base(self, base):
        self.nc.sbuf_base = base

    def ps(self, name, shape=(P, 512), dt=FP32):
        return self.ctx.enter_context(self.nc.psum_tensor(f"{self.prefix}_ps_{name}", list(shape), dt))

    def sem(self, name):
        return self.ctx.enter_context(self.nc.semaphore(f"{self.prefix}_{name}"))


@contextmanager
def scope(nc, prefix):
    with ExitStack() as ctx:
        yield Scope(nc, prefix, ctx)


def load_phase(nc, M, D):
    with scope(nc, "ld") as s:
        loaded = s.sem("loaded")
        zeroed = s.sem("zeroed")
        with nc.Block() as block:
            @block.sync
            def _(sp):
                sp.dma_start(M.xT[:, :, :], D["xT"].rearrange("(k p) t -> p k t", p=P)).then_inc(loaded, 16)
                sp.wait_ge(loaded, 16)

            @block.gpsimd
            def _(pool):
                nc.gpsimd.memset(M.ident[:, :], 0.0).then_inc(zeroed, 1)
                nc.gpsimd.memset(M.ones[:, :], 1.0)
                nc.gpsimd.memset(M.ident16[:, :], 0.0).then_inc(zeroed, 1)
                pool.wait_ge(zeroed, 2)
                nc.gpsimd.affine_select(out=M.ident16[:, :], in_=M.ident16[:, :], compare_op=ALU.not_equal,
                                        fill=1.0, base=0, pattern=[[-1, P]], channel_multiplier=1)
                nc.gpsimd.affine_select(out=M.ident[:, :], in_=M.ident[:, :], compare_op=ALU.not_equal,
                                        fill=1.0, base=0, pattern=[[-1, P]],
                                        channel_multiplier=1).then_inc(zeroed, 1)


HEADS, HD = 32, 64
FEAT = HEADS * HD
PAIRS = HEADS // 2
CHUNKS = SEQ // P
HALVES = 2
UNITS = HALVES * BATCH
TURNS = PAIRS // HALVES


def gate_phase(nc, M, D, G):
    with scope(nc, "gt") as s:
        w = [s.sb(f"w{j}", [P, KD, P]) for j in range(HALVES)]
        wH = [s.sb(f"wH{j}", [P, KD, P], FP32R) for j in range(HALVES)]
        wL = [s.sb(f"wL{j}", [P, KD, P], FP32R) for j in range(HALVES)]
        bank = [s.ps(f"bank{n}") for n in range(4)]
        w_loaded = [s.sem(f"w_loaded{j}") for j in range(HALVES)]
        x_high, x_low = s.sem("x_high"), s.sem("x_low")
        w_high, w_low = s.sem("w_high"), s.sem("w_low")
        product = s.sem("product")
        gate = s.sem("gate")

        def done(i, k):
            return i * UNITS + (UNITS + k + 1)

        with nc.Block() as block:
            @block.sync
            def _(sp):
                sp.sem_inc(w_low, HALVES)
                with sp.Fori(0, TURNS) as i:
                    for j in range(HALVES):
                        sp.wait_ge(w_low, i * HALVES + j + 1)
                        sp.dma_start(w[j][:, :, :],
                                     D["gate_w"][ds(i * HALVES + j, 1), :, :].rearrange("o p (k f) -> p (o k) f", k=KD)
                                     ).then_inc(w_loaded[j], 16)

            @block.gpsimd
            def _(pool):
                with pool.Fori(0, TURNS) as i:
                    for j in range(HALVES):
                        pool.wait_ge(w_loaded[j], i * 16 + 16)
                        wait_apart(pool, product, done(i, BATCH * (j + 1) - 1 - UNITS), M.passed)
                        nc.gpsimd.tensor_copy(wH[j][:, :, :], w[j][:, :, :]).then_inc(w_high, 1)
                        wait_apart(pool, w_high, i * HALVES + j + 1, M.passed)
                        nc.gpsimd.tensor_tensor(wL[j][:, :, :], w[j][:, :, :], wH[j][:, :, :].bitcast(FP32),
                                                ALU.subtract).then_inc(w_low, 1)

            @block.vector
            def _(dve):
                for b in range(BATCH):
                    t = slice(b * BLK, (b + 1) * BLK)
                    dve.wait_ge(x_high, b + 1)
                    nc.vector.tensor_tensor(M.xL[:, :, t], M.xT[:, :, t], M.xH[:, :, t].bitcast(FP32),
                                            ALU.subtract).then_inc(x_low, 1)

            @block.tensor
            def _(pe):
                pe.sem_inc(product, UNITS)
                with pe.Fori(0, TURNS) as i:
                    for j in range(HALVES):
                        pe.wait_ge(w_low, i * HALVES + (HALVES + j + 1))
                        for b in range(BATCH):
                            k = j * BATCH + b
                            t = slice(b * BLK, (b + 1) * BLK)
                            pe.wait_ge(x_low, b + 1)
                            pe.wait_ge(gate, done(i, k - 4))
                            for c in range(KD):
                                nc.tensor.matmul(bank[k % 4][:, :], wH[j][:, c, :], M.xH[:, c, t],
                                                 start=(c == 0), stop=False)
                                nc.tensor.matmul(bank[k % 4][:, :], wH[j][:, c, :], M.xL[:, c, t],
                                                 start=False, stop=False)
                                last = nc.tensor.matmul(bank[k % 4][:, :], wL[j][:, c, :], M.xH[:, c, t],
                                                        start=False, stop=(c == KD - 1))
                            last.then_inc(product, 1)

            @block.scalar
            def _(act):
                for b in range(BATCH):
                    t = slice(b * BLK, (b + 1) * BLK)
                    nc.scalar.activation(M.xH[:, :, t], M.xT[:, :, t], ACT.Copy).then_inc(x_high, 1)
                act.sem_inc(gate, UNITS)
                with act.Fori(0, TURNS) as i:
                    for j in range(HALVES):
                        for b in range(BATCH):
                            k = j * BATCH + b
                            act.wait_ge(product, done(i, k))
                            nc.scalar.activation(G[:, ds(i * HALVES + j, 1), b * BLK:(b + 1) * BLK],
                                                 bank[k % 4][:, :].unsqueeze(1), ACT.Sigmoid).then_inc(gate, 1)


TBL = 2 * P + P + 2 + 1


def decay_table():
    import numpy as np
    base = 1.0 / 2.0 ** (8.0 / HEADS)
    slope = base ** (np.arange(HEADS) + 1.0) * (1.0 + 1e-5)
    r = np.arange(P, dtype=np.float64)
    t = np.zeros((PAIRS, P, TBL))
    for a in range(PAIRS):
        for h in range(2):
            m = slope[2 * a + h]
            dist = r[None, :] - r[:, None]
            t[a, :, h * P:(h + 1) * P] = np.where(dist >= 0, np.exp(-m * np.maximum(dist, 0)), 0.0)
            t[a, h * HD:(h + 1) * HD, 2 * P:3 * P] = np.exp(-m * (r + 1))[None, :]
            t[a, :, 3 * P + h] = np.exp(-m * (P - 1 - r))
            t[a, h * HD:(h + 1) * HD, 3 * P + 2] = np.exp(-m * P)
    return t.astype(np.float32)


def attention_phase(nc, M, D, G, squares_sum):
    with scope(nc, "at") as s:
        w, wL = zip(*(s.sb_both(f"w{j}", [P, KD, 3 * P]) for j in range(HALVES)))
        wH = [s.sb(f"wH{j}", [P, KD, 4 * P], FP32R) for j in range(HALVES)]
        tbl = [s.sb(f"tbl{j}", [P, TBL]) for j in range(HALVES)]
        nw = [s.sb(f"nw{j}", [P, 1]) for j in range(HALVES)]
        qT = [s.sb(f"qT{n}", [P, BLK]) for n in range(2)]
        kT = [s.sb(f"kT{n}", [P, BLK]) for n in range(2)]
        v = [s.sb(f"v{n}", [P, CHUNKS, P]) for n in range(2)]
        q_decayed = s.sb("q_decayed", [P, CHUNKS - 1, P])
        k_decayed = s.sb("k_decayed", [P, CHUNKS - 1, P])
        weights = s.sb("weights", [P, 2, BLK])
        state = s.sb("state", [P, CHUNKS - 1, P])

        ps_q, ps_k, ps_v, ps_kt = s.ps("q"), s.ps("k"), s.ps("v"), s.ps("kt")
        ps_score = [s.ps(f"score{h}") for h in range(2)]
        ps_out, ps_state = s.ps("out"), s.ps("state_sum")

        w_loaded = [s.sem(f"w_loaded{j}") for j in range(HALVES)]
        w_high, w_low = s.sem("w_high"), s.sem("w_low")
        q_product, k_product, v_product = s.sem("q_product"), s.sem("k_product"), s.sem("v_product")
        q_ready, k_ready, v_ready = s.sem("q_ready"), s.sem("k_ready"), s.sem("v_ready")
        v_copied, v_summed = s.sem("v_copied"), s.sem("v_summed")
        k_turned = s.sem("k_turned")
        k_decay_ready = s.sem("k_decay_ready")
        q_decay_ready = s.sem("q_decay_ready")
        scores = s.sem("scores")
        weights_ready = s.sem("weights_ready")
        state_product = s.sem("state_product")
        state_step = s.sem("state_step")
        attended = s.sem("attended")
        squared = s.sem("squared")
        gated = s.sem("gated")
        summed = s.sem("summed")
        zeroed = s.sem("zeroed")

        def done(i, k, n=1):
            return (i * UNITS + (UNITS + k + 1)) * n

        with nc.Block() as block:
            @block.sync
            def _(sp):
                def load(j, a):
                    for to, name in ((w[j][:, :, :], "qkv_w"), (tbl[j][:, :], "decay"), (nw[j][:, :], "norm_w")):
                        of = D[name][ds(a, 1), :, :]
                        of = of.rearrange("o p (k f) -> p (o k) f", k=KD) if name == "qkv_w" else of.rearrange(
                            "o p f -> (o p) f")
                        sp.dma_start(to, of).then_inc(w_loaded[j], 16)

                load(0, 0)
                with sp.Fori(0, TURNS) as i:
                    sp.wait_ge(gated, done(i, -1))
                    load(1, i * HALVES + 1)
                    sp.wait_ge(gated, done(i, BATCH - 1))
                    load(0, i * HALVES + 2)

            def project_v(pe, i, k, half):
                j, b = k // BATCH, k % BATCH
                pe.wait_ge(v_summed, done(i, k - 1, 2) + half)
                for t in range(2):
                    start = b * BLK + (2 * half + t) * P
                    for c in range(KD):
                        nc.tensor.matmul(ps_v[:, 2 * t * P:2 * (t + 1) * P], M.xH[:, c, start:start + P],
                                         wH[j][:, c, 2 * P:4 * P], start=(c == 0), stop=False, skip_group_check=True)
                        last = nc.tensor.matmul(ps_v[:, 2 * t * P:(2 * t + 1) * P], M.xL[:, c, start:start + P],
                                                wH[j][:, c, 2 * P:3 * P], start=False, stop=(c == KD - 1),
                                                skip_group_check=True)
                last.then_inc(v_product, 1)

            def project(pe, i, k):
                j, b, n = k // BATCH, k % BATCH, k % 2
                if b == 0:
                    pe.wait_ge(w_low, i * HALVES + j + 1)
                project_v(pe, i, k, 0)
                for ready, bank, done_sem, col in ((k_ready, ps_k, k_product, P), (q_ready, ps_q, q_product, 0)):
                    pe.wait_ge(ready, done(i, k - 1))
                    t = slice(b * BLK, (b + 1) * BLK)
                    for c in range(KD):
                        nc.tensor.matmul(bank[:, :], wH[j][:, c, col:col + P], M.xH[:, c, t], start=(c == 0), stop=False)
                        nc.tensor.matmul(bank[:, :], wH[j][:, c, col:col + P], M.xL[:, c, t], start=False, stop=False)
                        last = nc.tensor.matmul(bank[:, :], wL[j][:, c, col:col + P], M.xH[:, c, t],
                                                start=False, stop=(c == KD - 1))
                    last.then_inc(done_sem, 1)
                project_v(pe, i, k, 1)

            @block.tensor
            def _(pe):
                pe.wait_ge(zeroed, 1)
                with pe.Fori(0, TURNS) as i:
                    project(pe, i, 0)
                    for k in range(UNITS):
                        n = k % 2
                        pe.wait_ge(k_ready, done(i, k))
                        pe.wait_ge(k_decay_ready, done(i, k - 1))
                        for t in range(CHUNKS - 1):
                            last = nc.tensor.transpose(ps_kt[:, t * P:(t + 1) * P], kT[n][:, t * P:(t + 1) * P],
                                                       M.ident[:, :])
                        last.then_inc(k_turned, 1)
                        pe.wait_ge(q_ready, done(i, k))
                        pe.wait_ge(weights_ready, done(i, k - 1, 2))
                        for t in range(CHUNKS):
                            for h in range(2):
                                r = slice(h * HD, (h + 1) * HD)
                                last = nc.tensor.matmul(ps_score[h][:, t * P:(t + 1) * P],
                                                        kT[n][r, t * P:(t + 1) * P], qT[n][r, t * P:(t + 1) * P],
                                                        start=True, stop=True)
                        last.then_inc(scores, 1)
                        if k + 1 < UNITS:
                            project(pe, i, k + 1)
                        pe.wait_ge(k_decay_ready, done(i, k))
                        pe.wait_ge(v_ready, done(i, k))
                        pe.wait_ge(state_step, done(i, k - 1, CHUNKS - 1))
                        for t in range(CHUNKS - 1):
                            for h in range(2):
                                r = slice(h * HD, (h + 1) * HD)
                                last = nc.tensor.matmul(ps_state[r, t * P + h * HD:t * P + (h + 1) * HD],
                                                        k_decayed[:, t, r], v[n][:, t, r], start=True, stop=True)
                        last.then_inc(state_product, 1)
                        pe.wait_ge(weights_ready, done(i, k, 2))
                        pe.wait_ge(gated, done(i, k - 1))
                        for t in range(CHUNKS):
                            for h in range(2):
                                r = slice(h * HD, (h + 1) * HD)
                                last = nc.tensor.matmul(ps_out[r, t * P:(t + 1) * P], v[n][:, t, r],
                                                        weights[:, h, t * P:(t + 1) * P], start=(t == 0),
                                                        stop=(t == 0), skip_group_check=True)
                        pe.wait_ge(q_decay_ready, done(i, k))
                        for t in range(1, CHUNKS):
                            pe.wait_ge(state_step, done(i, k - 1, CHUNKS - 1) + t)
                            last = nc.tensor.matmul(ps_out[:, t * P:(t + 1) * P], state[:, t - 1, :],
                                                    q_decayed[:, t - 1, :], start=False, stop=True,
                                                    skip_group_check=True)
                        last.then_inc(attended, 1)

            @block.scalar
            def _(act):
                for sem in (q_ready, k_ready, v_ready, squared):
                    act.sem_inc(sem, UNITS)

                def evacuate(i, k):
                    n = k % 2
                    act.wait_ge(k_product, done(i, k) - UNITS)
                    act.wait_ge(attended, done(i, k - 2))
                    nc.scalar.activation(kT[n][:, :], ps_k[:, :], ACT.Silu).then_inc(k_ready, 1)
                    act.wait_ge(q_product, done(i, k) - UNITS)
                    act.wait_ge(summed, done(i, k - 2))
                    nc.scalar.activation(qT[n][:, :], ps_q[:, :], ACT.Silu).then_inc(q_ready, 1)
                    act.wait_ge(v_summed, done(i, k, 2))
                    values = v[n][:, :, :].rearrange("p a b -> p (a b)")
                    nc.scalar.activation(values, values, ACT.Silu).then_inc(v_ready, 1)

                with act.Fori(0, TURNS) as i:
                    evacuate(i, 0)
                    for k in range(UNITS):
                        if k + 1 < UNITS:
                            evacuate(i, k + 1)
                        act.wait_ge(attended, done(i, k))
                        nc.scalar.activation(qT[k % 2][:, :], ps_out[:, :], ACT.Square).then_inc(squared, 1)

            @block.vector
            def _(dve):
                nc.vector.memset(ps_state[:, :], 0.0).then_inc(zeroed, 1)
                dve.sem_inc(k_decay_ready, UNITS)
                dve.sem_inc(weights_ready, 2 * UNITS)
                dve.sem_inc(state_step, (CHUNKS - 1) * UNITS)
                dve.sem_inc(gated, UNITS)
                dve.sem_inc(v_summed, 2 * UNITS)

                def sum_v(i, k):
                    dve.wait_ge(attended, done(i, k - 2))
                    for half in range(2):
                        dve.wait_ge(v_product, done(i, k, 2) - 2 * UNITS - 1 + half)
                        parts = ps_v[:, :].rearrange("p (t a f) -> p t a f", t=2, a=2)
                        nc.vector.tensor_copy(v[k % 2][:, 2 * half:2 * half + 2, :], parts[:, :, 0, :]
                                              ).then_inc(v_copied, 1)
                        dve.wait_ge(v_copied, done(i, k, 2) - 2 * UNITS - 1 + half)
                        nc.vector.tensor_tensor(v[k % 2][:, 2 * half:2 * half + 2, :],
                                                v[k % 2][:, 2 * half:2 * half + 2, :], parts[:, :, 1, :],
                                                ALU.add).then_inc(v_summed, 1)

                with dve.Fori(0, TURNS) as i:
                    sum_v(i, 0)
                    for k in range(UNITS):
                        j, b = k // BATCH, k % BATCH
                        t_ = tbl[j]
                        if b == 0:
                            dve.wait_ge(w_loaded[j], i * 48 + 48)
                        dve.wait_ge(k_turned, done(i, k) - UNITS)
                        nc.vector.tensor_tensor(
                            k_decayed[:, :, :].rearrange("p t (h e) -> p t h e", h=2),
                            ps_kt[:, 0:(CHUNKS - 1) * P].rearrange("p (t h e) -> p t h e", t=CHUNKS - 1, h=2),
                            t_[:, 3 * P:3 * P + 2].unsqueeze(1).unsqueeze(3).broadcast_to([P, CHUNKS - 1, 2, HD]),
                            ALU.mult).then_inc(k_decay_ready, 1)
                        dve.wait_ge(scores, done(i, k) - UNITS)
                        dve.wait_ge(attended, done(i, k - 1))
                        for h in range(2):
                            nc.vector.tensor_tensor(
                                weights[:, h, :].rearrange("p (t q) -> p t q", t=CHUNKS),
                                ps_score[h][:, :].rearrange("p (t q) -> p t q", t=CHUNKS),
                                t_[:, h * P:(h + 1) * P].unsqueeze(1).broadcast_to([P, CHUNKS, P]),
                                ALU.mult).then_inc(weights_ready, 1)
                        if k + 1 < UNITS:
                            sum_v(i, k + 1)
                        dve.wait_ge(state_product, done(i, k) - UNITS)
                        nc.vector.tensor_copy(state[:, 0, :], ps_state[:, 0:P]).then_inc(state_step, 1)
                        for t in range(1, CHUNKS - 1):
                            dve.wait_ge(state_step, done(i, k - 1, CHUNKS - 1) + t)
                            nc.vector.scalar_tensor_tensor(state[:, t, :], state[:, t - 1, :],
                                                           t_[:, 3 * P + 2:3 * P + 3],
                                                           ps_state[:, t * P:(t + 1) * P],
                                                           ALU.mult, ALU.add).then_inc(state_step, 1)
                        dve.wait_ge(squared, done(i, k))
                        g = G[:, ds(i * HALVES + j, 1), b * BLK:(b + 1) * BLK]
                        nc.vector.scalar_tensor_tensor(g, ps_out[:, :].unsqueeze(1), nw[j][:, 0:1], g,
                                                       ALU.mult, ALU.mult).then_inc(gated, 1)

            @block.gpsimd
            def _(pool):
                nc.gpsimd.memset(squares_sum[:, :], 0.0).then_inc(summed, 1)
                pool.wait_ge(summed, 1)
                pool.sem_inc(summed, UNITS - 1)
                pool.sem_inc(q_decay_ready, UNITS)
                pool.sem_inc(attended, UNITS)

                def cut(j, loads, pair):
                    need_apart(pool, w_loaded[j], loads * 48, M.passed)
                    nc.gpsimd.tensor_copy(wH[j][:, :, 0:3 * P], w[j][:, :, :]).then_inc(w_high, 1)
                    need_apart(pool, w_high, pair + 1, M.passed)
                    for to, of in ((wH[j][:, :, 3 * P:4 * P], slice(2 * P, 3 * P)), (wL[j][:, :, 0:2 * P], slice(0, 2 * P))):
                        last = nc.gpsimd.tensor_tensor(to, w[j][:, :, of], wH[j][:, :, of].bitcast(FP32), ALU.subtract)
                    last.then_inc(w_low, 1)

                cut(0, 1, 0)
                with pool.Fori(0, TURNS) as i:
                    for k in range(UNITS):
                        if k % BATCH == 2:
                            j = 1 - k // BATCH
                            cut(j, i + 2 - j, i * HALVES + k // BATCH + 1)
                        j, b, n = k // BATCH, k % BATCH, k % 2
                        if b == 0:
                            pool.wait_ge(w_loaded[j], i * 48 + 48)
                        pool.wait_ge(q_ready, done(i, k))
                        pool.wait_ge(attended, done(i, k - 1))
                        nc.gpsimd.tensor_tensor(q_decayed[:, :, :],
                                                qT[n][:, P:BLK].rearrange("p (t q) -> p t q", t=CHUNKS - 1),
                                                tbl[j][:, 2 * P:3 * P].unsqueeze(1).broadcast_to([P, CHUNKS - 1, P]),
                                                ALU.mult).then_inc(q_decay_ready, 1)
                        pool.wait_ge(squared, done(i, k))
                        part = squares_sum[:, b * BLK:(b + 1) * BLK]
                        nc.gpsimd.tensor_tensor(part, part, qT[n][:, :], ALU.add).then_inc(summed, 1)


class Residual:

    TPB = BLK // P

    def __init__(self, nc, M, s, residual):
        self.nc, self.M, self.residual = nc, M, residual
        self.y = s.sb("branch", [P, KD, BLK])
        self.bank = [s.ps(f"turned{n}") for n in range(KD)]
        self.turned = s.sem("turned")
        self.added = s.sem("added")

    def tensor(self, pe, i, y_sem, y_value, y=None):
        y = self.y if y is None else y
        nc = self.nc
        pe.wait_ge(y_sem, y_value)
        pe.wait_ge(self.added, i * KD + KD)
        for t in range(self.TPB):
            for c in range(KD):
                last = nc.tensor.transpose(self.bank[t // 2][:, (t % 2) * DM + c * P:(t % 2) * DM + (c + 1) * P],
                                           y[:, c, t * P:(t + 1) * P], self.M.ident[:, :])
            if t % 2:
                last.then_inc(self.turned, 1)

    def vector(self, dve, i, stats=True):
        for h in range(KD):
            x = self.M.x[:, ds(i * self.TPB + 2 * h, 2), :]
            dve.wait_ge(self.turned, i * KD + h + 1)
            self.nc.vector.scalar_tensor_tensor(x, x, float(self.residual),
                                                self.bank[h][:, :].rearrange("p (t d) -> p t d", t=2),
                                                ALU.mult, ALU.add).then_inc(self.added, 1)
        if not stats:
            return
        wait_apart(dve, self.added, i * KD + 2 * KD, self.M.passed)
        for t in range(self.TPB):
            n = ds(i * self.TPB + t, 1)
            self.nc.vector.bn_stats(self.M.stats[:, n, :].rearrange("p o s -> p (o s)"),
                                    self.M.x[:, n, :].rearrange("p o d -> p (o d)")
                                    ).then_inc(self.M.norm_sems["stat"], 1)


NORM_SEMS = ("stat", "aggregate", "spread", "root", "scale", "normed", "turned")


def layernorm_phase(nc, M, out=None, stats_ready=True):
    GROUP = 4
    GROUPS = TILES // GROUP
    with scope(nc, f"ln{M.norms}") as s:
        before_t, before_g = M.norms * TILES, M.norms * GROUPS
        M.norms += 1
        mv = s.sb("mv", [P, TILES, 2])
        var = s.sb("var", [P, TILES])
        rstd = s.sb("rstd", [P, TILES])
        banks = [s.ps(f"bank{n}") for n in range(8)]
        stat, aggregate, spread, root, scale, normed, turned = (M.norm_sems[n] for n in NORM_SEMS)

        def tiles(g):
            return range(g * GROUP, (g + 1) * GROUP)

        def part(g):
            return slice(g * GROUP, (g + 1) * GROUP)

        with nc.Block() as block:
            @block.vector
            def _(dve):
                def spreads(g):
                    if not stats_ready:
                        for t in tiles(g):
                            nc.vector.bn_stats(M.stats[:, t, :], M.x[:, t, :]).then_inc(stat, 1)
                    for t in tiles(g):
                        dve.wait_ge(stat, before_t + t + 1)
                        nc.vector.bn_aggr(mv[:, t, :], M.stats[:, t, :]).then_inc(aggregate, 1)
                    dve.wait_ge(aggregate, before_t + (g + 1) * GROUP)
                    nc.vector.tensor_scalar(var[:, part(g)], mv[:, part(g), 1], LN_EPS, None, ALU.add
                                            ).then_inc(spread, 1)

                def normalize(g):
                    dve.wait_ge(root, before_g + g + 1)
                    nc.vector.reciprocal(rstd[:, part(g)], rstd[:, part(g)]).then_inc(scale, 1)
                    dve.wait_ge(scale, before_g + g + 1)
                    for t in tiles(g):
                        nc.vector.tensor_scalar(M.x[:, t, :], M.x[:, t, :], mv[:, t, 0:1], rstd[:, t:t + 1],
                                                ALU.subtract, ALU.mult).then_inc(normed, 1)

                for g in range(GROUPS):
                    spreads(g)
                    if g:
                        normalize(g - 1)
                normalize(GROUPS - 1)

            @block.scalar
            def _(act):
                def copies(g):
                    for t in range(g * GROUP, (g + 1) * GROUP, 2):
                        act.wait_ge(turned, before_t + t + 2)
                        nc.scalar.activation(M.xT[:, :, t * P:(t + 2) * P],
                                             banks[t // 2][:, :].rearrange("p (k t) -> p k t", k=KD), ACT.Copy)

                for g in range(GROUPS):
                    act.wait_ge(spread, before_g + g + 1)
                    nc.scalar.activation(rstd[:, part(g)], var[:, part(g)], ACT.Sqrt).then_inc(root, 1)
                    if g and out is None:
                        copies(g - 1)
                if out is None:
                    copies(GROUPS - 1)

            @block.tensor
            def _(pe):
                if out is None:
                    for t in range(TILES):
                        pe.wait_ge(normed, before_t + t + 1)
                        for c in range(KD):
                            last = nc.tensor.transpose(
                                banks[t // 2][:, c * DM + (t % 2) * P:c * DM + (t % 2 + 1) * P],
                                M.x[:, t, c * P:(c + 1) * P], M.ident[:, :])
                        last.then_inc(turned, 1)

            @block.sync
            def _(sp):
                if out is not None:
                    rows = out.rearrange("b s d -> (b s) d").rearrange("(n p) d -> p n d", p=P)
                    for g in range(GROUPS):
                        sp.wait_ge(normed, before_t + (g + 1) * GROUP)
                        sp.dma_start(rows[:, part(g), :], M.x[:, part(g), :]).then_inc(M.stored, 16)
                    sp.wait_ge(M.stored, GROUPS * 16)


def projection_phase(nc, M, D, G, squares_sum):
    with scope(nc, "pr") as s:
        wo, woL = s.sb_both("wo", [P, PAIRS, DM])
        woH = M.xL[:, :, :].rearrange("p k t -> p (k t)").rearrange("p (a d) -> p a d", a=PAIRS)
        inv = squares_sum
        NG = 3
        GH = [s.sb(f"GH{n}", [P, BLK], FP32R) for n in range(NG)]
        GL = [s.sb(f"GL{n}", [P, BLK], FP32R) for n in range(NG)]
        eps = s.sb("eps", [P, 1])
        bank = [s.ps(f"bank{n}") for n in range(KD)]
        ps_sum = [s.ps(f"sum{n}") for n in range(NBLK)]
        LOADS = 4
        wo_loaded, x_loaded = [s.sem(f"wo_loaded{n}") for n in range(LOADS)], s.sem("x_loaded")
        wo_high, wo_low = s.sem("wo_high"), s.sem("wo_low")
        G_high, G_low, used = s.sem("G_high"), s.sem("G_low"), s.sem("used")
        ready, summed, rooted, inverted = s.sem("ready"), s.sem("summed"), s.sem("rooted"), s.sem("inverted")
        scaled = s.sem("scaled")
        res = Residual(nc, M, s, 1.0)

        def reused(i, a):
            return i * PAIRS + (PAIRS + 1) + (a - NG if a else -1)

        with nc.Block() as block:
            @block.sync
            def _(sp):
                for n in range(LOADS):
                    part = slice(n * PAIRS // LOADS, (n + 1) * PAIRS // LOADS)
                    sp.dma_start(wo[:, part, :], D["out_w"].rearrange("(a p) d -> p a d", p=P)[:, part, :]
                                 ).then_inc(wo_loaded[n], 16)
                sp.dma_start(M.x[:, :, :], D["x"].rearrange("(n p) d -> p n d", p=P)).then_inc(x_loaded, 16)

            @block.gpsimd
            def _(pool):
                for a in range(PAIRS):
                    pool.wait_ge(wo_loaded[a * LOADS // PAIRS], 16)
                    nc.gpsimd.tensor_copy(woH[:, a, :], wo[:, a, :]).then_inc(wo_high, 1)
                    pool.wait_ge(wo_high, a + 1)
                    nc.gpsimd.tensor_tensor(woL[:, a, :], wo[:, a, :], woH[:, a, :].bitcast(FP32), ALU.subtract
                                            ).then_inc(wo_low, 1)

            @block.tensor
            def _(pe):
                pe.sem_inc(used, PAIRS)
                for n in range(NBLK):
                    nc.tensor.matmul(ps_sum[n][:, :], M.ones[:, :], squares_sum[:, n * BLK:(n + 1) * BLK],
                                     start=True, stop=True).then_inc(summed, 1)
                with pe.Fori(0, NBLK) as i:
                    pe.wait_ge(scaled, i * KD + KD)
                    for a in range(PAIRS):
                        pe.wait_ge(wo_low, a + 1)
                        pe.wait_ge(G_low, i * PAIRS + a + 1)
                        for d in range(KD):
                            of = slice(d * P, (d + 1) * P)
                            nc.tensor.matmul(bank[d][:, :], woH[:, a, of], GH[a % NG][:, :], start=(a == 0), stop=False)
                            nc.tensor.matmul(bank[d][:, :], woH[:, a, of], GL[a % NG][:, :], start=False, stop=False)
                            last = nc.tensor.matmul(bank[d][:, :], woL[:, a, of], GH[a % NG][:, :],
                                                    start=False, stop=(a == PAIRS - 1))
                        last.then_inc(used, 1)
                    res.tensor(pe, i, scaled, i * KD + 2 * KD)

            @block.scalar
            def _(act):
                act.wait_ge(ready, 1)
                for n in range(NBLK):
                    act.wait_ge(summed, n + 1)
                    nc.scalar.activation(inv[:, n * BLK:(n + 1) * BLK], ps_sum[n][:, :], ACT.Sqrt, scale=1.0 / FEAT,
                                         bias=eps[:, 0:1]).then_inc(rooted, 1)
                with act.Fori(0, NBLK) as i:
                    for a in range(PAIRS):
                        wait_apart(act, used, reused(i, a), M.passed)
                        nc.scalar.activation(GH[a % NG][:, :].unsqueeze(1), G[:, a:a + 1, ds(i * BLK, BLK)], ACT.Copy
                                             ).then_inc(G_high, 1)

            @block.vector
            def _(dve):
                nc.vector.memset(eps[:, :], 1e-5).then_inc(ready, 1)
                dve.sem_inc(scaled, KD)
                dve.sem_inc(res.added, KD)
                with dve.Fori(0, NBLK) as i:
                    of_block = inv[:, ds(i * BLK, BLK)]
                    wait_apart(dve, rooted, i + 1, M.passed)
                    for a in range(PAIRS):
                        if a % 4 == 3:
                            quarter = inv[:, ds(i * BLK + a // 4 * P, P)]
                            nc.vector.reciprocal(quarter, quarter).then_inc(inverted, 1)
                        wait_apart(dve, used, reused(i, a), M.passed)
                        wait_apart(dve, G_high, i * PAIRS + a + 1, M.passed)
                        nc.vector.tensor_tensor(GL[a % NG][:, :].unsqueeze(1), G[:, a:a + 1, ds(i * BLK, BLK)],
                                                GH[a % NG][:, :].unsqueeze(1).bitcast(FP32), ALU.subtract
                                                ).then_inc(G_low, 1)
                    wait_apart(dve, inverted, i * 4 + 4, M.passed)
                    wait_apart(dve, used, (i + 2) * PAIRS, M.passed)
                    for d in range(KD):
                        nc.vector.tensor_tensor(res.y[:, d, :], bank[d][:, :], of_block, ALU.mult
                                                ).then_inc(scaled, 1)
                    dve.wait_ge(x_loaded, 16)
                    res.vector(dve, i, stats=False)


ROUTED, SHARED, FF = 16, 2, 176
TOP_K = 4
EXPERTS = ROUTED + SHARED
PARTS = 3
FTILES = -(-EXPERTS * FF // P)
LOADS = 5
FPL = FTILES // LOADS
CUT_EARLY = 4


def expert_rows():
    import numpy as np
    t = np.zeros((PARTS, EXPERTS, FTILES * P))
    for e in range(EXPERTS):
        t[:, e, e * FF:(e + 1) * FF] = 1.0
        t[:, e, EXPERTS * FF + e] = 1.0
    return t.reshape(PARTS * EXPERTS, FTILES * P).astype(np.uint16) * ONE_BITS


def router_phase(nc, M, D, gate_parts, load_weights, cut_weights):
    with scope(nc, "ro") as s:
        cent = s.sb("cent", [P, KD, ROUTED])
        bias = s.sb("bias", [P, ROUTED])
        score = s.sb("score", [P, TILES, ROUTED])
        top = s.sb("top", [P, TILES, 8])
        kept = s.sb("kept", [P, TILES, ROUTED])
        total = s.sb("total", [P, TILES])
        g = s.sb("g", [P, TILES, EXPERTS])
        parts = s.sb("parts", [P, TILES, PARTS, EXPERTS], BF16)
        rest = [s.sb(f"rest{n}", [P, TILES, EXPERTS]) for n in range(PARTS - 1)]
        ps_score = s.ps("score")
        ps_part = [s.ps(f"part{n}", (P, 1024), BF16) for n in range(2)]
        loaded, product, squashed, step = s.sem("loaded"), s.sem("product"), s.sem("squashed"), s.sem("step")
        g_ready, parts_ready, turned = s.sem("g_ready"), s.sem("parts_ready"), s.sem("turned")
        with nc.Block() as block:
            @block.sync
            def _(sp):
                sp.dma_start(cent[:, :, :], D["centroids"].rearrange("(k p) e -> p k e", p=P)).then_inc(loaded, 16)
                sp.dma_start(bias[:, :], D["route_bias"].partition_broadcast(P)).then_inc(loaded, 16)
                load_weights(sp)

            @block.gpsimd
            def _(pool):
                cut_weights(pool)

            @block.tensor
            def _(pe):
                pe.wait_ge(loaded, 32)
                for t in range(TILES):
                    for c in range(KD):
                        last = nc.tensor.matmul(ps_score[:, t * ROUTED:(t + 1) * ROUTED],
                                                M.xT[:, c, t * P:(t + 1) * P], cent[:, c, :],
                                                start=(c == 0), stop=(c == KD - 1))
                last.then_inc(product, 1)
                pe.wait_ge(parts_ready, PARTS)
                for t in range(TILES):
                    last = nc.tensor.transpose(ps_part[t // 8][0:PARTS * EXPERTS, t % 8 * P:(t % 8 + 1) * P],
                                               parts[:, t, :, :].rearrange("p a e -> p (a e)"), M.ident16[:, :])
                    if t % 8 == 7:
                        last.then_inc(turned, 1)

            @block.scalar
            def _(act):
                act.wait_ge(product, 1)
                nc.scalar.activation(score[:, :, :].rearrange("p t e -> p (t e)"),
                                     ps_score[:, 0:TILES * ROUTED], ACT.Sigmoid).then_inc(squashed, 1)
                for n in range(2):
                    act.wait_ge(turned, n + 1)
                    nc.scalar.activation(gate_parts[:, n * 1024:(n + 1) * 1024],
                                         ps_part[n][0:PARTS * EXPERTS, :], ACT.Copy)

            @block.vector
            def _(dve):
                def wide(ap):
                    return ap.broadcast_to([P, TILES, ROUTED])

                nc.vector.memset(g[:, :, ROUTED:EXPERTS], 1.0)
                dve.wait_ge(loaded, 32)
                dve.wait_ge(squashed, 1)
                nc.vector.tensor_tensor(score[:, :, :], score[:, :, :], wide(bias[:, :].unsqueeze(1)),
                                        ALU.add).then_inc(step, 1)
                dve.wait_ge(step, 1)
                for t in range(TILES):
                    last = nc.vector.max(top[:, t, :], score[:, t, :])
                last.then_inc(step, 1)
                dve.wait_ge(step, 2)
                nc.vector.tensor_tensor(kept[:, :, :], score[:, :, :], wide(top[:, :, TOP_K - 1:TOP_K]),
                                        ALU.is_ge).then_inc(step, 1)
                dve.wait_ge(step, 3)
                nc.vector.tensor_tensor(kept[:, :, :], kept[:, :, :], score[:, :, :], ALU.mult).then_inc(step, 1)
                dve.wait_ge(step, 4)
                nc.vector.tensor_reduce(total[:, :], kept[:, :, :], AX.X, ALU.add).then_inc(step, 1)
                dve.wait_ge(step, 5)
                nc.vector.tensor_scalar(total[:, :], total[:, :], 1e-8, None, ALU.max).then_inc(step, 1)
                dve.wait_ge(step, 6)
                nc.vector.reciprocal(total[:, :], total[:, :]).then_inc(step, 1)
                dve.wait_ge(step, 7)
                nc.vector.tensor_tensor(g[:, :, 0:ROUTED], kept[:, :, :], wide(total[:, :].unsqueeze(2)),
                                        ALU.mult).then_inc(g_ready, 1)
                dve.wait_ge(g_ready, 1)
                whole = g
                for n in range(PARTS):
                    nc.vector.tensor_copy(parts[:, :, n, :], whole[:, :, :]).then_inc(parts_ready, 1)
                    if n < PARTS - 1:
                        dve.wait_ge(parts_ready, n + 1)
                        nc.vector.tensor_tensor(rest[n][:, :, :], whole[:, :, :], parts[:, :, n, :],
                                                ALU.subtract).then_inc(step, 1)
                        dve.wait_ge(step, 8 + n)
                        whole = rest[n]


def experts_phase(nc, M, D):
    with scope(nc, "mo") as s:
        gate_parts = s.sb("gate_parts", [PARTS * EXPERTS, TOKENS], BF16)
        w1, w1L = s.sb_both("w1", [P, KD, FTILES * P])
        w2, w2L = s.sb_both("w2", [P, FTILES, DM])
        w_loaded = [s.sem(f"w_loaded{n}") for n in range(LOADS)]

        def load_weights(sp):
            for n in range(LOADS):
                c = slice(n * FPL * P, (n + 1) * FPL * P)
                sp.dma_start(w1[:, :, c], D["w1"].rearrange("(k p) f -> p k f", p=P)[:, :, c]
                             ).then_inc(w_loaded[n], 16)
                sp.dma_start(w2[:, n * FPL:(n + 1) * FPL, :],
                             D["w2"].rearrange("(f p) d -> p f d", p=P)[:, n * FPL:(n + 1) * FPL, :]
                             ).then_inc(w_loaded[n], 16)

        w1H = s.sb("w1H", [P, KD, FTILES * P], FP32R)
        w2H = s.sb("w2H", [P, FTILES, DM], FP32R)
        w_high, w_low = s.sem("w_high"), s.sem("w_low")

        def cut_weights(pool, tiles):
            for f in tiles:
                pool.wait_ge(w_loaded[f // FPL], 32)
                fs = slice(f * P, (f + 1) * P)
                nc.gpsimd.tensor_copy(w1H[:, :, fs], w1[:, :, fs]).then_inc(w_high, 1)
                nc.gpsimd.tensor_copy(w2H[:, f, :], w2[:, f, :]).then_inc(w_high, 1)
                pool.wait_ge(w_high, 2 * f + 1)
                nc.gpsimd.tensor_tensor(w1L[:, :, fs], w1[:, :, fs], w1H[:, :, fs].bitcast(FP32), ALU.subtract
                                        ).then_inc(w_low, 1)
                pool.wait_ge(w_high, 2 * f + 2)
                nc.gpsimd.tensor_tensor(w2L[:, f, :], w2[:, f, :], w2H[:, f, :].bitcast(FP32), ALU.subtract
                                        ).then_inc(w_low, 1)

        router_phase(nc, M, D, gate_parts, load_weights, lambda pool: cut_weights(pool, range(CUT_EARLY)))
        xH = s.sb("xH", [P, KD, TOKENS], FP32R)
        xL = M.xL
        b1 = s.sb("b1", [P, FTILES])
        rows = s.sb("rows", [PARTS * EXPERTS, FTILES * P], BF16)
        NH = 3
        hidden = [s.sb(f"hidden{n}", [P, BLK]) for n in range(2)]
        gated = [s.sb(f"gated{n}", [P, BLK]) for n in range(2)]
        gatedH = [s.sb(f"gatedH{n}", [P, BLK], FP32R) for n in range(NH)]
        gatedL = [s.sb(f"gatedL{n}", [P, BLK], FP32R) for n in range(NH)]
        ps_h = [s.ps(f"h{n}") for n in range(2)]
        ps_g = [s.ps(f"g{n}") for n in range(2)]
        acc = [s.ps(f"acc{n}") for n in range(KD)]
        small_loaded = s.sem("small_loaded")
        x_high, x_low = s.sem("x_high"), s.sem("x_low")
        high_ready, low_ready = s.sem("high_ready"), s.sem("low_ready")
        h_product, g_product, relu_ready = s.sem("h_product"), s.sem("g_product"), s.sem("relu_ready")
        gated_ready, used = s.sem("gated_ready"), s.sem("used")
        product, y_ready = s.sem("product"), s.sem("y_ready")
        res = Residual(nc, M, s, 2.0)

        def done(i, f):
            return i * FTILES + (FTILES + f + 1)

        with nc.Block() as block:
            @block.sync
            def _(sp):
                sp.dma_start(b1[:, :], D["b1"]).then_inc(small_loaded, 16)
                sp.dma_start(rows[:, :], D["expert_rows"].bitcast(BF16)).then_inc(small_loaded, 16)

            @block.tensor
            def _(pe):
                pe.sem_inc(used, FTILES)
                pe.wait_ge(small_loaded, 32)
                with pe.Fori(0, NBLK) as i:
                    pe.wait_ge(x_low, i + 1)
                    for f in range(FTILES + 2):
                        if f < FTILES:
                            fs = slice(f * P, (f + 1) * P)
                            pe.wait_ge(w_low, 2 * f + 2)
                            pe.wait_ge(relu_ready, done(i, f - 2))
                            for c in range(KD):
                                xs = (slice(None), c, ds(i * BLK, BLK))
                                nc.tensor.matmul(ps_h[f % 2][:, :], w1H[:, c, fs], xH[xs], start=(c == 0), stop=False)
                                nc.tensor.matmul(ps_h[f % 2][:, :], w1H[:, c, fs], xL[xs], start=False, stop=False)
                                last = nc.tensor.matmul(ps_h[f % 2][:, :], w1L[:, c, fs], xH[xs],
                                                        start=False, stop=(c == KD - 1))
                            last.then_inc(h_product, 1)
                            wait_apart(pe, gated_ready, done(i, f - 2), M.passed)
                            nc.tensor.matmul(ps_g[f % 2][:, :], rows[:, fs], gate_parts[:, ds(i * BLK, BLK)],
                                             start=True, stop=True).then_inc(g_product, 1)
                        if f == 1:
                            pe.wait_ge(y_ready, i * KD + KD)
                        if f >= 2:
                            g = f - 2
                            pe.wait_ge(low_ready, done(i, g))
                            for d in range(KD):
                                of = slice(d * P, (d + 1) * P)
                                nc.tensor.matmul(acc[d][:, :], w2H[:, g, of], gatedH[g % NH][:, :],
                                                 start=(g == 0), stop=False)
                                nc.tensor.matmul(acc[d][:, :], w2H[:, g, of], gatedL[g % NH][:, :],
                                                 start=False, stop=False)
                                last = nc.tensor.matmul(acc[d][:, :], w2L[:, g, of], gatedH[g % NH][:, :],
                                                        start=False, stop=(g == FTILES - 1))
                            last.then_inc(used, 1)
                    res.tensor(pe, i, y_ready, i * KD + 2 * KD)

            @block.gpsimd
            def _(pool):
                cut_weights(pool, range(CUT_EARLY, FTILES))

            @block.scalar
            def _(act):
                act.sem_inc(relu_ready, FTILES)
                act.sem_inc(high_ready, FTILES)
                act.sem_inc(y_ready, KD)
                for n in range(NBLK):
                    nc.scalar.activation(xH[:, :, n * BLK:(n + 1) * BLK], M.xT[:, :, n * BLK:(n + 1) * BLK], ACT.Copy
                                         ).then_inc(x_high, 1)
                act.wait_ge(small_loaded, 32)

                def high(i, f):
                    act.wait_ge(gated_ready, done(i, f))
                    act.wait_ge(used, done(i, f - NH))
                    nc.scalar.activation(gatedH[f % NH][:, :], gated[f % 2][:, :], ACT.Copy).then_inc(high_ready, 1)

                with act.Fori(0, NBLK) as i:
                    for f in range(FTILES):
                        act.wait_ge(h_product, done(i, f) - FTILES)
                        act.wait_ge(gated_ready, done(i, f - 2))
                        nc.scalar.activation(hidden[f % 2][:, :], ps_h[f % 2][:, :], ACT.Relu,
                                             bias=b1[:, f:f + 1]).then_inc(relu_ready, 1)
                        if f >= 1:
                            high(i, f - 1)
                    high(i, FTILES - 1)
                    act.wait_ge(used, done(i, FTILES - 1))
                    for d in range(KD):
                        nc.scalar.activation(res.y[:, d, :], acc[d][:, :], ACT.Copy).then_inc(y_ready, 1)

            @block.vector
            def _(dve):
                dve.sem_inc(gated_ready, FTILES)
                dve.sem_inc(low_ready, FTILES)
                dve.sem_inc(res.added, KD)
                for n in range(NBLK):
                    b = slice(n * BLK, (n + 1) * BLK)
                    dve.wait_ge(x_high, n + 1)
                    nc.vector.tensor_tensor(xL[:, :, b], M.xT[:, :, b], xH[:, :, b].bitcast(FP32), ALU.subtract
                                            ).then_inc(x_low, 1)

                def low(i, f):
                    dve.wait_ge(high_ready, done(i, f))
                    nc.vector.tensor_tensor(gatedL[f % NH][:, :], gated[f % 2][:, :], gatedH[f % NH][:, :].bitcast(FP32),
                                            ALU.subtract).then_inc(low_ready, 1)

                with dve.Fori(0, NBLK) as i:
                    for f in range(FTILES):
                        dve.wait_ge(relu_ready, done(i, f))
                        dve.wait_ge(g_product, done(i, f) - FTILES)
                        dve.wait_ge(low_ready, done(i, f - 2))
                        nc.vector.tensor_tensor(gated[f % 2][:, :], hidden[f % 2][:, :], ps_g[f % 2][:, :],
                                                ALU.mult).then_inc(gated_ready, 1)
                        if f >= 1:
                            low(i, f - 1)
                    low(i, FTILES - 1)
                    res.vector(dve, i)


STATES, DT_RANK = 16, 128
BC = 2 * STATES
HALF = 2 * SEQ
SEQ_HALF = HALF // SEQ


def state_rows():
    import numpy as np
    t = np.zeros((PARTS, BC, BC, P))
    t[:, np.arange(BC), np.arange(BC), :] = 1.0
    return t.reshape(PARTS * BC, BC * P).astype(np.uint16) * ONE_BITS


def step_phase(nc, M, D, dt, dtx, bc_parts, decay):
    with scope(nc, "dt") as s:
        wx = s.sb("wx", [P, KD, DT_RANK + PARTS * BC])
        wdt = s.sb("wdt", [P, DM])
        bx = s.sb("bx", [P, 1])
        bbc = s.sb("bbc", [PARTS * BC, 1])
        bdt = s.sb("bdt", [P, KD])
        rank = s.sb("rank", [P, BLK])
        bc = s.sb("bc", [PARTS * BC, BLK])
        high = s.sb("high", [PARTS * BC, BLK], BF16)
        rest = s.sb("rest", [PARTS * BC, BLK])
        mid = s.sb("mid", [PARTS * BC, BLK], BF16)
        rest2 = s.sb("rest2", [PARTS * BC, BLK])
        size = [s.sb(f"size{d}", [P, BLK]) for d in range(KD)]
        e = [s.sb(f"e{d}", [P, BLK]) for d in range(KD)]
        log = [s.sb(f"log{d}", [P, BLK]) for d in range(KD)]
        one_e = [s.sb(f"one_e{d}", [P, BLK]) for d in range(KD)]
        lost = [s.sb(f"lost{d}", [P, BLK]) for d in range(KD)]
        positive = [s.sb(f"positive{d}", [P, BLK]) for d in range(KD)]
        ps_rank, ps_bc = s.ps("rank"), s.ps("bc")
        ps_dt = [s.ps(f"dt{d}") for d in range(KD)]
        loaded, rank_product, bc_product, dt_product = (s.sem(n) for n in ("loaded", "rank_product", "bc_product", "dt_product"))
        rank_ready, bc_ready, bc_step = s.sem("rank_ready"), s.sem("bc_ready"), s.sem("bc_step")
        size_ready, e_ready, log_ready, dt_step = s.sem("size_ready"), s.sem("e_ready"), s.sem("log_ready"), s.sem("dt_step")
        bc_kept = s.sem("bc_kept")
        a_step = s.sem("a_step")
        LOADED = 7 * 16
        VS = 5

        def step(i, d, n):
            return (i * KD + d) * VS + (n + KD * VS + 1)

        def last_step(i, d, n):
            return (i * KD + d) * VS + (n + 1)
        with nc.Block() as block:
            @block.sync
            def _(sp):
                for to, of in ((wx[:, :, :], D["wx"].rearrange("(k p) r -> p k r", p=P)), (wdt[:, :], D["wdt"]),
                               (bx[:, :], D["bx"][0:DT_RANK, :]), (bbc[:, :], D["bx"][DT_RANK:, :]),
                               (bdt[:, :], D["bdt"]), (decay[:, :, :], D["a_log"]),
                               (M.state_rows[:, :], D["state_rows"].bitcast(BF16))):
                    sp.dma_start(to, of).then_inc(loaded, 16)

            @block.tensor
            def _(pe):
                pe.wait_ge(loaded, LOADED)
                with pe.Fori(0, NBLK) as i:
                    for to, cols, sem, free in ((ps_rank[:, :], slice(0, DT_RANK), rank_product, rank_ready),
                                                (ps_bc[0:PARTS * BC, :], slice(DT_RANK, DT_RANK + PARTS * BC),
                                                 bc_product, bc_ready)):
                        pe.wait_ge(free, i + 1)
                        for c in range(KD):
                            last = nc.tensor.matmul(to, wx[:, c, cols], M.xT[:, c, ds(i * BLK, BLK)],
                                                    start=(c == 0), stop=(c == KD - 1))
                        last.then_inc(sem, 1)
                    pe.wait_ge(rank_ready, i + 2)
                    pe.wait_ge(dt_step, last_step(i, KD - 1, 1))
                    for d in range(KD):
                        nc.tensor.matmul(ps_dt[d][:, :], wdt[:, d * P:(d + 1) * P], rank[:, :],
                                         start=True, stop=True).then_inc(dt_product, 1)

            @block.scalar
            def _(act):
                act.sem_inc(rank_ready, 1)
                act.sem_inc(bc_ready, 1)
                act.wait_ge(loaded, LOADED)
                nc.scalar.activation(decay[:, :, :], decay[:, :, :], ACT.Exp).then_inc(a_step, 1)
                with act.Fori(0, NBLK) as i:
                    act.wait_ge(rank_product, i + 1)
                    nc.scalar.activation(rank[:, :], ps_rank[:, :], ACT.Identity, bias=bx[:, 0:1]).then_inc(rank_ready, 1)
                    act.wait_ge(bc_product, i + 1)
                    act.wait_ge(bc_kept, i + 1)
                    nc.scalar.activation(bc[:, :], ps_bc[0:PARTS * BC, :], ACT.Identity, bias=bbc[:, 0:1]
                                         ).then_inc(bc_ready, 1)
                    for d in range(KD):
                        act.wait_ge(dt_product, i * KD + d + 1)
                        nc.scalar.activation(size[d][:, :], ps_dt[d][:, :], ACT.Abs, bias=bdt[:, d:d + 1]
                                             ).then_inc(size_ready, 1)
                    for d in range(KD):
                        act.wait_ge(size_ready, i * KD + d + 1)
                        act.wait_ge(dt_step, last_step(i, d, 3))
                        nc.scalar.activation(e[d][:, :], size[d][:, :], ACT.Exp, scale=-1.0).then_inc(e_ready, 1)
                    for d in range(KD):
                        act.wait_ge(e_ready, i * KD + d + 1)
                        act.wait_ge(dt_step, last_step(i, d, 5))
                        nc.scalar.activation(log[d][:, :], e[d][:, :], ACT.Ln, bias=1.0).then_inc(log_ready, 1)

            @block.vector
            def _(dve):
                dve.sem_inc(dt_step, KD * VS + 1)
                dve.wait_ge(a_step, 1)
                nc.vector.tensor_scalar(decay[:, :, :], decay[:, :, :], -1.0, None, ALU.mult).then_inc(a_step, 1)
                dve.wait_ge(loaded, LOADED)
                dve.sem_inc(bc_kept, 1)
                with dve.Fori(0, NBLK) as i:
                    def keep(n, of):
                        rows = slice(n * BC, (n + 1) * BC)
                        return nc.vector.tensor_copy(bc_parts[rows, ds(i * BLK, BLK)], of[rows, :])

                    wait_apart(dve, bc_ready, i + 2, M.passed)
                    nc.vector.tensor_copy(high[:, :], bc[:, :]).then_inc(bc_step, 1)
                    keep(0, bc)
                    dve.wait_ge(bc_step, i * 4 + 1)
                    nc.vector.tensor_tensor(rest[:, :], bc[:, :], high[:, :], ALU.subtract).then_inc(bc_step, 1)
                    wait_apart(dve, bc_step, i * 4 + 2, M.passed)
                    nc.vector.tensor_copy(mid[:, :], rest[:, :]).then_inc(bc_step, 1)
                    keep(1, rest)
                    dve.wait_ge(bc_step, i * 4 + 3)
                    nc.vector.tensor_tensor(rest2[:, :], rest[:, :], mid[:, :], ALU.subtract).then_inc(bc_step, 1)
                    wait_apart(dve, bc_step, i * 4 + 4, M.passed)
                    keep(2, rest2).then_inc(bc_kept, 1)
                    for d in range(KD):
                        dt_out = dt[:, d:d + 1, ds(i * BLK, BLK)]
                        dve.wait_ge(size_ready, i * KD + d + 1)
                        nc.vector.tensor_scalar(positive[d][:, :], ps_dt[d][:, :], bdt[:, d:d + 1], 0.0,
                                                ALU.add, ALU.max).then_inc(dt_step, 1)
                        dve.wait_ge(e_ready, i * KD + d + 1)
                        nc.vector.tensor_scalar(one_e[d][:, :], e[d][:, :], 1.0, None, ALU.add).then_inc(dt_step, 1)
                        dve.wait_ge(dt_step, step(i, d, 2))
                        nc.vector.scalar_tensor_tensor(lost[d][:, :], one_e[d][:, :], 1.0, e[d][:, :],
                                                       ALU.subtract, ALU.subtract).then_inc(dt_step, 1)
                        dve.wait_ge(log_ready, i * KD + d + 1)
                        dve.wait_ge(dt_step, step(i, d, 3))
                        nc.vector.tensor_tensor(log[d][:, :], log[d][:, :], lost[d][:, :], ALU.subtract
                                                ).then_inc(dt_step, 1)
                        dve.wait_ge(dt_step, step(i, d, 4))
                        nc.vector.tensor_tensor(dt_out, log[d][:, :].unsqueeze(1), positive[d][:, :].unsqueeze(1),
                                                ALU.add).then_inc(dt_step, 1)

            @block.gpsimd
            def _(pool):
                with pool.Fori(0, NBLK) as i:
                    for d in range(KD):
                        wait_apart(pool, dt_step, step(i, d, VS), M.passed)
                        t = ds(i * BLK, BLK)
                        nc.gpsimd.tensor_tensor(dtx[:, d:d + 1, t], dt[:, d:d + 1, t], M.xT[:, d:d + 1, t], ALU.mult)

def scan_phase(nc, M, D):
    with scope(nc, "sc") as s:
        dt = s.sb("dt", [P, KD, TOKENS])
        dtx = s.sb("dtx", [P, KD, TOKENS])
        bc_parts = s.sb("bc_parts", [PARTS * BC, TOKENS], BF16)
        decay = s.sb("decay", [P, KD, STATES])
        M.state_rows = s.sb("state_rows", [PARTS * BC, BC * P], BF16)
        y = s.sb("y", [P, KD, TOKENS])
        step_phase(nc, M, D, dt, dtx, bc_parts, decay)
        bs = [s.sb(f"bs{n}", [P, HALF]) for n in range(2)]
        a = [[s.sb(f"a{n}{d}", [P, HALF]) for d in range(KD)] for n in range(2)]
        bx = [[s.sb(f"bx{n}{d}", [P, HALF]) for d in range(KD)] for n in range(2)]
        h = [s.sb(f"h{d}", [P, HALF]) for d in range(KD)]
        hc = [[s.sb(f"hc{n}{d}", [P, HALF]) for d in range(KD)] for n in range(2)]
        with scope(nc, "s2") as q:
            ps_b, ps_c = q.ps("b", (P, HALF)), q.ps("c", (P, HALF))
            ps_y = [q.ps(f"y{d}", (P, HALF)) for d in range(KD)]
            b_product, c_product, y_sum = q.sem("b_product"), q.sem("c_product"), q.sem("y_sum")
            b_ready, a_ready, bx_ready = q.sem("b_ready"), q.sem("a_ready"), q.sem("bx_ready")
            scanned, hc_ready, y_ready = q.sem("scanned"), q.sem("hc_ready"), q.sem("y_ready")

            def done(i, n):
                return i * STATES + (STATES + n + 1)

            def done2(i, n, d=KD - 1):
                return i * (STATES * KD) + (STATES + n) * KD + d + 1

            with nc.Block() as block:
                def spread(i, to, row):
                    for t in range(HALF // BLK):
                        last = nc.tensor.matmul(to[:, t * BLK:(t + 1) * BLK],
                                                M.state_rows[:, row * P:(row + 1) * P],
                                                bc_parts[:, ds(i * HALF + t * BLK, BLK)], start=True, stop=True)
                    return last

                @block.tensor
                def _(pe):
                    pe.sem_inc(y_sum, STATES * KD)
                    with pe.Fori(0, TOKENS // HALF) as i:
                        for n in range(-1, STATES + 1):
                            if n + 1 < STATES:
                                wait_apart(pe, b_ready, done(i, n), M.passed)
                                spread(i, ps_b, n + 1).then_inc(b_product, 1)
                            if 0 <= n < STATES:
                                wait_apart(pe, hc_ready, done2(i, n - 1), M.passed)
                                spread(i, ps_c, STATES + n).then_inc(c_product, 1)
                            if n == 1:
                                pe.wait_ge(y_ready, i * KD + KD)
                            if n >= 1:
                                for d in range(KD):
                                    pe.wait_ge(hc_ready, done2(i, n - 1, d))
                                    for t in range(HALF // BLK):
                                        last = nc.tensor.matmul(ps_y[d][:, t * BLK:(t + 1) * BLK], M.ident[:, :],
                                                                hc[(n - 1) % 2][d][:, t * BLK:(t + 1) * BLK],
                                                                start=(n == 1), stop=(n == STATES))
                                    last.then_inc(y_sum, 1)

                @block.scalar
                def _(act):
                    act.sem_inc(b_ready, STATES)
                    act.sem_inc(y_ready, KD)
                    with act.Fori(0, TOKENS // HALF) as i:
                        for n in range(STATES):
                            act.wait_ge(b_product, done(i, n) - STATES)
                            act.wait_ge(bx_ready, done2(i, n - 2))
                            nc.scalar.activation(bs[n % 2][:, :], ps_b[:, :], ACT.Copy).then_inc(b_ready, 1)
                            for d in range(KD):
                                wait_apart(act, scanned, done2(i, n - 2, d), M.passed)
                                nc.scalar.activation(a[n % 2][d][:, :].unsqueeze(1),
                                                     dt[:, d:d + 1, ds(i * HALF, HALF)], ACT.Exp,
                                                     scale=decay[:, d, n:n + 1]).then_inc(a_ready, 1)
                        for d in range(KD):
                            act.wait_ge(y_sum, done2(i, STATES - 1, d))
                            nc.scalar.activation(y[:, d:d + 1, ds(i * HALF, HALF)], ps_y[d][:, :].unsqueeze(1),
                                                 ACT.Copy).then_inc(y_ready, 1)

                @block.gpsimd
                def _(pool):
                    pool.sem_inc(bx_ready, STATES * KD)
                    with pool.Fori(0, TOKENS // HALF) as i:
                        for n in range(STATES):
                            wait_apart(pool, b_ready, done(i, n), M.passed)
                            for d in range(KD):
                                wait_apart(pool, scanned, done2(i, n - 2, d), M.passed)
                                nc.gpsimd.tensor_tensor(bx[n % 2][d][:, :].unsqueeze(1),
                                                        dtx[:, d:d + 1, ds(i * HALF, HALF)],
                                                        bs[n % 2][:, :].unsqueeze(1), ALU.mult).then_inc(bx_ready, 1)

                @block.vector
                def _(dve):
                    dve.sem_inc(scanned, STATES * KD)
                    dve.sem_inc(hc_ready, STATES * KD)
                    with dve.Fori(0, TOKENS // HALF) as i:
                        for n in range(STATES):
                            for d in range(KD):
                                dve.wait_ge(a_ready, done2(i, n, d) - STATES * KD)
                                dve.wait_ge(bx_ready, done2(i, n, d))
                                dve.wait_ge(hc_ready, done2(i, n - 1, d))
                                for q_ in range(SEQ_HALF):
                                    t = slice(q_ * SEQ, (q_ + 1) * SEQ)
                                    last = nc.vector.tensor_tensor_scan(h[d][:, t], a[n % 2][d][:, t],
                                                                        bx[n % 2][d][:, t], 0.0, ALU.mult, ALU.add)
                                last.then_inc(scanned, 1)
                            for d in range(KD):
                                dve.wait_ge(scanned, done2(i, n, d))
                                dve.wait_ge(c_product, done(i, n) - STATES)
                                dve.wait_ge(y_sum, done2(i, n - 2, d))
                                nc.vector.tensor_tensor(hc[n % 2][d][:, :], h[d][:, :], ps_c[:, :], ALU.mult
                                                        ).then_inc(hc_ready, 1)
        with scope(nc, "s3") as q:
            res = Residual(nc, M, q, 1.0)
            with nc.Block() as block:
                @block.tensor
                def _(pe):
                    for i in range(NBLK):
                        res.tensor(pe, i, res.added, i * KD + KD, y[:, :, i * BLK:(i + 1) * BLK])

                @block.vector
                def _(dve):
                    dve.sem_inc(res.added, KD)
                    with dve.Fori(0, NBLK) as i:
                        res.vector(dve, i)


CROSS, PRIV, RETR = 1024, 128, 128
RHEADS, K_HEAD = 8, 8
KEYS = 45
KHD = RETR // 2
PAIRED = KEYS * KEYS
COLS = PAIRED + PAIRED % 2
EBLK = -(-COLS // P)
CUT = [(0, 1024), (1024, COLS)]
CUT_IN_THREE = (2, 6)
CUT3 = ((0, 676), (676, 1352), (1352, COLS))
QUARTER = tuple((a, min(a + 512, COLS)) for a in range(0, COLS, 512))
NEVER = -1.0e30
REPLACED = -3.0e38


def pair_rows():
    import numpy as np
    col = np.arange(COLS)
    e = np.minimum(col, PAIRED - 1)
    t = np.zeros((2 * KEYS, COLS), np.float32)
    t[e // KEYS, col] = 1.0
    t[KEYS + e % KEYS, col] = 1.0
    return t


def private_phase(nc, M, D, h, wk, load_tables):
    UPT = CROSS // P
    with scope(nc, "pv") as s:
        wu, wuL = s.sb_both("wu", [P, KD, CROSS])
        wd, wdL = s.sb_both("wd", [P, UPT, PRIV])
        wuH = s.sb("wuH", [P, KD, CROSS], FP32R)
        wdH = s.sb("wdH", [P, UPT, PRIV], FP32R)
        xH, xL = s.sb("xH", [P, KD, TOKENS], FP32R), M.xL
        bu = s.sb("bu", [P, UPT])
        bd = s.sb("bd", [P, 1])
        wq = s.sb("wq", [KHD, 2 * RHEADS, PRIV])
        keys = s.sb("keys", [KHD, 2 * RHEADS, KEYS])
        NB, LAG = 4, 2
        up = [s.sb(f"up{n}", [P, BLK]) for n in range(NB)]
        upH = [s.sb(f"upH{n}", [P, BLK], FP32R) for n in range(NB)]
        upL = [s.sb(f"upL{n}", [P, BLK], FP32R) for n in range(NB)]
        ps_up = [s.ps(f"up{n}") for n in range(NB)]
        ps_h = s.ps("h")
        ps_k = [s.ps(f"k{n}") for n in range(2)]
        loaded, up_product, up_ready, up_used = s.sem("loaded"), s.sem("up_product"), s.sem("up_ready"), s.sem("up_used")
        x_high, x_low, w_high, w_low = s.sem("x_high"), s.sem("x_low"), s.sem("w_high"), s.sem("w_low")
        up_high, up_low = s.sem("up_high"), s.sem("up_low")
        h_product, h_ready, k_product = s.sem("h_product"), s.sem("h_ready"), s.sem("k_product")

        def done(i, m):
            return i * UPT + (UPT + m + 1)

        with nc.Block() as block:
            @block.sync
            def _(sp):
                for to, of in ((wu[:, :, :], D["w_up"].rearrange("(k p) c -> p k c", p=P)), (bu[:, :], D["b_up"]),
                               (wd[:, :, :], D["w_down"].rearrange("(m p) r -> p m r", p=P)), (bd[:, :], D["b_down"]),
                               (wq[:, :, :], D["w_q"]), (keys[:, :, :], D["keys"])):
                    sp.dma_start(to, of).then_inc(loaded, 16)
                load_tables(sp)

            @block.tensor
            def _(pe):
                pe.sem_inc(up_used, UPT)
                pe.wait_ge(loaded, 6 * 16)
                for n in range(2 * RHEADS):
                    last = nc.tensor.matmul(ps_k[n // RHEADS][:, n % RHEADS * KEYS:(n % RHEADS + 1) * KEYS],
                                            wq[:, n, :], keys[:, n, :], start=True, stop=True)
                last.then_inc(k_product, 1)
                with pe.Fori(0, NBLK) as i:
                    pe.wait_ge(x_low, i + 1)
                    for m in range(UPT + LAG):
                        if m < UPT:
                            pe.wait_ge(w_low, 2 * m + 2)
                            pe.wait_ge(up_ready, done(i, m - NB))
                            of = slice(m * P, (m + 1) * P)
                            for c in range(KD):
                                xs = (slice(None), c, ds(i * BLK, BLK))
                                nc.tensor.matmul(ps_up[m % NB][:, :], wuH[:, c, of], xH[xs], start=(c == 0), stop=False)
                                nc.tensor.matmul(ps_up[m % NB][:, :], wuH[:, c, of], xL[xs], start=False, stop=False)
                                last = nc.tensor.matmul(ps_up[m % NB][:, :], wuL[:, c, of], xH[xs],
                                                        start=False, stop=(c == KD - 1))
                            last.then_inc(up_product, 1)
                        if m == LAG:
                            pe.wait_ge(h_ready, i + 1)
                        if m >= LAG:
                            g = m - LAG
                            pe.wait_ge(up_low, done(i, g))
                            nc.tensor.matmul(ps_h[:, :], wdH[:, g, :], upH[g % NB][:, :], start=(g == 0), stop=False)
                            nc.tensor.matmul(ps_h[:, :], wdH[:, g, :], upL[g % NB][:, :], start=False, stop=False)
                            last = nc.tensor.matmul(ps_h[:, :], wdL[:, g, :], upH[g % NB][:, :],
                                                    start=False, stop=(g == UPT - 1))
                            last.then_inc(up_used, 1)

            @block.gpsimd
            def _(pool):
                pool.wait_ge(loaded, 6 * 16)
                for m in range(UPT):
                    of = slice(m * P, (m + 1) * P)
                    nc.gpsimd.tensor_copy(wuH[:, :, of], wu[:, :, of]).then_inc(w_high, 1)
                    nc.gpsimd.tensor_copy(wdH[:, m, :], wd[:, m, :]).then_inc(w_high, 1)
                    pool.wait_ge(w_high, 2 * m + 1)
                    nc.gpsimd.tensor_tensor(wuL[:, :, of], wu[:, :, of], wuH[:, :, of].bitcast(FP32), ALU.subtract
                                            ).then_inc(w_low, 1)
                    pool.wait_ge(w_high, 2 * m + 2)
                    nc.gpsimd.tensor_tensor(wdL[:, m, :], wd[:, m, :], wdH[:, m, :].bitcast(FP32), ALU.subtract
                                            ).then_inc(w_low, 1)

            @block.vector
            def _(dve):
                dve.sem_inc(up_low, UPT)
                dve.sem_inc(h_ready, 1)
                for n in range(NBLK):
                    t = slice(n * BLK, (n + 1) * BLK)
                    dve.wait_ge(x_high, n + 1)
                    nc.vector.tensor_tensor(xL[:, :, t], M.xT[:, :, t], xH[:, :, t].bitcast(FP32), ALU.subtract
                                            ).then_inc(x_low, 1)
                with dve.Fori(0, NBLK) as i:
                    for m in range(UPT):
                        wait_apart(dve, up_ready, done(i, m), M.passed)
                        wait_apart(dve, up_used, done(i, m - NB), M.passed)
                        nc.vector.tensor_copy(upH[m % NB][:, :], up[m % NB][:, :]).then_inc(up_high, 1)
                        dve.wait_ge(up_high, i * UPT + m + 1)
                        nc.vector.tensor_tensor(upL[m % NB][:, :], up[m % NB][:, :], upH[m % NB][:, :].bitcast(FP32),
                                                ALU.subtract).then_inc(up_low, 1)
                    wait_apart(dve, up_used, done(i, UPT - 1), M.passed)
                    nc.vector.tensor_scalar(h[:, ds(i * BLK, BLK)], ps_h[:, :], bd[:, 0:1], None, ALU.add
                                            ).then_inc(h_ready, 1)

            @block.scalar
            def _(act):
                act.sem_inc(up_ready, UPT)
                for n in range(NBLK):
                    t = slice(n * BLK, (n + 1) * BLK)
                    nc.scalar.activation(xH[:, :, t], M.xT[:, :, t], ACT.Copy).then_inc(x_high, 1)
                act.wait_ge(loaded, 6 * 16)
                with act.Fori(0, NBLK) as i:
                    for m in range(UPT):
                        act.wait_ge(up_product, done(i, m) - UPT)
                        act.wait_ge(up_low, done(i, m - NB))
                        nc.scalar.activation(up[m % NB][:, :], ps_up[m % NB][:, :], ACT.Silu,
                                             bias=bu[:, m:m + 1]).then_inc(up_ready, 1)
                act.wait_ge(k_product, 1)
                for n in range(2):
                    nc.scalar.activation(wk[:, n * RHEADS * KEYS:(n + 1) * RHEADS * KEYS],
                                         ps_k[n][:, 0:RHEADS * KEYS], ACT.Copy)


PE_STEPS = """
    sums:0 fill_z:0 turn_Z:0 sums:1 sums:2 fill_z:1 sums:3 sums:4 sums:5 turn_Z:1 turn_Z:2 sums:6
    sums:7 fill_z:2 scores:0 sums:8 scores:1 fill_z:3 turn_kept:0 sums:9 sums:10 sums:11 turn_kept:1
    sums:12 sums:13 sums:14 turn_Z:3 sums:15 sums:16 sums:17 product:0 product:1 product:2 product:3
""".split()
ACT_STEPS = """
    exps:0 copy_z:0 exps:1 exps:2 copy_Z:0 copy_h exps:3 copy_z:1 exps:4 exps:5 silus:6 copy_Z:1
    copy_Z:2 silus:7 copy_scores:0 copy_z:2 exps:6 copy_scores:1 exps:7 exps:8 exps:9 copy_kept:0
    copy_z:3 exps:10 exps:11 exps:12 exps:13 exps:14 soften exps:15 copy_Z:3 copy_kept:1 exps:16
    exps:17 silus:0 silus:1 silus:2 silus:3 silus:4 silus:5
""".split()
DVE_STEPS = """
    top_eights replace candidates mask:0 mask:1 mask:2 weigh:0 weigh:1 mask:3 mask:4 keep mask:5
    bests replace_bests weigh:3 ninths weigh:4 mask:6 mask:7 mask:8 weigh:5 mask:9 mask:10 mask:11
    thresholds weigh:6 low_parts:0 mask:12 mask:13 mask:14 weigh:7 low_parts:1 mask:15 weigh:10
    weigh:14 mask:16 weigh:15 weigh:16 totals mask:17 weigh:17 add_out
""".split()
POOL_STEPS = """
    add:6 weigh:2 weigh:8 weigh:9 add:7 weigh:11 weigh:12 weigh:13 add:1 add:2 add:3 add:4 add:5
""".split()


def take(steps, do):
    for step in steps:
        name, _, n = step.partition(":")
        do[name](int(n)) if n else do[name]()


def retrieval_phase(nc, M, D):
    with scope(nc, "re") as s:
        h = s.sb("h", [P, TOKENS])
        wk = s.sb("wk", [P, RHEADS * 2 * KEYS])
        down = s.sb("down", [P, COLS])
        up = s.sb("up", [P, EBLK, DM])
        z = [s.sb(f"z{n}", [P, COLS]) for n in range(2)]
        tables_loaded = s.sem("tables_loaded")

        def load_tables(sp):
            sp.dma_start(down[:, :], D["down"]).then_inc(tables_loaded, 16)
            sp.dma_start(z[1][0:2 * KEYS, :], D["pairs"]).then_inc(tables_loaded, 16)
            sp.dma_start(up[:, 0:EBLK - 1, :],
                         D["up"][0:(EBLK - 1) * P, :].rearrange("(a p) d -> p a d", p=P)).then_inc(tables_loaded, 16)
            sp.dma_start(up[0:COLS % P, EBLK - 1, :], D["up"][(EBLK - 1) * P:COLS, :]).then_inc(tables_loaded, 16)

        private_phase(nc, M, D, h, wk, load_tables)
        pairs = s.sb("pairs", [2 * KEYS, COLS], FP32R)
        hs = [s.sb(f"hs{n}", [P, P]) for n in range(2)]
        sim = s.sb("sim", [P, 2 * RHEADS, KEYS])
        top = s.sb("top", [P, 2 * RHEADS, K_HEAD])
        left = s.sb("left", [P, 2 * RHEADS, KEYS])
        kept = s.sb("kept", [P, 2 * RHEADS, KEYS])
        cand = s.sb("cand", [P, RHEADS, K_HEAD, K_HEAD])
        best = s.sb("best", [P, RHEADS, 8])
        ninth = top[:, 0:RHEADS, :]
        soft = s.sb("soft", [P, RHEADS, 8])
        thr = [s.sb(f"thr{n}", [P, RHEADS]) for n in range(2)]
        shift = [s.sb(f"shift{n}", [P, RHEADS]) for n in range(2)]
        total = [s.sb(f"total{n}", [P, RHEADS]) for n in range(2)]
        keptH = [s.sb(f"keptH{n}", [2 * KEYS, RHEADS, P], FP32R) for n in range(2)]
        keptL = [s.sb(f"keptL{n}", [2 * KEYS, RHEADS, P], FP32R) for n in range(2)]
        NE = 4
        ex = [s.sb(f"ex{n}", [P, 1024]) for n in range(NE)]
        u = s.sb("u", [P, RHEADS, COLS])
        Z = [M.xT[:, n, 0:COLS] for n in range(2)]
        ZT = s.sb("ZT", [P, EBLK, P])
        NR = 3
        ring = [s.ps(f"ring{n}", (P, 1024)) for n in range(NR)]
        misc = [s.ps(f"misc{n}") for n in range(2)]

        names = ("late_sum hs_ready filled z_filled z_ready sim_product sim_ready kept_ready kept_turned keptT_ready "
                 "prep ex_ready masked weighted pool_weighted silu_ready summed z_turned zT_ready out_product "
                 "out_added soft_in soft_ready total_ready prep_step cand_ready high_ready pairs_ready").split()
        S = {n: s.sem(n) for n in names}
        UNITS = [(k, a, b) for k in range(RHEADS) for a, b in (CUT3 if k in CUT_IN_THREE else CUT)]
        NU = len(UNITS)
        LATE = 640
        FIRST = 6
        HEAD_END = [max(i for i in range(NU) if UNITS[i][0] == k) + 1 for k in range(RHEADS)]
        ON_POOL = [int(step[6:]) for step in POOL_STEPS if step[:6] == "weigh:"]
        ON_DVE = [i for i in range(NU) if i not in ON_POOL]

        def weighs_before(T, unit, mine):
            return T * len(mine) + sum(i < unit for i in mine)

        kinds = {"turn_Z": "Z", "turn_kept": "kept", "scores": "sim", "fill_z": "z"}
        USES = [("product", 0) if step == "product:0" else (kinds[step.partition(":")[0]], int(step.partition(":")[2]))
                for step in PE_STEPS if step == "product:0" or step.partition(":")[0] in kinds]
        TILE = {"Z": -2, "kept": 1, "sim": 2, "z": 1, "product": -2}
        READ = {"Z": ("zT_ready", 4), "kept": ("keptT_ready", 2), "sim": ("sim_ready", 2),
                "z": ("z_ready", 4), "product": ("out_added", 1)}

        def bank(kind, j):
            return misc[USES.index((kind, j)) % 2]

        def bank_wait(pe, T, kind, j):
            i = USES.index((kind, j))
            t, last = T, i - 2
            while True:
                if last < 0:
                    t, last = t - 1, (len(USES) - 1 if i % 2 == 0 else len(USES) - 2)
                before, b = USES[last]
                tile = t + TILE[before]
                if not isinstance(t, int) or 0 <= tile < TILES:
                    break
                if t < -2:
                    return
                last -= 2
            name, each = READ[before]
            need(pe, S[name], tile * each + (b + 1) + (before == "product"))
            if before == "product" and not isinstance(t, int):
                before, b = USES[last - 2]
                name, each = READ[before]
                need(pe, S[name], (t + TILE[before]) * each + (b + 1))

        def pe_turn(pe, T, n, live, ahead, behind, scored):
            def sums(i):
                if not live:
                    return
                k, a, b = UNITS[i]
                need(pe, S["masked"], T * NU + (i - NR + 1))
                need(pe, S["keptT_ready"], T * 2 + (1 + k // 4))
                for c in range(a, b, 512):
                    e = min(c + 512, b)
                    nc.tensor.matmul(ring[i % NR][:, c - a:e - a], keptH[n][:, k, :], pairs[:, c:e],
                                     start=True, stop=False)
                    last = nc.tensor.matmul(ring[i % NR][:, c - a:e - a], keptL[n][:, k, :], pairs[:, c:e],
                                            start=False, stop=True)
                last.then_inc(S["filled"], 1)

            def turn_Z(g):
                if not behind:
                    return
                if g == 0:
                    need(pe, S["summed"], (T - 1) * (RHEADS - 1))
                    if not ahead and T - 2 == TILES - 1:
                        need(pe, S["late_sum"], RHEADS - 1)
                bank_wait(pe, T, "Z", g)
                for q in range(4):
                    blk = 4 * g + q
                    w = min(P, COLS - blk * P)
                    last = nc.tensor.transpose(bank("Z", g)[0:w, q * P:(q + 1) * P],
                                               Z[n][:, blk * P:blk * P + w], M.ident[:, :])
                last.then_inc(S["z_turned"], 1)

            def turn_kept(m):
                if not ahead:
                    return
                need(pe, S["kept_ready"], T + 2)
                bank_wait(pe, T, "kept", m)
                for q in range(4):
                    k = 4 * m + q
                    last = nc.tensor.transpose(bank("kept", m)[0:2 * KEYS, q * P:(q + 1) * P],
                                               kept[:, 2 * k:2 * k + 2, :].rearrange("p a k -> p (a k)"),
                                               M.ident[:, :])
                last.then_inc(S["kept_turned"], 1)

            def scores(m):
                if not scored:
                    return
                need(pe, S["hs_ready"], T + 3)
                bank_wait(pe, T, "sim", m)
                nc.tensor.matmul(bank("sim", m)[:, 0:RHEADS * KEYS], hs[n][:, :],
                                 wk[:, m * RHEADS * KEYS:(m + 1) * RHEADS * KEYS],
                                 start=True, stop=True).then_inc(S["sim_product"], 1)

            def fill_z(j):
                if not ahead:
                    return
                bank_wait(pe, T, "z", j)
                a, b = QUARTER[j]
                nc.tensor.matmul(bank("z", j)[:, 0:b - a], hs[1 - n][:, :], down[:, a:b],
                                 start=True, stop=True).then_inc(S["z_filled"], 1)

            def product(part):
                if not behind:
                    return
                if part == 0:
                    need(pe, S["zT_ready"], (T - 2) * 4 + 4)
                    bank_wait(pe, T, "product", 0)
                for blk in range(part * EBLK // 4, (part + 1) * EBLK // 4):
                    w = min(P, COLS - blk * P)
                    last = nc.tensor.matmul(bank("product", 0)[:, 0:DM], ZT[0:w, blk, :], up[0:w, blk, :],
                                            start=(blk == 0), stop=(blk == EBLK - 1))
                if part == 3:
                    last.then_inc(S["out_product"], 1)

            take(PE_STEPS, dict(sums=sums, turn_Z=turn_Z, turn_kept=turn_kept, scores=scores, fill_z=fill_z,
                                product=product))

        def act_turn(act, T, n, live, last_silus, ahead, behind, scored):
            def exps(i):
                if not live:
                    return
                k, a, b = UNITS[i]
                if i == 0:
                    need(act, S["prep"], T + 1)
                need(act, S["filled"], T * NU + (i + 1))
                need(act, S["masked"], T * NU + (i + 1 - NE))
                nc.scalar.activation(ex[(n * NU + i) % NE][:, 0:b - a], ring[i % NR][:, 0:b - a], ACT.Exp,
                                     bias=shift[n][:, k:k + 1]).then_inc(S["ex_ready"], 1)

            def silus(k):
                t, b = (T, n) if k < FIRST else (T - 1, 1 - n)
                if not (live if k < FIRST else last_silus):
                    return
                need(act, S["total_ready"], t + 1)
                need(act, S["weighted"], weighs_before(t, HEAD_END[k], ON_DVE))
                need(act, S["pool_weighted"], weighs_before(t, HEAD_END[k], ON_POOL))
                nc.scalar.activation(u[:, k, :], u[:, k, :], ACT.Silu, scale=total[b][:, k:k + 1]
                                     ).then_inc(S["silu_ready"], 1)

            def copy_h():
                if not scored:
                    return
                nc.scalar.activation(hs[n][:, :], h[:, ds((T + 2) * P, P)], ACT.Copy).then_inc(S["hs_ready"], 1)

            def copy_Z(g):
                if not behind:
                    return
                need(act, S["z_turned"], (T - 2) * 4 + (g + 1))
                need(act, S["out_product"], T - 1)
                full = min(4, (COLS - 4 * g * P) // P)
                last = nc.scalar.activation(ZT[:, 4 * g:4 * g + full, :].rearrange("p a t -> p (a t)"),
                                            bank("Z", g)[:, 0:full * P], ACT.Copy)
                if full < 4:
                    w = COLS % P
                    last = nc.scalar.activation(ZT[0:w, 4 * g + full, :],
                                                bank("Z", g)[0:w, full * P:(full + 1) * P], ACT.Copy)
                last.then_inc(S["zT_ready"], 1)

            def copy_kept(m):
                if not ahead:
                    return
                need(act, S["kept_turned"], T * 2 + (3 + m))
                nc.scalar.activation(keptH[1 - n][:, 4 * m:4 * m + 4, :].rearrange("k h t -> k (h t)"),
                                     bank("kept", m)[0:2 * KEYS, :], ACT.Copy).then_inc(S["high_ready"], 1)

            def copy_scores(m):
                if not scored:
                    return
                need(act, S["sim_product"], T * 2 + (5 + m))
                need(act, S["kept_ready"], T + 2)
                nc.scalar.activation(sim[:, m * RHEADS:(m + 1) * RHEADS, :].rearrange("p a k -> p (a k)"),
                                     bank("sim", m)[:, 0:RHEADS * KEYS], ACT.Copy).then_inc(S["sim_ready"], 1)

            def copy_z(j):
                if not ahead:
                    return
                need(act, S["z_filled"], T * 4 + (5 + j))
                if j == 0:
                    need(act, S["weighted"], weighs_before(T, 0, ON_DVE))
                    need(act, S["pool_weighted"], weighs_before(T, 0, ON_POOL))
                a, b = QUARTER[j]
                nc.scalar.activation(z[1 - n][:, a:b], bank("z", j)[:, 0:b - a], ACT.Copy).then_inc(S["z_ready"], 1)

            def soften():
                if not ahead:
                    return
                need(act, S["soft_in"], T + 2)
                nc.scalar.activation(soft[:, :, :], soft[:, :, :], ACT.Exp).then_inc(S["soft_ready"], 1)

            take(ACT_STEPS, dict(copy_h=copy_h, exps=exps, silus=silus, copy_Z=copy_Z, copy_kept=copy_kept,
                                 copy_scores=copy_scores, copy_z=copy_z, soften=soften))

        CH = 9

        def dve_turn(dve, T, n, live, ahead, behind):
            def chain(c):
                return (T + 1) * CH + c

            def mask(i):
                if not live:
                    return
                k, a, b = UNITS[i]
                need(dve, S["ex_ready"], T * NU + (i + 1))
                if a == 0:
                    need(dve, S["summed"], (T - 1) * (RHEADS - 1) + max(k, 1))
                nc.vector.scalar_tensor_tensor(u[:, k, a:b], ring[i % NR][:, 0:b - a], thr[n][:, k:k + 1],
                                               ex[(n * NU + i) % NE][:, 0:b - a], ALU.is_ge, ALU.mult
                                               ).then_inc(S["masked"], 1)

            def weigh(i):
                if not live:
                    return
                k, a, b = UNITS[i]
                need(dve, S["z_ready"], T * 4 + 4)
                need(dve, S["masked"], T * NU + (i + 1))
                nc.vector.tensor_tensor(u[:, k, a:b], u[:, k, a:b], z[n][:, a:b], ALU.mult).then_inc(S["weighted"], 1)

            def top_eights():
                if not ahead:
                    return
                need_apart(dve, S["sim_ready"], T * 2 + 4, M.passed)
                for q in range(2 * RHEADS):
                    last = nc.vector.max(top[:, q, :], sim[:, q, :])
                last.then_inc(S["prep_step"], 1)

            def replace():
                if not ahead:
                    return
                need_apart(dve, S["prep_step"], chain(1), M.passed)
                for q in range(2 * RHEADS):
                    last = nc.vector.match_replace(out=left[:, q, :], in_to_replace=top[:, q, :],
                                                   in_values=sim[:, q, :], imm_value=REPLACED)
                last.then_inc(S["prep_step"], 1)

            def candidates():
                if not ahead:
                    return
                nc.vector.tensor_tensor(
                    cand[:, :, :, :],
                    top[:, :, :].rearrange("p (h a) k -> p h a k", a=2)[:, :, 0, :].unsqueeze(3)
                    .broadcast_to([P, RHEADS, K_HEAD, K_HEAD]),
                    top[:, :, :].rearrange("p (h a) k -> p h a k", a=2)[:, :, 1, :].unsqueeze(2)
                    .broadcast_to([P, RHEADS, K_HEAD, K_HEAD]), ALU.add).then_inc(S["cand_ready"], 1)
                need(dve, S["prep_step"], chain(2))
                nc.vector.tensor_tensor(left[:, :, :], left[:, :, :], sim[:, :, :], ALU.is_equal
                                        ).then_inc(S["prep_step"], 1)

            def keep():
                if not ahead:
                    return
                need(dve, S["prep_step"], chain(3))
                need(dve, S["kept_turned"], T * 2 + 2)
                nc.vector.scalar_tensor_tensor(kept[:, :, :], left[:, :, :], NEVER, sim[:, :, :],
                                               ALU.mult, ALU.add).then_inc(S["kept_ready"], 1)

            def bests():
                if not ahead:
                    return
                need_apart(dve, S["cand_ready"], T + 2, M.passed)
                for q in range(RHEADS):
                    last = nc.vector.max(best[:, q, :], cand[:, q, :, :].rearrange("p a b -> p (a b)"))
                last.then_inc(S["prep_step"], 1)

            def replace_bests():
                if not ahead:
                    return
                need_apart(dve, S["prep_step"], chain(4), M.passed)
                for q in range(RHEADS):
                    last = nc.vector.match_replace(out=cand[:, q, :, :].rearrange("p a b -> p (a b)"), in_to_replace=best[:, q, :],
                                                   in_values=cand[:, q, :, :].rearrange("p a b -> p (a b)"),
                                                   imm_value=REPLACED)
                last.then_inc(S["prep_step"], 1)
                nc.vector.tensor_scalar(shift[1 - n][:, :], best[:, :, 0], -1.0, None, ALU.mult
                                        ).then_inc(S["prep_step"], 1)

            def ninths():
                if not ahead:
                    return
                need_apart(dve, S["prep_step"], chain(5), M.passed)
                for q in range(RHEADS):
                    last = nc.vector.max(ninth[:, q, :], cand[:, q, :, :].rearrange("p a b -> p (a b)"))
                last.then_inc(S["prep_step"], 1)

            def thresholds():
                if not ahead:
                    return
                need(dve, S["prep_step"], chain(6))
                nc.vector.tensor_tensor(soft[:, :, :], best[:, :, :],
                                        shift[1 - n][:, :].unsqueeze(2).broadcast_to([P, RHEADS, 8]),
                                        ALU.add).then_inc(S["soft_in"], 1)
                need(dve, S["prep_step"], chain(7))
                nc.vector.tensor_tensor(thr[1 - n][:, :], best[:, :, K_HEAD - 1], ninth[:, :, 0], ALU.add
                                        ).then_inc(S["prep_step"], 1)
                need(dve, S["prep_step"], chain(8))
                nc.vector.tensor_scalar(thr[1 - n][:, :], thr[1 - n][:, :], 0.5, None, ALU.mult
                                        ).then_inc(S["prep"], 1)

            def totals():
                if not ahead:
                    return
                need(dve, S["soft_ready"], T + 2)
                need(dve, S["silu_ready"], T * RHEADS)
                nc.vector.tensor_reduce(total[1 - n][:, :], soft[:, :, :], AX.X, ALU.add).then_inc(S["prep_step"], 1)
                need(dve, S["prep_step"], chain(9))
                nc.vector.reciprocal(total[1 - n][:, :], total[1 - n][:, :]).then_inc(S["total_ready"], 1)

            def low_parts(m):
                if not ahead:
                    return
                need(dve, S["high_ready"], T * 2 + (3 + m))
                four = slice(4 * m, 4 * m + 4)
                nc.vector.tensor_tensor(keptL[1 - n][:, four, :],
                                        bank("kept", m)[0:2 * KEYS, :].rearrange("k (h t) -> k h t", h=4),
                                        keptH[1 - n][:, four, :].bitcast(FP32), ALU.subtract).then_inc(S["keptT_ready"], 1)

            def add_late(k):
                if T != (TILES - 1 if k < FIRST else TILES):
                    return
                b = (TILES - 1) % 2
                need(dve, S["silu_ready"], (TILES - 1) * RHEADS + (k + 1))
                if k == 1:
                    need(dve, S["z_turned"], (TILES - 2) * 4)
                else:
                    need(dve, S["late_sum"], k - 1)
                nc.vector.tensor_tensor(Z[b][:, LATE:COLS], u[:, 0, LATE:COLS] if k == 1 else Z[b][:, LATE:COLS],
                                        u[:, k, LATE:COLS], ALU.add).then_inc(S["late_sum"], 1)

            def add_out():
                if not behind:
                    return
                need(dve, S["out_product"], T)
                x = M.x[:, ds(T - 2, 1), :]
                nc.vector.tensor_tensor(x, bank("product", 0)[:, 0:DM].unsqueeze(1), x, ALU.add
                                        ).then_inc(S["out_added"], 1)

            take(DVE_STEPS, dict(mask=mask, weigh=weigh, top_eights=top_eights, replace=replace,
                                 candidates=candidates, keep=keep, bests=bests, replace_bests=replace_bests,
                                 ninths=ninths, thresholds=thresholds, totals=totals, low_parts=low_parts,
                                 add_out=add_out))
            if not ahead:
                for k in list(range(1, FIRST)) if live else list(range(FIRST, RHEADS)):
                    add_late(k)

        def pool_turn(pool, T, n, live, last_silus):
            def add(k):
                t, b = (T, n) if k < FIRST else (T - 1, 1 - n)
                if not (live if k < FIRST else last_silus):
                    return
                need(pool, S["silu_ready"], t * RHEADS + (k + 1))
                if k == 1:
                    need(pool, S["z_turned"], (t - 1) * 4)
                else:
                    need(pool, S["summed"], t * (RHEADS - 1) + (k - 1))
                cols = slice(0, LATE if isinstance(t, int) and t == TILES - 1 else COLS)
                nc.gpsimd.tensor_tensor(Z[b][:, cols], u[:, 0, cols] if k == 1 else Z[b][:, cols], u[:, k, cols],
                                        ALU.add).then_inc(S["summed"], 1)

            def weigh(i):
                if not live:
                    return
                k, a, b = UNITS[i]
                need(pool, S["z_ready"], T * 4 + 4)
                need_apart(pool, S["masked"], T * NU + (i + 1), M.passed)
                nc.gpsimd.tensor_tensor(u[:, k, a:b], u[:, k, a:b], z[n][:, a:b], ALU.mult
                                        ).then_inc(S["pool_weighted"], 1)

            take(POOL_STEPS, dict(add=add, weigh=weigh))

        def turns(eng, turn):
            for T in (-2, -1, 0, 1):
                turn(T, T % 2, T >= 0, T >= 1, T >= -1, False, True)
            with eng.Fori(0, (TILES - 4) // 2) as i:
                for n in range(2):
                    turn(i * 2 + (2 + n), n, True, True, True, True, True)
            for T in range(TILES - 2, TILES + 2):
                turn(T, T % 2, T < TILES, T <= TILES, T < TILES - 1, True, False)

        with nc.Block() as block:
            @block.tensor
            def _(pe):
                pe.wait_ge(tables_loaded, 64)
                pe.wait_ge(S["pairs_ready"], 1)
                pe.sem_inc(S["out_product"], 1)
                turns(pe, lambda T, n, live, last, ahead, behind, scored: pe_turn(pe, T, n, live, ahead, behind, scored))

            @block.scalar
            def _(act):
                turns(act, lambda T, n, live, last, ahead, behind, scored: act_turn(act, T, n, live, last, ahead, behind, scored))

            @block.vector
            def _(dve):
                dve.wait_ge(tables_loaded, 64)
                nc.vector.tensor_copy(pairs[:, :], z[1][0:2 * KEYS, :]).then_inc(S["pairs_ready"], 1)
                dve.sem_inc(S["out_added"], 1)
                turns(dve, lambda T, n, live, last, ahead, behind, scored: dve_turn(dve, T, n, live, ahead, behind))

            @block.gpsimd
            def _(pool):
                turns(pool, lambda T, n, live, last, ahead, behind, scored: pool_turn(pool, T, n, live, last))


class Memory:
    pass


def build(nc, D):
    M = Memory()
    M.norms = 0
    with scope(nc, "all") as s:
        M.xT, M.xL = s.sb_both("xT", [P, KD, TOKENS])
        M.x, xH = s.sb_both("x", [P, TILES, DM])
        M.xH = xH[:, :, :].rearrange("p n d -> p (n d)").rearrange("p (k t) -> p k t", k=KD)
        M.ident = s.sb("ident", [P, P])
        M.passed = s.sem("passed")
        M.norm_sems = {n: s.sem(f"norm_{n}") for n in NORM_SEMS}
        M.stored = s.sem("stored")
        M.stats = s.sb("stats", [P, TILES, 6])
        M.ident16 = s.sb("ident16", [P, P], BF16)
        with scope(nc, "g") as g:
            M.ones = g.sb("ones", [P, P])
            load_phase(nc, M, D)
            G = g.sb("gated", [P, PAIRS, TOKENS])
            squares_sum = g.sb("squares_sum", [P, TOKENS])
            gate_phase(nc, M, D, G)
            attention_phase(nc, M, D, G, squares_sum)
            projection_phase(nc, M, D, G, squares_sum)
        layernorm_phase(nc, M, stats_ready=False)
        experts_phase(nc, M, D)
        layernorm_phase(nc, M)
        scan_phase(nc, M, D)
        layernorm_phase(nc, M)
        retrieval_phase(nc, M, D)
        layernorm_phase(nc, M, D["out"], stats_ready=False)


def kernel(**inputs):
    import numpy as np
    import concourse.bacc as bacc
    from concourse.bass_utils import run_bass_kernel_spmd as run

    I = {k: np.asarray(v) for k, v in inputs.items()}
    x = I["L0_attn_hidden_states"].reshape(TOKENS, DM)
    qkv = I["L0_attn_qkv_w"].reshape(PAIRS, 2, 3, HD, DM)
    qkv = qkv.transpose(0, 4, 2, 1, 3).reshape(PAIRS, KD, P, 3 * P).transpose(0, 2, 1, 3)
    gate = I["L0_attn_gate_w"].reshape(PAIRS, P, KD, P).transpose(0, 3, 2, 1)
    A = dict(
        x=x, xT=x.T,
        qkv_w=np.pad(qkv.reshape(PAIRS, P, KD * 3 * P), ((0, 1), (0, 0), (0, 0))),
        gate_w=gate.reshape(PAIRS, P, KD * P),
        norm_w=np.pad(I["L0_attn_norm_w"].reshape(PAIRS, P, 1), ((0, 1), (0, 0), (0, 0))),
        decay=np.pad(decay_table(), ((0, 1), (0, 0), (0, 0))),
        out_w=I["L0_attn_out_w"].T,
    )
    wq = I["L1_ffn_W_q"].reshape(2, RHEADS, KHD, PRIV)
    pad_experts = lambda a: np.pad(a[:PAIRED], ((0, COLS - PAIRED), (0, 0)))
    keys = I["L1_ffn_keys"]
    A.update(
        w_up=I["L1_ffn_W_up"].T, b_up=I["L1_ffn_b_up"].reshape(-1, P).T,
        w_down=I["L1_ffn_W_down"].T, b_down=I["L1_ffn_b_down"][:, None],
        w_q=wq.transpose(2, 1, 0, 3).reshape(KHD, 2 * RHEADS, PRIV),
        keys=keys.transpose(3, 0, 2, 1).reshape(KHD, 2 * RHEADS, KEYS),
        down=pad_experts(I["L1_ffn_down_embed"]).T, up=pad_experts(I["L1_ffn_up_embed"]),
        pairs=pair_rows(),
    )
    pad = FTILES * P - EXPERTS * FF

    def hidden_rows(routed, shared, axis):
        a = np.concatenate([routed, shared], 0)
        a = a.transpose(1, 0, 2).reshape(DM, EXPERTS * FF) if axis == 1 else a.reshape(EXPERTS * FF, -1)
        return np.pad(a, ((0, 0), (0, pad)) if axis == 1 else ((0, pad), (0, 0)))

    second = hidden_rows(I["L0_ffn_routed_w2"], I["L0_ffn_shared_w2"], 0)
    second[EXPERTS * FF:EXPERTS * (FF + 1)] = np.concatenate([I["L0_ffn_routed_b2"], I["L0_ffn_shared_b2"]], 0)
    first_bias = hidden_rows(I["L0_ffn_routed_b1"], I["L0_ffn_shared_b1"], 0)
    first_bias[EXPERTS * FF:EXPERTS * (FF + 1)] = 1.0
    A.update(
        centroids=I["L0_ffn_centroids"].T, route_bias=I["L0_ffn_bias"],
        w1=hidden_rows(I["L0_ffn_routed_w1"], I["L0_ffn_shared_w1"], 1),
        w2=second, b1=first_bias.reshape(FTILES, P).T,
        expert_rows=expert_rows(),
    )
    wx, bx = I["L1_attn_W_xproj"].T, I["L1_attn_b_xproj"][:, None]
    A.update(
        wx=np.concatenate([wx[:, :DT_RANK]] + [wx[:, DT_RANK:]] * PARTS, 1),
        bx=np.concatenate([bx[:DT_RANK]] + [bx[DT_RANK:]] * PARTS, 0),
        wdt=I["L1_attn_W_dt"].T, bdt=I["L1_attn_b_dt"].reshape(KD, P).T,
        a_log=I["L1_attn_A_log"].reshape(KD, P, STATES).transpose(1, 0, 2),
        state_rows=state_rows(),
    )
    nc = bacc.Bacc("TRN2", target_bir_lowering=False, num_devices=1)
    D, arrays = {}, {}
    for name, a in A.items():
        a = np.ascontiguousarray(a)
        arrays[f"in_{name}_dram"] = a
        D[name] = nc.dram_tensor(f"in_{name}_dram", a.shape, mybir.dt.from_np(a.dtype),
                                 kind="ExternalInput").ap()
    D["out"] = nc.dram_tensor("out_0_dram", (BATCH, SEQ, DM), FP32, kind="ExternalOutput").ap()
    build(nc, D)
    r = run(nc, [arrays], core_ids=[0])
    return r.results[0]["out_0_dram"]
```
